# Optimizing a Trainium2 kernel written in Bass

```python
import numpy as np
import jax
import jax.numpy as jnp

def _softmax(x, axis=-1):
    return jax.nn.softmax(x, axis=axis)

def _gelu(x):
    return jax.nn.gelu(x, approximate=True)

def _silu(x):
    return jax.nn.silu(x)

def _sigmoid(x):
    return jax.nn.sigmoid(x)

def _layernorm(x, axis=-1, eps=1e-05):
    m = jnp.mean(x, axis=axis, keepdims=True)
    v = jnp.var(x, axis=axis, keepdims=True)
    return (x - m) / jnp.sqrt(v + eps)

def _scatter_add(tgt, idx, src, axis=0):
    return tgt.at[idx].add(src)

def _segment_sum(src, seg, n):
    return jax.ops.segment_sum(src, seg, n)
kernel_name = 'mk_gnn_preln_d4_gnn_r32_128532'

def setup_inputs(seed: int=0):
    np.random.seed(seed)
    _w = jnp.asarray

    def _rec_inputs():
        import jax
        import jax.numpy as jnp
        _gk = jax.random.key(seed)
        x = 0.00011 + 1 * jax.random.normal(jax.random.fold_in(_gk, 1), (3125, 48), jnp.float32)
        src = jax.random.randint(jax.random.fold_in(_gk, 2), (100000,), 0, 3125, jnp.int32)
        dst = jnp.minimum((3125 * jax.random.uniform(jax.random.fold_in(_gk, 3), (100000,)) ** 2.0).astype(jnp.int32), 99999)
        _o = jnp.argsort(dst, stable=True)
        src = src[_o]
        dst = dst[_o]
        edge_attr_16 = 0.000196303 + 1.00016 * jax.random.normal(jax.random.fold_in(_gk, 12), (100000, 16), jnp.float32)
        edge_type_8 = jax.random.randint(jax.random.fold_in(_gk, 14), (100000,), 0, 8, jnp.int32)
        edge_weight1 = jax.random.uniform(jax.random.fold_in(_gk, 15), (100000, 1), jnp.float32, 0.0, 1)
        return (x, src, dst, edge_attr_16, edge_type_8, edge_weight1)
    x, src, dst, edge_attr_16, edge_type_8, edge_weight1 = _rec_inputs()

    def _L0_gnn_setup():
        import jax, jax.numpy as jnp
        import numpy as np
        N_NODES = 3125
        N_EDGES = 50000
        D_FEAT = 48
        N_LAYERS = 2
        key = jax.random.key(seed)
        k1, k2, k3 = jax.random.split(key, 3)
        row = jax.random.randint(k1, (N_EDGES,), 0, N_NODES, dtype=jnp.int32)
        col = jax.random.randint(k2, (N_EDGES,), 0, N_NODES, dtype=jnp.int32)
        x = jax.random.normal(k3, (N_NODES, D_FEAT), dtype=jnp.float32)
        return {'row': row, 'col': col, 'x': x}
    _L0_gnn_all = _L0_gnn_setup()
    _L0_gnn_in = {k: v for k, v in _L0_gnn_all.items() if k in ()}
    del _L0_gnn_all

    def _L1_gnn_setup():
        import jax, jax.numpy as jnp
        import numpy as np
        N_NODES = 50000
        N_EDGES = 50000
        IN_FEAT = 48
        OUT_FEAT = 48
        NUM_RELS = 8
        key = jax.random.key(seed)
        ks = jax.random.split(key, 9)
        s1 = float(np.sqrt(2.0) * np.sqrt(6.0 / (IN_FEAT + IN_FEAT)))
        s2 = float(np.sqrt(2.0) * np.sqrt(6.0 / (IN_FEAT + OUT_FEAT)))
        return {'inputs': jax.random.normal(ks[0], (N_NODES, IN_FEAT), dtype=jnp.float32), 'norm': jax.random.uniform(ks[1], (N_EDGES, 1), dtype=jnp.float32), 'weight1': jax.random.uniform(ks[2], (NUM_RELS, IN_FEAT, IN_FEAT), jnp.float32, -s1, s1), 'weight2': jax.random.uniform(ks[3], (NUM_RELS, IN_FEAT, OUT_FEAT), jnp.float32, -s2, s2), 'bias1': jax.random.normal(ks[4], (IN_FEAT,), dtype=jnp.float32) * 0.1, 'bias2': jax.random.normal(ks[5], (OUT_FEAT,), dtype=jnp.float32) * 0.1, 'src': jax.random.randint(ks[6], (N_EDGES,), 0, N_NODES, dtype=jnp.int64) if jax.config.jax_enable_x64 else jax.random.randint(ks[6], (N_EDGES,), 0, N_NODES).astype(jnp.int32), 'dst': jax.random.randint(ks[7], (N_EDGES,), 0, N_NODES).astype(jnp.int32), 'rel_type': jax.random.randint(ks[8], (N_EDGES,), 0, NUM_RELS).astype(jnp.int32)}
    _L1_gnn_all = _L1_gnn_setup()
    _L1_gnn_in = {k: v for k, v in _L1_gnn_all.items() if k in ('weight1', 'weight2', 'bias1', 'bias2')}
    del _L1_gnn_all

    def _L2_gnn_setup():
        import jax, jax.numpy as jnp
        import numpy as np
        import math
        K = 10
        A = 1.0
        B = 1.0
        ALPHA = 1.0

        def _An(n, a, b):
            nab = 2 * n + a + b
            return nab * (nab - 1) * (nab - 2) / (2 * n * (nab - n) * (nab - 2))

        def _Bn(n, a, b):
            nab = 2 * n + a + b
            return (nab - 1) * (a * a - b * b) / (2 * n * (nab - n) * (nab - 2))

        def _Cn(n, a, b):
            nab = 2 * n + a + b
            return -(2 * (n + a - 1) * (n + b - 1) * nab) / (2 * n * (nab - n) * (nab - 2))

        def _norm_weights(a, b):
            ws = []
            for i in range(K + 1):
                t1 = math.pow(2.0, a + b + 1) / (2 * i + a + b + 1)
                t2 = math.exp(math.lgamma(i + a + 1) - math.lgamma(i + a + b + 1))
                t3 = math.exp(math.lgamma(i + b + 1) - math.lgamma(i + 1))
                ws.append(math.sqrt(t1 * t2 * t3))
            return ws
        key = jax.random.key(seed)
        k1, k2 = jax.random.split(key)
        N, E, D = (3125, 50000, 48)
        x = jax.random.normal(k1, (N, D), dtype=jnp.float32)
        edge_index = jax.random.randint(k2, (2, E), 0, N, dtype=jnp.int64)
        lap_coefs = jnp.ones((K + 1,), dtype=jnp.float32)
        mf_weights = jnp.ones((1, K + 1, 1), dtype=jnp.float32)
        return {'x': x, 'edge_index': edge_index, 'lap_coefs': lap_coefs, 'mf_weights': mf_weights}
    _L2_gnn_all = _L2_gnn_setup()
    _L2_gnn_in = {k: v for k, v in _L2_gnn_all.items() if k in ('lap_coefs', 'mf_weights')}
    del _L2_gnn_all

    def _L3_gnn_setup():
        import jax, jax.numpy as jnp
        import numpy as np
        N_NODES = 3125
        N_EDGES = 50000
        N_FEAT = 48
        N_EDGE_FEAT = 16
        HIDDEN = 128
        key = jax.random.key(seed)
        ks = jax.random.split(key, 8)
        tot = 2 * N_FEAT + N_EDGE_FEAT
        s1 = 1.0 / np.sqrt(tot)
        s2 = 1.0 / np.sqrt(HIDDEN)
        return {'x': jax.random.normal(ks[0], (N_NODES, N_FEAT), dtype=jnp.float32), 'edge_index': jax.random.randint(ks[1], (2, N_EDGES), 0, N_NODES, dtype=jnp.int64), 'edge_feat': jax.random.normal(ks[2], (N_EDGES, N_EDGE_FEAT), dtype=jnp.float32), 'W1': jax.random.normal(ks[3], (tot, HIDDEN), dtype=jnp.float32) * s1, 'b1': jnp.zeros((HIDDEN,), dtype=jnp.float32), 'W2': jax.random.normal(ks[4], (HIDDEN, HIDDEN), dtype=jnp.float32) * s2, 'b2': jnp.zeros((HIDDEN,), dtype=jnp.float32), 'W3': jax.random.normal(ks[5], (HIDDEN, N_FEAT), dtype=jnp.float32) * s2, 'b3': jnp.zeros((N_FEAT,), dtype=jnp.float32)}
    _L3_gnn_all = _L3_gnn_setup()
    _L3_gnn_in = {k: v for k, v in _L3_gnn_all.items() if k in ('W1', 'b1', 'W2', 'b2', 'W3', 'b3')}
    del _L3_gnn_all
    return {'x': x, 'src': src, 'dst': dst, 'edge_attr_16': edge_attr_16, 'edge_type_8': edge_type_8, 'edge_weight1': edge_weight1, 'L1_gnn_weight1': _L1_gnn_in['weight1'], 'L1_gnn_weight2': _L1_gnn_in['weight2'], 'L1_gnn_bias1': _L1_gnn_in['bias1'], 'L1_gnn_bias2': _L1_gnn_in['bias2'], 'L2_gnn_lap_coefs': _L2_gnn_in['lap_coefs'], 'L2_gnn_mf_weights': _L2_gnn_in['mf_weights'], 'L3_gnn_W1': _L3_gnn_in['W1'], 'L3_gnn_b1': _L3_gnn_in['b1'], 'L3_gnn_W2': _L3_gnn_in['W2'], 'L3_gnn_b2': _L3_gnn_in['b2'], 'L3_gnn_W3': _L3_gnn_in['W3'], 'L3_gnn_b3': _L3_gnn_in['b3']}

def reference(x, src, dst, edge_attr_16, edge_type_8, edge_weight1, L1_gnn_weight1, L1_gnn_weight2, L1_gnn_bias1, L1_gnn_bias2, L2_gnn_lap_coefs, L2_gnn_mf_weights, L3_gnn_W1, L3_gnn_b1, L3_gnn_W2, L3_gnn_b2, L3_gnn_W3, L3_gnn_b3):
    import jax
    import jax.numpy as jnp

    def _L0_gnn_ref(row, col, x):
        import jax, jax.numpy as jnp
        import numpy as np
        N_NODES = 3125
        N_EDGES = 50000
        D_FEAT = 48
        N_LAYERS = 2
        n = x.shape[0]
        loop = jnp.arange(n, dtype=row.dtype)
        r = jnp.concatenate([row, loop])
        c = jnp.concatenate([col, loop])
        deg = jax.ops.segment_sum(jnp.ones(r.shape, dtype=x.dtype), r, num_segments=n)
        dinv = jnp.where(deg > 0, jax.lax.rsqrt(deg), 0.0)
        w = dinv[r] * dinv[c]
        for _ in range(N_LAYERS):
            x = jax.ops.segment_sum(w[:, None] * x[c], r, num_segments=n)
        return x

    def _L1_gnn_ref(inputs, norm, weight1, weight2, bias1, bias2, src, dst, rel_type):
        import jax, jax.numpy as jnp
        import numpy as np
        N_NODES = 50000
        N_EDGES = 50000
        IN_FEAT = 48
        OUT_FEAT = 48
        NUM_RELS = 8
        h1 = jax.nn.relu(jnp.einsum('ni,rij->nrj', inputs, weight1) + bias1)
        h2 = jnp.einsum('nrj,rjo->nro', h1, weight2)
        msg = h2[src, rel_type] * norm
        agg = jax.ops.segment_sum(msg, dst, num_segments=inputs.shape[0])
        return jax.nn.relu(agg + bias2)

    def _L2_gnn_ref(x, edge_index, lap_coefs, mf_weights):
        import jax, jax.numpy as jnp
        import numpy as np
        import math
        K = 10
        A = 1.0
        B = 1.0
        ALPHA = 1.0

        def _An(n, a, b):
            nab = 2 * n + a + b
            return nab * (nab - 1) * (nab - 2) / (2 * n * (nab - n) * (nab - 2))

        def _Bn(n, a, b):
            nab = 2 * n + a + b
            return (nab - 1) * (a * a - b * b) / (2 * n * (nab - n) * (nab - 2))

        def _Cn(n, a, b):
            nab = 2 * n + a + b
            return -(2 * (n + a - 1) * (n + b - 1) * nab) / (2 * n * (nab - n) * (nab - 2))

        def _norm_weights(a, b):
            ws = []
            for i in range(K + 1):
                t1 = math.pow(2.0, a + b + 1) / (2 * i + a + b + 1)
                t2 = math.exp(math.lgamma(i + a + 1) - math.lgamma(i + a + b + 1))
                t3 = math.exp(math.lgamma(i + b + 1) - math.lgamma(i + 1))
                ws.append(math.sqrt(t1 * t2 * t3))
            return ws
        N = x.shape[0]
        src = edge_index[0]
        dst = edge_index[1]
        deg = jax.ops.segment_sum(jnp.ones(src.shape, dtype=x.dtype), dst, num_segments=N)
        dinv = jnp.where(deg > 0, jax.lax.rsqrt(jnp.where(deg > 0, deg, 1.0)), 0.0)
        enorm = dinv[src] * dinv[dst]

        def prop(h):
            return jax.ops.segment_sum(enorm[:, None] * h[src], dst, num_segments=N)
        nw = _norm_weights(A, B)
        c0 = (A - B) / 2.0
        c1 = (A + B + 2.0) / 2.0
        P0 = x
        P1 = c0 * x + c1 * prop(x)
        outs = [P0, P1]
        for n in range(2, K + 1):
            an, bn, cn = (_An(n, A, B), _Bn(n, A, B), _Cn(n, A, B))
            outs.append(bn * outs[-1] + cn * outs[-2] + an * prop(outs[-1]))
        lap = jnp.cumprod(ALPHA * jnp.tanh(lap_coefs))
        coef_outs = [outs[0] / nw[0]]
        for i in range(1, K + 1):
            coef_outs.append(lap[i - 1] / nw[i] * outs[i])
        stacked = jnp.stack(coef_outs, axis=1)
        return jnp.sum(stacked * mf_weights, axis=1)

    def _L3_gnn_ref(x, edge_index, edge_feat, W1, b1, W2, b2, W3, b3):
        import jax, jax.numpy as jnp
        import numpy as np
        N_NODES = 3125
        N_EDGES = 50000
        N_FEAT = 48
        N_EDGE_FEAT = 16
        HIDDEN = 128
        source = edge_index[0]
        target = edge_index[1]
        edge = jnp.concatenate([x[source], x[target], edge_feat], axis=-1)
        h = jax.nn.relu(edge @ W1 + b1)
        h = jax.nn.relu(h @ W2 + b2)
        message = h @ W3 + b3
        n = x.shape[0]
        msum = jax.ops.segment_sum(message, target, num_segments=n)
        cnt = jax.ops.segment_sum(jnp.ones((target.shape[0],), dtype=x.dtype), target, num_segments=n)
        update = msum / jnp.maximum(cnt, 1.0)[:, None]
        return x + update
    edge_index = jnp.stack([src, dst])
    h = jnp.maximum(_layernorm(x, axis=-1), 0.0)
    x = x + _L0_gnn_ref(src, dst, h)
    h = jnp.maximum(_layernorm(x, axis=-1), 0.0)
    x = x + _L1_gnn_ref(h, edge_weight1, L1_gnn_weight1, L1_gnn_weight2, L1_gnn_bias1, L1_gnn_bias2, src, dst, edge_type_8)
    h = jnp.maximum(_layernorm(x, axis=-1), 0.0)
    x = x + _L2_gnn_ref(h, edge_index, L2_gnn_lap_coefs, L2_gnn_mf_weights)
    h = jnp.maximum(_layernorm(x, axis=-1), 0.0)
    x = x + _L3_gnn_ref(h, edge_index, edge_attr_16, L3_gnn_W1, L3_gnn_b1, L3_gnn_W2, L3_gnn_b2, L3_gnn_W3, L3_gnn_b3)
    return x

_drawn_inputs = setup_inputs


def setup_inputs(seed=0):
    import zlib

    import numpy as np

    out = dict(_drawn_inputs(seed))
    spreads = {'L2_gnn_lap_coefs': (1.0, 0.6),
     'L2_gnn_mf_weights': (1.0, 0.6),
     'L3_gnn_b1': (0.0, 0.8),
     'L3_gnn_b2': (0.0, 0.8),
     'L3_gnn_b3': (0.0, 2.0)}
    factors = {'edge_attr_16': 8.0,
     'L3_gnn_W1': 3.012,
     'L3_gnn_W2': 3.029,
     'L3_gnn_W3': 2.877,
     'L1_gnn_bias2': 4.201}
    for name, (base, spread) in spreads.items():
        noise = np.random.default_rng([zlib.crc32(name.encode()), seed]).standard_normal(out[name].shape)
        drawn = base * np.exp(spread * noise) if base else spread * noise
        out[name] = jnp.asarray(drawn.astype(out[name].dtype))
    for name, factor in factors.items():
        out[name] = (out[name] * factor).astype(out[name].dtype)
    return out
```

```python
from contextlib import ExitStack
import math

import concourse.bass as bass
from concourse import mybir

ALU = mybir.AluOpType
ACT = mybir.ActivationFunctionType
AX = mybir.AxisListType
F32 = mybir.dt.float32
BF16 = mybir.dt.bfloat16
F16 = mybir.dt.float16
I32 = mybir.dt.int32
U32 = mybir.dt.uint32

P = 128
N, D = 3125, 48
E = 100000
NT = -(-N // P)
NP = NT * P
NREM = N - (NT - 1) * P
RE = 1024
RP = -(-E // RE)
RREM = E - (RP - 1) * RE
HE = 256
NH = RP * RE // HE
NC = 2 * NH
NG = NH // 2
WIN = 24
QS = WIN + 2
NQ = NT + 1
HALFQ = NQ // 2 * WIN
LASTBASE = NP - WIN
ADJ = NT * NP
NWT = NT + 2
REL = 8
HID = 128
EF = 16
K = 10
PART = 3 * D
TPB = 3
NB = -(-NT // TPB)
BIG = 16384.0


def jacobi():
    a = b = 1.0
    an, cn = [(a + b + 2.0) / 2.0], [0.0]
    for n in range(2, K + 1):
        nab = 2 * n + a + b
        an.append(nab * (nab - 1) * (nab - 2) / (2 * n * (nab - n) * (nab - 2)))
        cn.append(-(2 * (n + a - 1) * (n + b - 1) * nab) / (2 * n * (nab - n) * (nab - 2)))
    norm = []
    for i in range(K + 1):
        t1 = math.pow(2.0, a + b + 1) / (2 * i + a + b + 1)
        t2 = math.exp(math.lgamma(i + a + 1) - math.lgamma(i + a + b + 1))
        t3 = math.exp(math.lgamma(i + b + 1) - math.lgamma(i + 1))
        norm.append(math.sqrt(t1 * t2 * t3))
    return an, cn, norm


class Count:

    def __init__(self, eng, sem):
        self.eng, self.sem, self.n, self.base = eng, sem, 0, 0

    def did(self, instruction):
        self.n += 1
        instruction.then_inc(self.sem, 1)

    def all(self):
        self.eng.wait_ge(self.sem, self.base + self.n)

    def do(self, instruction):
        self.did(instruction)
        self.all()


def gnn(nc, x_d, src_d, dst_d, ea_d, et_d, ew_d, w1_d, w2_d, b1_d, b2_d, lap_d, mf_d,
        m1_d, mb1_d, m2_d, mb2_d, m3_d, mb3_d, out_d):
    ctx = ExitStack()
    with ctx:
        def sb(name, shape, dt):
            return ctx.enter_context(nc.sbuf_tensor(name, shape, dt))

        def sem(name):
            return ctx.enter_context(nc.semaphore(name))

        msg_table = nc.dram_tensor("msg_table", (NP * REL, D), F32, kind="Internal").ap()
        node_table = nc.dram_tensor("node_table", (NP, D), F32, kind="Internal").ap()
        rel_rows = nc.dram_tensor("rel_rows", (NC, P), BF16, kind="Internal").ap()

        adj = sb("adj", [P, ADJ], F16)
        scr = sb("scr", [P, 6700], F32)
        x = sb("x", [P, NT * D], F32)
        rel_b = sb("rel_b", [P, NC], F32)
        norm_c = sb("norm_c", [P, NC], F32)
        idx_msg = sb("idx_msg", [P, NC], U32)
        idx_src = sb("idx_src", [P, NC], U32)
        iota_code = sb("iota_code", [P, NQ * WIN], F16)
        iota_256 = sb("iota_256", [P, 256], F16)
        iota_p = sb("iota_p", [P, 2], F32)
        ident = sb("ident", [P, P], F32)
        identh = sb("identh", [P, P], F16)
        ones = sb("ones", [P, P], F32)
        onesh = sb("onesh", [P, 2], F16)
        base_row = sb("base_row", [1, 2 + NH], I32)
        tile_row = sb("tile_row", [1, NG], I32)
        passes = sb("passes", [1, 2], I32)
        stat = sb("stat", [P, 9 * NT], F32)
        dinv_in = sb("dinv_in", [P, NT], F32)
        cnt_in = sb("cnt_in", [P, NT], F32)
        rec = sb("rec", [P, 3 * K + 1], F32)
        small = sb("small", [P, 64], F32)
        smi = sb("smi", [P, 16], I32)
        psum = ctx.enter_context(nc.psum_tensor("psum", [P, 8, 512], F32))
        psum_h = psum[:, :, :].bitcast(F16)
        x3 = x[:, :].rearrange("p (q f) -> p q f", f=D)
        adj3 = adj[:, :].rearrange("p (q n) -> p q n", n=NP)

        adj_f = adj[:, :].bitcast(F32)
        ROW0 = ADJ // 2 - 8 * RE

        def row(k):
            return adj_f[0:P, ROW0 + k * RE:ROW0 + (k + 1) * RE]
        dst_i, src_i, typ_i = (row(k).bitcast(I32) for k in range(3))
        nrm_f, dst_f, t_a, t_b, t_c = (row(k) for k in range(3, 8))
        code_c = scr[:, 0:NC]
        rel_a = scr[:, NC:2 * NC]
        q_c = scr[:, 2 * NC:3 * NC]
        r_c = scr[:, 3 * NC:4 * NC]
        ROWS = [t_b, t_c, t_b, t_c, t_b, t_c, nrm_f]
        COLS = [rel_a, q_c, r_c, rel_b[:, :], idx_msg[:, :], idx_src[:, :], norm_c[:, :]]
        s_final = sem("s_final")

        s_fill = sem("s_fill")
        s_in = sem("s_in")
        s_x = sem("s_x")
        s_const = sem("s_const")
        s_id0 = sem("s_id0")
        s_zero = sem("s_zero")
        v_seq = sem("v_seq")
        s_rowready = sem("s_rowready")
        s_rowt = sem("s_rowt")
        s_rowout = sem("s_rowout")
        s_statready = sem("s_statready")
        s_statrow = sem("s_statrow")
        s_passes = sem("s_passes")
        s_code = sem("s_code")
        s_oh = sem("s_oh")
        s_built = sem("s_built")
        s_stage = sem("s_stage")
        s_add = sem("s_add")
        s_adj = sem("s_adj")
        s_tp = sem("s_tp")
        s_tx = sem("s_tx")
        s_ty = sem("s_ty")
        s_deg = sem("s_deg")
        s_degread = sem("s_degread")
        s_var = sem("s_var")
        s_root = sem("s_root")
        s_xp = sem("s_xp")
        s_prop = sem("s_prop")
        s_bank = sem("s_bank")
        s_out = sem("s_out")

        H1T = scr[0:96, 0:2048].rearrange("p (c n) -> p c n", c=4)
        HT = scr[0:D, 2048:3072].rearrange("p (s n) -> p s n", s=2)
        H2 = scr[:, 3072:3840].rearrange("p (s c) -> p s c", s=2)
        W1R = scr[0:D, 3840:4224]
        W2R = scr[0:96, 4224:4608].rearrange("p (c j) -> p c j", c=4)
        B1R = scr[0:96, 4608:4609]
        H = scr[:, 4616:5816].rearrange("p (q f) -> p q f", f=D)
        LNT = scr[:, 0:1200].rearrange("p (q f) -> p q f", f=D)
        GM = scr[:, 0:768].rearrange("p (s c) -> p s c", s=4)
        IDX = scr[:, 768:784].bitcast(U32).rearrange("p (s c) -> p s c", s=4)
        WOH = scr[:, 784:2832].rearrange("p (s t c) -> p s t c", s=2, t=4)
        ACC = scr[:, 2832:2832 + NWT * D]
        B2R = scr[:, 4128:4128 + D]
        REL1 = scr[:, 4176:4176 + NC]
        TILE1 = scr[0:1, 4960:4960 + NG].bitcast(I32)
        HCH = [(c * 4, min(NT, c * 4 + 4)) for c in range(-(-NT // 4))]

        spot = [0]

        def place(n):
            spot[0] += n
            return adj_f[:, spot[0] - n:spot[0]]
        PD = place(NWT * 3 * HID // 2).bitcast(BF16)
        G3 = place(4 * 4 * 64).rearrange("p (s t c) -> p s t c", s=4, t=4)
        GT = place(2 * 512).rearrange("p (s c) -> p s c", s=2)
        REL_ROW = place(4 * 256).bitcast(BF16).rearrange("p (s c) -> p s c", s=4)
        OHT = place(2 * 512).bitcast(BF16).rearrange("p (s w c) -> p s w c", s=2, w=2)
        OHF = place(2 * 1024).rearrange("p (s t c) -> p s t c", s=2, t=4)
        R1 = place(2 * 512).rearrange("p (s c) -> p s c", s=2)
        R2 = place(2 * 512).rearrange("p (s c) -> p s c", s=2)
        MS = place(2 * 4 * D).rearrange("p (s c) -> p s c", s=2)
        ACC3 = place(NWT * D)
        REL3 = place(NC)
        CLAMP = place(NC)
        RELT = place(7 * P // 2).bitcast(BF16).rearrange("p (j c) -> p j c", j=7)
        H3 = place(NT * D).rearrange("p (q f) -> p q f", f=D)
        LNT3 = place(NT * D).rearrange("p (q f) -> p q f", f=D)
        HT3 = place(2 * 512).rearrange("p (s c) -> p s c", s=2)
        PDR = place(512)
        W1AC, W1B, W2M, W3M = place(HID), place(HID), place(HID), place(D)
        BM = place(2)
        B3R = place(D)
        TILE3 = place(2 + NG)[0:1, :].bitcast(I32)
        IDX3 = place(16).bitcast(U32).rearrange("p (s c) -> p s c", s=4)

        s_w = sem("s_w")
        s_wz = sem("s_wz")
        s_h = sem("s_h")
        s_ht = sem("s_ht")
        s_htc = sem("s_htc")
        s_h1 = sem("s_h1")
        s_h1r = sem("s_h1r")
        s_h2 = sem("s_h2")
        s_h2c = sem("s_h2c")
        s_tab = [sem("s_tab0"), sem("s_tab1")]
        s_loop1 = sem("s_loop1")
        s_idx = sem("s_idx")
        s_gath = [sem(f"s_gath{k}") for k in range(4)]
        s_woh = sem("s_woh")
        s_seg = sem("s_seg")
        s_acc = sem("s_acc")
        s_shift = sem("s_shift")
        s_coef = sem("s_coef")
        s_lap = sem("s_lap")
        s_lapin = sem("s_lapin")
        s_coefb = sem("s_coefb")
        v_l2 = sem("v_l2")
        s_w3in = sem("s_w3in")
        s_l2done = sem("s_l2done")
        s_node = sem("s_node")
        s_ht3 = sem("s_ht3")
        s_htc3 = sem("s_htc3")
        s_pd = sem("s_pd")
        s_pdc = sem("s_pdc")
        s_clamp = sem("s_clamp")
        s_relt = sem("s_relt")
        s_reltc = sem("s_reltc")
        s_relst = sem("s_relst")
        s_idx3 = sem("s_idx3")
        s_in3 = [sem(f"s_in3{k}") for k in range(4)]
        s_ef = [sem(f"s_ef{k}") for k in range(4)]
        s_rel3 = [sem(f"s_rel3{k}") for k in range(4)]
        s_t3 = sem("s_t3")
        s_gt = sem("s_gt")
        s_oht = sem("s_oht")
        s_z1 = sem("s_z1")
        s_r1 = sem("s_r1")
        s_z2 = sem("s_z2")
        s_r2 = sem("s_r2")
        s_w3 = sem("s_w3")
        s_msg = sem("s_msg")
        s_ohf = sem("s_ohf")
        s_seg3 = sem("s_seg3")
        s_acc3 = sem("s_acc3")
        s_shift3 = sem("s_shift3")
        s_mark = sem("s_mark")
        AN, CN, NORM = jacobi()

        block = ctx.enter_context(nc.Block())

        CH = [(q, m, min(8, NT - m)) for q in range(NT) for m in range(q, NT, 8)]
        LOWER = []
        for q, m, c in CH:
            LOWER.append((LOWER[-1] if LOWER else 0) + (m + c - 1 > q))
        adj_blk = adj[:, :].rearrange("p (q m r) -> p q m r", m=NT, r=P)
        NCONST = 7

        XP = [scr[:, k * 1800:(k + 1) * 1800].bitcast(BF16).rearrange("p (q j f) -> p q j f", j=3, f=D) for k in range(2)]
        PA = scr[:, 3600:4800].rearrange("p (q f) -> p q f", f=D)
        PB = scr[:, 4800:6000].rearrange("p (q f) -> p q f", f=D)
        TY = scr[:, 6000:6000 + TPB * D].rearrange("p (q f) -> p q f", f=D)
        TR = scr[:, 6144:6144 + TPB * D].rearrange("p (q f) -> p q f", f=D)
        BANKS = [(b * TPB, min(NT, (b + 1) * TPB)) for b in range(NB)]
        OHQ = scr[:, 4 * NC:4 * NC + 4 * NQ * WIN // 2].bitcast(F16).rearrange("p (s t c) -> p s t c", s=2, t=2)
        o = 4 * NC + 4 * NQ * WIN // 2
        OHR = scr[:, o:o + 256].bitcast(F16).rearrange("p (s t c) -> p s t c", s=2, t=2)
        o += 256
        STG = scr[:, o:o + NQ * WIN].bitcast(F16).rearrange("p (s c) -> p s c", s=2)

        def st(k, n=1):
            return stat[:, k * NT:(k + n) * NT]

        def bc(a, n=D):
            return a.unsqueeze(2).broadcast_to((a.shape[0], a.shape[1], n))

        @block.sync
        def _(sp):
            sp.wait_ge(s_fill, 4)
            for dst, src in ((dst_i, dst_d), (src_i, src_d), (typ_i, et_d)):
                sp.dma_start(dst[0:RP - 1, :], src[0:(RP - 1) * RE].rearrange("(p c) -> p c", c=RE)).then_inc(s_in, 16)
                sp.dma_start(dst[RP - 1:RP, 0:RREM], src[(RP - 1) * RE:E].rearrange("(p c) -> p c", c=RREM)).then_inc(s_in, 16)
            sp.dma_start(nrm_f[0:RP - 1, :], ew_d[0:(RP - 1) * RE, :].rearrange("(p c) o -> p (c o)", c=RE)).then_inc(s_in, 16)
            sp.dma_start(nrm_f[RP - 1:RP, 0:RREM], ew_d[(RP - 1) * RE:E, :].rearrange("(p c) o -> p (c o)", c=RREM)).then_inc(s_in, 16)
            sp.wait_ge(s_fill, 5)
            sp.dma_start(x3[:, 0:NT - 1, :], x_d[0:(NT - 1) * P, :].rearrange("(q r) f -> r q f", r=P)).then_inc(s_x, 16)
            sp.dma_start(x3[0:NREM, NT - 1, :], x_d[(NT - 1) * P:N, :]).then_inc(s_x, 16)
            sp.wait_ge(s_wz, 1)
            sp.dma_start(W1R.rearrange("p (r j) -> p r j", r=REL), w1_d.rearrange("r i j -> i r j")).then_inc(s_w, 16)
            w2_v = w2_d.rearrange("(c s) i j -> s i c j", s=2)
            for k in range(2):
                sp.dma_start(W2R[k * D:(k + 1) * D, :, k * D:(k + 1) * D], w2_v[k]).then_inc(s_w, 16)
                sp.dma_start(B1R[k * D:(k + 1) * D, :], b1_d.rearrange("(p o) -> p o", o=1)).then_inc(s_w, 16)
            table = msg_table.rearrange("(q r e) f -> q r (e f)", r=P, e=REL)
            for q in range(NT):
                sp.wait_ge(s_h2c, q + 1)
                sp.dma_start(table[q], H2[:, q % 2, :]).then_inc(s_tab[q % 2], 16)
            sp.wait_ge(s_loop1, 1)
            sp.dma_start(B2R, b2_d.partition_broadcast(P)).then_inc(s_w, 16)
            sp.dma_start(small[0:1, 0:K + 1], lap_d.rearrange("(o k) -> o k", o=1)).then_inc(s_lapin, 16)
            sp.dma_start(small[0:1, 16:16 + K + 1], mf_d.rearrange("o k e -> o (k e)")).then_inc(s_lapin, 16)
            sp.wait_ge(s_l2done, 1)
            for dst, src in ((W1AC[0:D, :], m1_d[0:D, :]), (W1AC[D:D + EF, :], m1_d[2 * D:2 * D + EF, :]), (W1B[0:D, :], m1_d[D:2 * D, :]),
                             (W2M, m2_d), (W3M, m3_d), (BM[:, 0:1], mb1_d.rearrange("(p o) -> p o", o=1)),
                             (BM[:, 1:2], mb2_d.rearrange("(p o) -> p o", o=1)), (B3R, mb3_d.partition_broadcast(P))):
                sp.dma_start(dst, src).then_inc(s_w3in, 16)
            sp.wait_ge(s_h, 2)
            sp.dma_start(node_table.rearrange("(q r) f -> r q f", r=P), H3).then_inc(s_node, 16)
            most = sp.value_load(passes[0:1, 1:2], min_val=0, max_val=NT)
            with sp.Fori(0, most // 2 + 1) as p:
                sp.wait_ge(s_reltc, p + 1)
                sp.wait_ge(s_oht, p * NG + 4)
                sp.dma_start(rel_rows.rearrange("(j c) e -> c j e", j=7), RELT[0:NC // 7, :, :]).then_inc(s_relst, 16)
                sp.wait_ge(s_relst, p * 16 + 16)
                sp.sem_inc(s_mark, 1)

                def load(i, n):
                    for k in range(4):
                        sp.wait_ge(s_oht, n + k + 1)
                        codes = rel_rows[bass.ds((i * 4 + k) * 4, 4), :] if not isinstance(i, int) else rel_rows[(i * 4 + k) * 4:(i * 4 + k) * 4 + 4, :]
                        sp.dma_start(REL_ROW[:, k, :], codes.rearrange("a b -> (a b)").partition_broadcast(P)).then_inc(s_rel3[k], 16)
                        sp.wait_ge(s_t3, n + k + 1)
                        for h in range(2):
                            if isinstance(i, int):
                                e0 = ((i * 4 + k) * 2 + h) * HE
                                m = min(HE, E - e0)
                                if m > 0:
                                    sp.dma_start(G3[0:m // 2, k, 2 * h:2 * h + 2, D:D + EF], ea_d[e0:e0 + m, :].rearrange("(p t) f -> p t f", t=2))\
                                      .then_inc(s_ef[k], 16 if h or e0 + HE < E else 32)
                            else:
                                sp.dma_start(G3[:, k, 2 * h:2 * h + 2, D:D + EF],
                                             ea_d[bass.ds(i * (8 * HE) + (2 * k + h) * HE, HE), :].rearrange("(p t) f -> p t f", t=2)).then_inc(s_ef[k], 16)
                with sp.Fori(0, NG // 4 - 1) as i:
                    load(i, sp.snap(p * NG + i * 4))
                load(NG // 4 - 1, sp.snap(p * NG + (NG - 4)))
            sp.wait_ge(s_final, 1)
            sp.dma_start(out_d[0:(NT - 1) * P, :].rearrange("(q r) f -> r q f", r=P), x3[:, 0:NT - 1, :]).then_inc(s_out, 16)
            sp.dma_start(out_d[(NT - 1) * P:N, :], x3[0:NREM, NT - 1, :]).then_inc(s_out, 16)
            sp.wait_ge(s_out, 32)

        @block.gpsimd
        def _(pool):
            for dst, fill in ((dst_i, -1), (src_i, 0), (typ_i, 0)):
                nc.gpsimd.memset(dst, fill).then_inc(s_fill, 1)
            nc.gpsimd.memset(nrm_f, 0.0).then_inc(s_fill, 1)
            nc.gpsimd.memset(x[:, :], 0.0).then_inc(s_fill, 1)
            nc.gpsimd.memset(ident[:, :], 0.0).then_inc(s_id0, 1)
            nc.gpsimd.memset(identh[:, :], 0.0).then_inc(s_id0, 1)
            nc.gpsimd.memset(ones[:, :], 1.0).then_inc(s_const, 1)
            nc.gpsimd.memset(onesh[:, :], 1.0).then_inc(s_const, 1)
            pool.wait_ge(s_id0, 2)
            for m in (ident, identh):
                nc.gpsimd.affine_select(out=m[:, :], in_=m[:, :], compare_op=ALU.not_equal, fill=1.0, base=0,
                                        pattern=[[-1, P]], channel_multiplier=1).then_inc(s_const, 1)
            nc.gpsimd.iota(iota_code[:, :], pattern=[[QS, NQ], [1, WIN]], base=0, channel_multiplier=0,
                           allow_small_or_imprecise_dtypes=True).then_inc(s_const, 1)
            nc.gpsimd.iota(iota_256[:, :], pattern=[[1, 256]], base=0, channel_multiplier=0,
                           allow_small_or_imprecise_dtypes=True).then_inc(s_const, 1)
            nc.gpsimd.iota(iota_p[:, :], pattern=[[P, 2]], base=0, channel_multiplier=1,
                           allow_small_or_imprecise_dtypes=True).then_inc(s_const, 1)
            nc.gpsimd.memset(adj_f[:, 0:ROW0], 0.0).then_inc(s_zero, 1)
            pool.wait_ge(s_rowready, 7)
            pool.wait_ge(s_rowt, 7)
            nc.gpsimd.memset(adj_f[:, ROW0:ADJ // 2], 0.0).then_inc(s_zero, 1)
            for n in range(K):
                nc.gpsimd.memset(rec[:, n:n + 1], 2.0 * AN[n]).then_inc(s_const, 1)
                nc.gpsimd.memset(rec[:, K + n:K + n + 1], CN[n]).then_inc(s_const, 1)
            for n in range(K + 1):
                nc.gpsimd.memset(rec[0:1, 2 * K + n:2 * K + n + 1], 1.0 / NORM[n]).then_inc(s_const, 1)
            pool.wait_ge(s_tab[0], 16 * ((NT + 1) // 2))
            pool.wait_ge(s_tab[1], 16 * (NT // 2))
            pool.wait_ge(s_loop1, 1)
            most = pool.value_load(passes[0:1, 1:2], min_val=0, max_val=NT)
            with pool.Fori(0, most // 2 + 1) as p:
                with pool.Fori(0, NG // 4) as i:
                    g = pool.snap(p * NG + i * 4)
                    for k in range(4):
                        pool.wait_ge(s_idx, g + k + 1)
                        pool.wait_ge(s_seg, g + k + 1)
                        pool.sem_inc(s_mark, 1)
                        for t in range(4):
                            pool.indirect_dma_start(out=GM[:, k, t * D:(t + 1) * D], out_offset=None, in_=msg_table,
                                                    in_offset=bass.IndirectOffsetOnAxis(ap=IDX[:, k, t:t + 1], axis=0)).then_inc(s_gath[k], 16)
            pool.wait_ge(s_node, 16)
            with pool.Fori(0, most // 2 + 1) as p:
                with pool.Fori(0, NG // 4) as i:
                    g = pool.snap(p * NG + i * 4)
                    for k in range(4):
                        pool.wait_ge(s_idx3, g + k + 1)
                        pool.wait_ge(s_t3, g + k + 1)
                        pool.sem_inc(s_mark, 1)
                        for t in range(4):
                            pool.indirect_dma_start(out=G3[:, k, t, 0:D], out_offset=None, in_=node_table,
                                                    in_offset=bass.IndirectOffsetOnAxis(ap=IDX3[:, k, t:t + 1], axis=0)).then_inc(s_in3[k], 16)

        @block.tensor
        def _(pe):
            pe.wait_ge(s_const, NCONST)
            for a, arr in enumerate(ROWS):
                pe.wait_ge(s_rowready, a + 1)
                if a >= 2:
                    pe.wait_ge(s_rowout, a - 1)
                for j in range(8):
                    b, t = j // 2, j % 2
                    bank = 2 * (a % 2) + j // 4
                    last = nc.tensor.transpose(psum[:, bank, (j % 4) * RP:(j % 4 + 1) * RP],
                                               arr[0:RP, b * HE + t:(b + 1) * HE:2], ident[0:RP, 0:RP])
                last.then_inc(s_rowt, 1)
            pe.wait_ge(s_statready, 1)
            for k in range(2):
                nc.tensor.matmul(psum[0:1, 4, k * P:(k + 1) * P], lhsT=small[:, 22 + k:23 + k], rhs=ident[:, :], start=True, stop=True)
                nc.tensor.matmul(psum[0:1, 6, k * RP:(k + 1) * RP], lhsT=small[0:RP, 12 + k:13 + k], rhs=ident[0:RP, 0:RP], start=True, stop=True)
            for b in range(4):
                last = nc.tensor.matmul(psum[0:1, 5, b * RP:(b + 1) * RP], lhsT=small[0:RP, b:b + 1], rhs=ident[0:RP, 0:RP], start=True, stop=True)
            last.then_inc(s_statrow, 1)
            pe.wait_ge(s_passes, 1)
            most = pe.value_load(passes[0:1, 0:1], min_val=0, max_val=N)
            pe.sem_inc(s_built, 2)
            with pe.Fori(0, most // WIN + 1) as p:
                with pe.Fori(0, NH // 4) as i:
                    g = pe.snap(p * NH + i * 4)
                    e = pe.snap(p * (NH + 2) + i * 4)
                    for k in range(4):
                        pe.wait_ge(s_oh, g + k + 1)
                        pe.wait_ge(s_stage, e + k + 1)
                        for t in range(2):
                            for half in range(2):
                                last = nc.tensor.matmul(psum[:, 4 + 2 * (k % 2) + half, 0:HALFQ], lhsT=OHR[:, k % 2, t, :],
                                                        rhs=OHQ[:, k % 2, t, half * HALFQ:(half + 1) * HALFQ], start=(t == 0), stop=(t == 1))
                        last.then_inc(s_built, 1)

            def transpose_adj(turn):
                for n, (q, m0, c) in enumerate(CH):
                    if n >= 4:
                        pe.wait_ge(s_tx, turn * len(CH) + n - 3)
                        pe.wait_ge(s_ty, turn * LOWER[-1] + LOWER[n - 4])
                    elif turn:
                        pe.wait_ge(s_tx, turn * len(CH))
                        pe.wait_ge(s_ty, turn * LOWER[-1])
                    bank = 2 * (n % 4)
                    for j in range(c):
                        last = nc.tensor.transpose(psum_h[:, bank, j * P:(j + 1) * P], adj_blk[:, q, m0 + j, :], identh[:, :])
                    for j in range(c):
                        if m0 + j > q:
                            last = nc.tensor.transpose(psum_h[:, bank + 1, j * P:(j + 1) * P], adj_blk[:, m0 + j, q, :], identh[:, :])
                    last.then_inc(s_tp, 1)

            def degrees(turn):
                pe.wait_ge(s_tx, (turn + 1) * len(CH))
                pe.wait_ge(s_ty, (turn + 1) * LOWER[-1])
                for m in range(NT):
                    for q in range(NT):
                        last = nc.tensor.matmul(psum[:, 0, m:m + 1], lhsT=adj_blk[:, q, m, :], rhs=onesh[:, 0:1], start=(q == 0), stop=(q == NT - 1))
                last.then_inc(s_deg, 1)

            def propagate(parts, banks_before):
                for b, (m0, m1) in enumerate(BANKS):
                    if b >= 8:
                        pe.wait_ge(s_bank, banks_before + b - 7)
                    for m in range(m0, m1):
                        for q in range(NT):
                            last = nc.tensor.matmul(psum[:, b % 8, (m - m0) * PART:(m - m0 + 1) * PART], lhsT=adj_blk[:, q, m, :],
                                                    rhs=parts[:, q, :, :], start=(q == 0), stop=(q == NT - 1))
                    last.then_inc(s_prop, 1)

            pe.wait_ge(s_adj, 1)
            transpose_adj(0)
            degrees(0)
            pe.wait_ge(s_degread, 1)
            for n in range(2):
                pe.wait_ge(s_xp, n + 1)
                propagate(XP[n], n * NB)
            pe.wait_ge(s_bank, 2 * NB)
            transpose_adj(1)
            degrees(1)
            def features(c, src, ready, ident_):
                m0, m1 = HCH[c]
                for j in range(m1 - m0):
                    last = nc.tensor.transpose(psum[0:D, 1, j * P:(j + 1) * P], src[:, m0 + j, :], ident_[:, :])
                last.then_inc(ready, 1)

            pe.wait_ge(s_w, 16 * 5)
            pe.wait_ge(s_h, 1)
            features(0, H, s_ht, ident)
            for c, (m0, m1) in enumerate(HCH):
                w = (m1 - m0) * P
                pe.wait_ge(s_htc, c + 1)
                for r in range(4):
                    nc.tensor.matmul(psum[0:96, 2 + r, 0:w], lhsT=W1R[:, r * 96:(r + 1) * 96], rhs=HT[:, c % 2, 0:w], start=True, stop=True).then_inc(s_h1, 1)
                if c + 1 < len(HCH):
                    features(c + 1, H, s_ht, ident)
                pe.wait_ge(s_h1r, 4 * c + 4)
                for j in range(m1 - m0):
                    q = m0 + j
                    if q >= 2:
                        pe.wait_ge(s_h2c, q - 1)
                    for r in range(4):
                        last = nc.tensor.matmul(psum[:, 6 + q % 2, r * 96:(r + 1) * 96], lhsT=H1T[:, r, j * P:(j + 1) * P], rhs=W2R[:, r, :], start=True, stop=True)
                    last.then_inc(s_h2, 1)
            pe.sem_inc(s_seg, 4)
            most = pe.value_load(passes[0:1, 1:2], min_val=0, max_val=NT)
            with pe.Fori(0, most // 2 + 1) as p:
                with pe.Fori(0, NG // 4) as i:
                    g = pe.snap(p * NG + i * 4)
                    u = pe.snap((p * (NG // 4) + i) * 64)
                    for k in range(4):
                        pe.wait_ge(s_woh, g + k + 1)
                        pe.wait_ge(s_gath[k], u + 64)
                        pe.wait_ge(s_acc, g + k + 1)
                        for w in range(2):
                            for t in range(4):
                                last = nc.tensor.matmul(psum[:, 4 + k % 2, w * D:(w + 1) * D], lhsT=WOH[:, k % 2, t, w * P:(w + 1) * P],
                                                        rhs=GM[:, k, t * D:(t + 1) * D], start=(t == 0), stop=(t == 3))
                        last.then_inc(s_seg, 1)
            pe.wait_ge(s_coef, 1)
            nc.tensor.matmul(psum[:, 7, 0:K + 1], lhsT=ones[0:1, :], rhs=small[0:1, 32:32 + K + 1], start=True, stop=True).then_inc(s_coefb, 1)
            with pe.Fori(0, K // 2) as i:
                for u in range(2):
                    pe.wait_ge(s_xp, i * 2 + (3 + u))
                    propagate(XP[u], pe.snap(i * (2 * NB) + (2 + u) * NB))
            pe.wait_ge(s_w3in, 16 * 8)
            pe.wait_ge(s_h, 2)
            features(0, H3, s_ht3, ident)
            for c, (m0, m1) in enumerate(HCH):
                pe.wait_ge(s_htc3, c + 1)
                if c >= 2:
                    pe.wait_ge(s_pdc, c - 1)
                for j in range(m1 - m0):
                    last = nc.tensor.matmul(psum[:, 2 + c % 2, j * HID:(j + 1) * HID], lhsT=HT3[0:D, c % 2, j * P:(j + 1) * P], rhs=W1B[0:D, :], start=True, stop=True)
                last.then_inc(s_pd, 1)
                if c + 1 < len(HCH):
                    features(c + 1, H3, s_ht3, ident)
            pe.wait_ge(s_pdc, len(HCH))
            tile = [pe.alloc_register(f"pe_tile{k}") for k in range(4)]
            pe.sem_inc(s_t3, 4)
            pe.sem_inc(s_z1, 2)
            pe.sem_inc(s_z2, 2)
            pe.sem_inc(s_w3, 2)
            pe.sem_inc(s_seg3, 2)

            def inputs_t(k, n, used):
                pe.wait_ge(s_ef[k], used)
                pe.wait_ge(s_in3[k], used * 2)
                pe.wait_ge(s_gt, n)
                pe.sem_inc(s_mark, 1)
                for t in range(4):
                    last = nc.tensor.transpose(psum[0:64, 4, t * P:(t + 1) * P], G3[:, k, t, :], ident[:, :])
                last.then_inc(s_t3, 1)

            def layer1(k, n, first_tile):
                pe.wait_ge(s_gt, n + 1)
                pe.wait_ge(s_r1, n + 1)
                nc.tensor.matmul(psum[:, k % 2, :], lhsT=W1AC[0:64, :], rhs=GT[0:64, k % 2, :], start=True, stop=False)
                pe.wait_ge(s_oht, n + 5)
                for w in range(2):
                    for c in range(3):
                        last = nc.tensor.matmul(psum[:, k % 2, :], lhsT=PD[:, bass.ds(first_tile * (3 * HID) + (w * 3 + c) * HID, HID)],
                                                rhs=OHT[:, k % 2, w, :], start=False, stop=(w == 1 and c == 2))
                last.then_inc(s_z1, 1)

            def layer2(k, n):
                pe.wait_ge(s_r1, n + 3)
                pe.wait_ge(s_r2, n + 1)
                nc.tensor.matmul(psum[:, 2 + k % 2, :], lhsT=W2M, rhs=R1[:, k % 2, :], start=True, stop=True).then_inc(s_z2, 1)

            def layer3(k, n):
                pe.wait_ge(s_r2, n + 3)
                pe.wait_ge(s_msg, n)
                for t in range(4):
                    last = nc.tensor.matmul(psum[:, 5, t * D:(t + 1) * D], lhsT=R2[:, k % 2, t * P:(t + 1) * P], rhs=W3M, start=True, stop=True)
                last.then_inc(s_w3, 1)

            def sums(k, n):
                pe.wait_ge(s_ohf, n + 1)
                pe.wait_ge(s_msg, n + 1)
                pe.wait_ge(s_acc3, n + 1)
                for w in range(2):
                    for t in range(4):
                        last = nc.tensor.matmul(psum[:, 6 + k % 2, w * D:(w + 1) * D], lhsT=OHF[:, k % 2, t, w * P:(w + 1) * P],
                                                rhs=MS[:, k % 2, t * D:(t + 1) * D], start=(t == 0), stop=(t == 3))
                last.then_inc(s_seg3, 1)

            def mlp(i, n, used, first=False, last=False):
                at = slice(2 + i * 4, 6 + i * 4) if isinstance(i, int) else bass.ds(i * 4 + 2, 4)
                pe.load(tile, TILE3[0:1, at])
                for k in range(4):
                    layer1(k, n + k, pe.snap(tile[k], min_val=0, max_val=NT))
                    if not (last and k == 3):
                        inputs_t((k + 1) % 4, n + (k + 1), used + (32 if k < 3 else 64))
                    if not (first and k == 0):
                        layer3(k - 1, n + (k - 1))
                    if not (first and k < 2):
                        sums(k - 2, n + (k - 2))
                    layer2(k, n + k)

            with pe.Fori(0, most // 2 + 1) as p:
                pe.wait_ge(s_shift3, p * 3 + 2)
                pe.wait_ge(s_clamp, p + 1)
                for j in range(7):
                    last = nc.tensor.transpose(psum[0:NC // 7, 2 * (j // 4), (j % 4) * P:(j % 4 + 1) * P], CLAMP[:, j * (NC // 7):(j + 1) * (NC // 7)], ident[:, :])
                last.then_inc(s_relt, 1)
                pe.wait_ge(s_reltc, p + 1)
                inputs_t(0, pe.snap(p * NG), pe.snap(p * (32 * NG // 4) + 32))
                mlp(0, pe.snap(p * NG), pe.snap(p * (32 * NG // 4)), first=True)
                with pe.Fori(1, NG // 4 - 1) as i:
                    mlp(i, pe.snap(p * NG + i * 4), pe.snap(p * (32 * NG // 4) + i * 32))
                mlp(NG // 4 - 1, pe.snap(p * NG + (NG - 4)), pe.snap(p * (32 * NG // 4) + 32 * (NG // 4 - 1)), last=True)
                layer3(3, pe.snap(p * NG + (NG - 1)))
                sums(2, pe.snap(p * NG + (NG - 2)))
                sums(3, pe.snap(p * NG + (NG - 1)))

        @block.scalar
        def _(act):
            for a, dest in enumerate(COLS):
                act.wait_ge(s_rowt, a + 1)
                for hf in range(2):
                    last = nc.scalar.activation(dest.rearrange("p (c j) -> p j c", j=8)[:, 4 * hf:4 * hf + 4, :],
                                                psum[:, 2 * (a % 2) + hf, 0:4 * RP].rearrange("p (j c) -> p j c", j=4), ACT.Copy)
                last.then_inc(s_rowout, 1)
            act.wait_ge(s_passes, 1)
            most = act.value_load(passes[0:1, 0:1], min_val=0, max_val=N)
            with act.Fori(0, most // WIN + 1) as p:
                with act.Fori(0, NH // 4) as i:
                    g = act.snap(p * NH + i * 4)
                    e = act.snap(p * (NH + 2) + i * 4)
                    for k in range(4):
                        act.wait_ge(s_built, g + k + 3)
                        act.wait_ge(s_add, e + k + 1)
                        nc.scalar.activation(STG[:, k % 2, :].rearrange("p (h c) -> p h c", h=2),
                                             psum[:, 4 + 2 * (k % 2):6 + 2 * (k % 2), 0:HALFQ], ACT.Copy, scale=0.5).then_inc(s_stage, 1)

            def transpose_adj(turn):
                for n, (q, m0, c) in enumerate(CH):
                    lo = max(m0, q + 1)
                    if m0 + c > lo:
                        act.wait_ge(s_tp, turn * len(CH) + n + 1)
                        nc.scalar.activation(adj_blk[:, q, lo:m0 + c, :],
                                             psum_h[:, 2 * (n % 4) + 1, (lo - m0) * P:c * P].rearrange("p (j r) -> p j r", r=P),
                                             ACT.Copy).then_inc(s_ty, 1)

            def root(n):
                act.wait_ge(s_var, n + 1)
                nc.scalar.activation(st(4), st(3), ACT.Sqrt).then_inc(s_root, 1)

            transpose_adj(0)
            root(0)
            root(1)
            transpose_adj(1)
            root(2)
            act.wait_ge(s_w, 16 * 5)
            for c, (m0, m1) in enumerate(HCH):
                w = (m1 - m0) * P
                if c:
                    act.wait_ge(s_h2, m0)
                for r in range(4):
                    act.wait_ge(s_h1, 4 * c + r + 1)
                    nc.scalar.activation(H1T[:, r, 0:w], psum[0:96, 2 + r, 0:w], ACT.Relu, bias=B1R).then_inc(s_h1r, 1)
            root(3)
            act.wait_ge(s_loop1, 1)
            most = act.value_load(passes[0:1, 1:2], min_val=0, max_val=NT)
            with act.Fori(0, most // 2 + 1) as p:
                with act.Fori(0, NG // 4) as i:
                    u = act.snap((p * (NG // 4) + i) * 64)
                    for k in range(4):
                        act.wait_ge(s_gath[k], u)
                        nc.scalar.copy(IDX[:, k, :], idx_msg[:, bass.ds(i * 16 + 4 * k, 4)]).then_inc(s_idx, 1)
            act.wait_ge(s_lapin, 32)
            nc.scalar.activation(small[0:1, 0:K + 1], small[0:1, 0:K + 1], ACT.Tanh).then_inc(s_lap, 1)
            root(4)
            root(5)
            act.sem_inc(s_r1, 2)
            act.sem_inc(s_r2, 2)
            act.wait_ge(s_w3in, 16 * 8)

            def stage(g, k, used):
                act.wait_ge(s_in3[k], used)
                nc.scalar.copy(IDX3[:, k, :], idx_src[:, g]).then_inc(s_idx3, 1)

            def inputs_out(k, n):
                act.wait_ge(s_t3, n + 5)
                act.wait_ge(s_z1, n + 1)
                nc.scalar.activation(GT[0:64, k % 2, :], psum[0:64, 4, :], ACT.Copy).then_inc(s_gt, 1)

            def mlp(i, n, used, last=False):
                for k in range(4):
                    act.wait_ge(s_z1, n + (k + 3))
                    act.wait_ge(s_z2, n + (k + 1))
                    nc.scalar.activation(R1[:, k % 2, :], psum[:, k % 2, :], ACT.Relu, bias=BM[:, 0:1]).then_inc(s_r1, 1)
                    if not (last and k == 3):
                        inputs_out(k + 1, n + (k + 1))
                    if not (last and k >= 2):
                        at = slice(i * 16 + 4 * k + 8, i * 16 + 4 * k + 12) if isinstance(i, int) else bass.ds(i * 16 + (4 * k + 8), 4)
                        stage(at, (k + 2) % 4, used + (0 if k < 2 else 64))
                    act.wait_ge(s_z2, n + (k + 3))
                    act.wait_ge(s_w3, n + (k + 1))
                    nc.scalar.activation(R2[:, k % 2, :], psum[:, 2 + k % 2, :], ACT.Relu, bias=BM[:, 1:2]).then_inc(s_r2, 1)

            with act.Fori(0, most // 2 + 1) as p:
                act.wait_ge(s_relt, p + 1)
                for j in range(2):
                    w = (4, 3)[j]
                    last = nc.scalar.activation(RELT[0:NC // 7, 4 * j:4 * j + w, :], psum[0:NC // 7, 2 * j, 0:w * P].rearrange("p (j c) -> p j c", j=w), ACT.Copy)
                last.then_inc(s_reltc, 1)
                for k in range(2):
                    stage(slice(4 * k, 4 * k + 4), k, act.snap(p * (64 * NG // 4)))
                inputs_out(0, act.snap(p * NG))
                with act.Fori(0, NG // 4 - 1) as i:
                    mlp(i, act.snap(p * NG + i * 4), act.snap(p * (64 * NG // 4) + i * 64))
                mlp(NG // 4 - 1, act.snap(p * NG + (NG - 4)), act.snap(p * (64 * NG // 4) + 64 * (NG // 4 - 1)), last=True)

        @block.vector
        def _(dve):
            V = Count(dve, v_seq)
            vec = nc.vector
            dve.wait_ge(s_in, 16 * 8)
            dve.wait_ge(s_const, NCONST)
            t_ai, t_bi = t_a.bitcast(I32), t_b.bitcast(I32)
            v4 = lambda a: a.rearrange("p (b c) -> p b c", b=4)
            v2 = lambda a: a.rearrange("p (b c) -> p b c", b=2)
            V.do(vec.tensor_copy(dst_f, dst_i))
            V.do(vec.tensor_scalar(t_a, dst_f, 0.0, BIG, ALU.is_lt, ALU.mult))
            V.do(vec.tensor_tensor(t_a, t_a, dst_f, ALU.add))
            V.did(vec.tensor_reduce(small[:, 4:8], v4(dst_f), AX.X, ALU.max))
            V.do(vec.tensor_reduce(small[:, 24:28], v4(t_a), AX.X, ALU.min))
            V.do(vec.tensor_scalar(small[:, 0:4], small[:, 24:28], float(N - 1), None, ALU.min))
            V.did(vec.tensor_reduce(small[:, 8:10], small[:, 0:4].rearrange("p (a b) -> p a b", b=2), AX.X, ALU.min))
            V.do(vec.tensor_reduce(small[:, 10:12], small[:, 4:8].rearrange("p (a b) -> p a b", b=2), AX.X, ALU.max))
            V.do(vec.tensor_copy(smi[:, 0:4], small[:, 8:12]))
            V.do(vec.tensor_scalar(smi[:, 4:8], smi[:, 0:4], 7, None, ALU.arith_shift_right))
            V.do(vec.tensor_copy(small[:, 12:16], smi[:, 4:8]))
            V.did(vec.tensor_tensor(small[:, 16:18], small[:, 14:16], small[:, 12:14], ALU.subtract))
            V.do(vec.tensor_tensor(small[:, 18:22], small[:, 4:8], small[:, 0:4], ALU.subtract))
            V.did(vec.tensor_reduce(small[:, 22:23], small[:, 18:22], AX.X, ALU.max))
            V.do(vec.tensor_reduce(small[:, 23:24], small[:, 16:18], AX.X, ALU.max))
            vec.tensor_scalar(small[:, 28:30], small[:, 12:14], float(P), None, ALU.mult).then_inc(s_statready, 1)
            dve.wait_ge(s_statready, 1)
            vec.tensor_tensor(v4(t_b), v4(dst_f), bc(small[:, 0:4], HE), ALU.subtract).then_inc(s_rowready, 1)
            V.did(vec.tensor_scalar(t_ai, src_i, 7, None, ALU.arith_shift_right))
            V.all()
            vec.tensor_scalar(t_c, t_ai, float(QS), None, ALU.mult).then_inc(s_rowready, 1)
            dve.wait_ge(s_rowready, 2)
            V.do(vec.tensor_scalar(t_ai, src_i, P - 1, None, ALU.bitwise_and))
            dve.wait_ge(s_rowt, 1)
            vec.tensor_copy(t_b, t_ai).then_inc(s_rowready, 1)
            dve.wait_ge(s_rowt, 2)
            vec.tensor_tensor(v2(t_c), v2(dst_f), bc(small[:, 28:30], 2 * HE), ALU.subtract).then_inc(s_rowready, 1)
            dve.wait_ge(s_rowt, 3)
            vec.scalar_tensor_tensor(t_b, src_i, float(REL), typ_i, ALU.mult, ALU.add).then_inc(s_rowready, 1)
            dve.wait_ge(s_rowt, 4)
            V.did(vec.tensor_copy(t_c, src_i))
            V.all()
            dve.sem_inc(s_rowready, 2)
            dve.wait_ge(s_statrow, 1)
            V.did(vec.tensor_reduce(small[0:1, 32:34], psum[0:1, 4, 0:2 * P].rearrange("p (a b) -> p a b", b=P), AX.X, ALU.max))
            V.did(vec.tensor_copy(base_row[0:1, 2:2 + NH].rearrange("o (c b) -> o b c", b=4), psum[0:1, 5, 0:4 * RP].rearrange("o (b c) -> o b c", c=RP)))
            V.did(vec.memset(base_row[0:1, 0:2], LASTBASE))
            V.did(vec.tensor_copy(tile_row[0:1, :].rearrange("o (c b) -> o b c", b=2), psum[0:1, 6, 0:2 * RP].rearrange("o (b c) -> o b c", c=RP)))
            V.all()
            V.do(vec.tensor_scalar(small[0:1, 34:36], small[0:1, 32:34], 0.0, None, ALU.max))
            vec.tensor_copy(passes[0:1, :], small[0:1, 34:36]).then_inc(s_passes, 1)
            dve.wait_ge(s_passes, 1)
            dve.wait_ge(s_rowout, 7)
            dve.wait_ge(s_zero, 2)
            most = dve.value_load(passes[0:1, 0:1], min_val=0, max_val=N)
            base = [dve.alloc_register(f"base{k}") for k in range(4)]
            adj_at = lambda b: adj3[:, :, bass.ds(b, WIN)]

            def add_step(k, b, count):
                b = dve.snap(b, min_val=0, max_val=LASTBASE)
                dve.wait_ge(s_stage, count + 1)
                dve.wait_ge(s_add, count)
                vec.tensor_tensor(adj_at(b), adj_at(b), STG[:, k % 2, 0:NT * WIN].rearrange("p (q c) -> p q c", c=WIN), ALU.add).then_inc(s_add, 1)

            with dve.Fori(0, most // WIN + 1) as p:
                g0 = dve.snap(p * NH)
                e0 = dve.snap(p * (NH + 2))
                c0 = dve.snap(p * 4)
                dve.wait_ge(s_add, e0)
                for k in range(2):
                    vec.memset(STG[:, k, :], 0.0).then_inc(s_stage, 1)
                dve.wait_ge(s_oh, g0)
                dve.wait_ge(s_code, c0)
                vec.tensor_scalar(code_c, rel_a, -1.0, float(WIN), ALU.max, ALU.min).then_inc(s_code, 1)
                dve.wait_ge(s_code, c0 + 1)
                vec.tensor_tensor(code_c, code_c, q_c, ALU.add).then_inc(s_code, 1)
                vec.tensor_scalar(rel_a, rel_a, float(WIN), None, ALU.subtract).then_inc(s_code, 1)
                dve.wait_ge(s_code, c0 + 3)
                dve.sem_inc(s_mark, 1)
                with dve.Fori(0, NH // 4) as i:
                    g = dve.snap(p * NH + i * 4)
                    e = dve.snap(p * (NH + 2) + i * 4)
                    dve.load(base, base_row[0:1, bass.ds(i * 4, 4)])
                    for k in range(4):
                        dve.wait_ge(s_built, g + k + 1)
                        for t in range(2):
                            vec.tensor_scalar(OHQ[:, k % 2, t, :], iota_code[:, :], code_c[:, bass.ds(i * 8 + (2 * k + t), 1)], None, ALU.is_equal)
                        for t in range(2):
                            last = vec.tensor_scalar(OHR[:, k % 2, t, :], iota_256[:, 0:P], r_c[:, bass.ds(i * 8 + (2 * k + t), 1)], None, ALU.is_equal)
                        last.then_inc(s_oh, 1)
                        add_step(k, base[k], e + k)
                dve.load(base[0:2], base_row[0:1, NH:NH + 2])
                for k in range(2):
                    add_step(k, base[k], e0 + (NH + k))
                dve.wait_ge(s_add, e0 + (NH + 2))
                vec.tensor_scalar(base_row[0:1, 2:2 + NH], base_row[0:1, 2:2 + NH], float(WIN), float(LASTBASE), ALU.add, ALU.min).then_inc(s_code, 1)
                dve.wait_ge(s_code, c0 + 4)
            dve.sem_inc(s_adj, 1)

            def transpose_adj(turn):
                for n, (q, m0, c) in enumerate(CH):
                    dve.wait_ge(s_tp, turn * len(CH) + n + 1)
                    vec.tensor_copy(adj_blk[:, m0:m0 + c, q, :], psum_h[:, 2 * (n % 4), 0:c * P].rearrange("p (j r) -> p j r", r=P)).then_inc(s_tx, 1)

            roots = [0]

            def inv_root(out, v, n):
                dve.sem_inc(s_var, 1)
                roots[0] += 1
                dve.wait_ge(s_root, roots[0])
                V.do(vec.reciprocal(st(5), st(4)))
                V.do(vec.tensor_tensor(st(6), st(5), st(5), ALU.mult))
                V.do(vec.tensor_tensor(st(6), st(6), st(3), ALU.mult))
                V.do(vec.tensor_scalar(st(6), st(6), -0.5, 1.5, ALU.mult, ALU.add))
                V.do(vec.tensor_tensor(out, st(5), st(6), ALU.mult))

            def layernorm(h, t):
                V.do(vec.tensor_reduce(st(0), x3, AX.X, ALU.add))
                V.do(vec.tensor_scalar(st(1), st(0), 1.0 / D, None, ALU.mult))
                V.do(vec.tensor_tensor(h, x3, bc(st(1)), ALU.subtract))
                V.do(vec.tensor_tensor(t, h, h, ALU.mult))
                V.do(vec.tensor_reduce(st(2), t, AX.X, ALU.add))
                V.do(vec.tensor_scalar(st(3), st(2), 1.0 / D, 1e-5, ALU.mult, ALU.add))
                inv_root(st(7), st(3), 0)
                V.do(vec.scalar_tensor_tensor(h, h, 0.0, bc(st(7)), ALU.max, ALU.mult))

            def split(parts, z, r, m0, m1, did=None):
                X = parts[:, m0:m1, :, :]
                V.do(vec.tensor_copy(X[:, :, 0, :], z))
                V.do(vec.tensor_tensor(r, z, X[:, :, 0, :], ALU.subtract))
                V.do(vec.tensor_copy(X[:, :, 1, :], r))
                V.do(vec.tensor_tensor(X[:, :, 2, :], r, X[:, :, 1, :], ALU.subtract))

            transpose_adj(0)
            dve.wait_ge(s_x, 32)
            V.all()
            layernorm(PA, PB)
            dve.wait_ge(s_deg, 1)
            vec.tensor_scalar(st(3), psum[:, 0, 0:NT], 2.0, 1.0, ALU.mult, ALU.add).then_inc(s_degread, 1)
            dve.wait_ge(s_degread, 1)
            inv_root(st(8), st(3), 0)
            V.do(vec.tensor_tensor(PA, PA, bc(st(8)), ALU.mult))
            split(XP[0], PA, PB, 0, NT)
            dve.sem_inc(s_xp, 1)
            for n in range(2):
                for b, (m0, m1) in enumerate(BANKS):
                    w = m1 - m0
                    z, y, r = PA[:, m0:m1, :], TY[:, 0:w, :], TR[:, 0:w, :]
                    dve.wait_ge(s_prop, n * NB + b + 1)
                    vec.tensor_reduce(y, psum[:, b % 8, 0:w * PART].rearrange("p (m c f) -> p m f c", c=3, f=D), AX.X, ALU.add).then_inc(s_bank, 1)
                    dve.wait_ge(s_bank, n * NB + b + 1)
                    V.do(vec.scalar_tensor_tensor(y, y, 2.0, z, ALU.mult, ALU.add))
                    V.do(vec.tensor_tensor(y, y, bc(st(8)[:, m0:m1]), ALU.mult))
                    if n == 0:
                        V.do(vec.tensor_tensor(z, y, bc(st(8)[:, m0:m1]), ALU.mult))
                        split(XP[1], z, r, m0, m1)
                    else:
                        V.do(vec.tensor_tensor(x3[:, m0:m1, :], x3[:, m0:m1, :], y, ALU.add))
                if n == 0:
                    dve.sem_inc(s_xp, 1)
            V.all()
            V.do(vec.memset(W2R, 0.0))
            dve.sem_inc(s_wz, 1)
            transpose_adj(1)
            layernorm(H, LNT)
            dve.sem_inc(s_h, 1)
            dve.wait_ge(s_deg, 2)
            V.do(vec.tensor_scalar(cnt_in[:, :], psum[:, 0, 0:NT], 2.0, None, ALU.mult))

            def features_out(c, dest, ready, done):
                dve.wait_ge(ready, c + 1)
                w = (HCH[c][1] - HCH[c][0]) * P
                vec.tensor_copy(dest[0:D, c % 2, 0:w], psum[0:D, 1, 0:w]).then_inc(done, 1)

            features_out(0, HT, s_ht, s_htc)
            for c, (m0, m1) in enumerate(HCH):
                if c + 1 < len(HCH):
                    features_out(c + 1, HT, s_ht, s_htc)
                for q in range(m0, m1):
                    dve.wait_ge(s_h2, q + 1)
                    if q >= 2:
                        dve.wait_ge(s_tab[q % 2], 16 * (q // 2))
                    vec.tensor_copy(H2[:, q % 2, :], psum[:, 6 + q % 2, 0:384]).then_inc(s_h2c, 1)
            V.do(vec.tensor_scalar(st(3), cnt_in[:, :], 1.0, None, ALU.max))
            inv_root(st(7), st(3), 0)
            V.do(vec.tensor_scalar(st(6), cnt_in[:, :], 0.0, None, ALU.is_gt))
            V.do(vec.tensor_tensor(dinv_in[:, :], st(7), st(6), ALU.mult))
            dve.wait_ge(s_tab[0], 16 * ((NT + 1) // 2))
            dve.wait_ge(s_tab[1], 16 * (NT // 2))
            V.did(vec.memset(ACC, 0.0))
            V.did(vec.tensor_copy(REL1, rel_b[:, :]))
            V.do(vec.tensor_copy(TILE1, tile_row[0:1, :]))
            dve.sem_inc(s_loop1, 1)
            dve.sem_inc(s_acc, 2)
            most = dve.value_load(passes[0:1, 1:2], min_val=0, max_val=NT)
            with dve.Fori(0, most // 2 + 1) as p:
                with dve.Fori(0, NG // 4) as i:
                    g = dve.snap(p * NG + i * 4)
                    dve.load(base, TILE1[0:1, bass.ds(i * 4, 4)])
                    for k in range(4):
                        dve.wait_ge(s_seg, g + (k + 3))
                        for t in range(4):
                            col = i * 16 + (4 * k + t)
                            last = vec.tensor_scalar(WOH[:, k % 2, t, :], iota_256[:, :], REL1[:, bass.ds(col, 1)], norm_c[:, bass.ds(col, 1)],
                                                     ALU.is_equal, ALU.mult)
                        last.then_inc(s_woh, 1)
                        dve.wait_ge(s_seg, g + (k + 5))
                        dve.wait_ge(s_acc, g + (k + 2))
                        at = ACC[:, bass.ds(dve.snap(base[k], min_val=0, max_val=NT) * D, 2 * D)]
                        vec.tensor_tensor(at, at, psum[:, 4 + k % 2, 0:2 * D], ALU.add).then_inc(s_acc, 1)
                dve.wait_ge(s_woh, p * NG + NG)
                vec.tensor_scalar(REL1, REL1, 2.0 * P, None, ALU.subtract).then_inc(s_shift, 1)
                vec.tensor_scalar(TILE1, TILE1, 2.0, float(NT), ALU.add, ALU.min).then_inc(s_shift, 1)
                dve.wait_ge(s_shift, p * 2 + 2)
                dve.wait_ge(s_acc, p * NG + (NG + 2))
            acc1 = ACC[:, 0:NT * D].rearrange("p (q f) -> p q f", f=D)
            dve.wait_ge(s_w, 16 * 6)
            V.do(vec.tensor_tensor(acc1, acc1, B2R.unsqueeze(1).broadcast_to((P, NT, D)), ALU.add))
            V.do(vec.scalar_tensor_tensor(x3, acc1, 0.0, x3, ALU.max, ALU.add))
            dve.wait_ge(s_lap, 1)
            dve.wait_ge(s_const, NCONST + 3 * K + 1)
            sm = lambda a, b: small[0:1, a:b]
            for n in range(1, K):
                V.do(vec.tensor_tensor(sm(n, n + 1), sm(n, n + 1), sm(n - 1, n), ALU.mult))
            V.do(vec.tensor_tensor(sm(32, 33 + K), sm(16, 17 + K), rec[0:1, 2 * K:3 * K + 1], ALU.mult))
            V.do(vec.tensor_tensor(sm(33, 33 + K), sm(33, 33 + K), sm(0, K), ALU.mult))
            dve.sem_inc(s_coef, 1)
            dve.wait_ge(s_coefb, 1)
            V.do(vec.tensor_copy(small[:, 48:48 + K + 1], psum[:, 7, 0:K + 1]))
            layernorm(PA, PB)
            V.do(vec.memset(PB, 0.0))
            V.do(vec.scalar_tensor_tensor(x3, PA, small[:, 48:49], x3, ALU.mult, ALU.add))
            for b, (m0, m1) in enumerate(BANKS):
                V.do(vec.tensor_tensor(TY[:, 0:m1 - m0, :], PA[:, m0:m1, :], bc(dinv_in[:, m0:m1]), ALU.mult))
                split(XP[0], TY[:, 0:m1 - m0, :], TR[:, 0:m1 - m0, :], m0, m1)
            dve.sem_inc(s_xp, 1)
            L = Count(dve, v_l2)
            PER = 2 * (1 + 8 * NB)
            with dve.Fori(0, K // 2) as i:
                L.base = dve.snap(i * PER)
                for u in range(2):
                    new = (PB, PA)[u]
                    n = i * 2 + u
                    L.do(vec.tensor_scalar(st(0), dinv_in[:, :], rec[:, bass.ds(n, 1)], None, ALU.mult))
                    for b, (m0, m1) in enumerate(BANKS):
                        w = m1 - m0
                        y, r, pn = TY[:, 0:w, :], TR[:, 0:w, :], new[:, m0:m1, :]
                        dve.wait_ge(s_prop, i * (2 * NB) + ((2 + u) * NB + b + 1))
                        vec.tensor_reduce(y, psum[:, b % 8, 0:w * PART].rearrange("p (m c f) -> p m f c", c=3, f=D), AX.X, ALU.add).then_inc(s_bank, 1)
                        dve.wait_ge(s_bank, i * (2 * NB) + ((2 + u) * NB + b + 1))
                        L.do(vec.tensor_tensor(y, y, bc(st(0)[:, m0:m1]), ALU.mult))
                        L.do(vec.scalar_tensor_tensor(pn, pn, rec[:, bass.ds(n + K, 1)], y, ALU.mult, ALU.add))
                        L.did(vec.scalar_tensor_tensor(x3[:, m0:m1, :], pn, small[:, bass.ds(n + 49, 1)], x3[:, m0:m1, :], ALU.mult, ALU.add))
                        L.do(vec.tensor_tensor(y, pn, bc(dinv_in[:, m0:m1]), ALU.mult))
                        X = XP[1 - u][:, m0:m1, :, :]
                        L.do(vec.tensor_copy(X[:, :, 0, :], y))
                        L.do(vec.tensor_tensor(r, y, X[:, :, 0, :], ALU.subtract))
                        L.do(vec.tensor_copy(X[:, :, 1, :], r))
                        L.do(vec.tensor_tensor(X[:, :, 2, :], r, X[:, :, 1, :], ALU.subtract))
                    dve.sem_inc(s_xp, 1)
                assert L.n == PER
            dve.sem_inc(s_l2done, 1)
            layernorm(H3, LNT3)
            dve.sem_inc(s_h, 1)
            V.did(vec.memset(PD[:, NT * 3 * HID:NWT * 3 * HID], 0.0))
            V.did(vec.memset(ACC3, 0.0))
            V.did(vec.tensor_copy(REL3, rel_b[:, :]))
            V.did(vec.memset(TILE3[0:1, 0:2], NT))
            V.did(vec.tensor_copy(TILE3[0:1, 2:2 + NG], tile_row[0:1, :]))
            V.all()
            dve.sem_inc(s_shift3, 2)
            features_out(0, HT3, s_ht3, s_htc3)
            for c, (m0, m1) in enumerate(HCH):
                w = (m1 - m0) * HID
                if c + 1 < len(HCH):
                    features_out(c + 1, HT3, s_ht3, s_htc3)
                dve.wait_ge(s_pd, c + 1)
                z = psum[:, 2 + c % 2, 0:w].rearrange("p (q f) -> p q f", f=HID)
                X = PD[:, m0 * 3 * HID:m1 * 3 * HID].rearrange("p (q j f) -> p q j f", j=3, f=HID)
                r = PDR[:, 0:w].rearrange("p (q f) -> p q f", f=HID)
                V.do(vec.tensor_copy(X[:, :, 0, :], z))
                V.do(vec.tensor_tensor(r, z, X[:, :, 0, :], ALU.subtract))
                V.do(vec.tensor_copy(X[:, :, 1, :], r))
                V.do(vec.tensor_tensor(X[:, :, 2, :], r, X[:, :, 1, :], ALU.subtract))
                dve.sem_inc(s_pdc, 1)
            dve.sem_inc(s_oht, 4)
            dve.sem_inc(s_acc3, 2)

            def one_hot_t(k, n, used):
                dve.wait_ge(s_rel3[k], used)
                dve.wait_ge(s_z1, n + 1)
                for w in range(2):
                    last = vec.tensor_scalar(OHT[:, k % 2, w, :], REL_ROW[:, k, :], iota_p[:, w:w + 1], None, ALU.is_equal)
                last.then_inc(s_oht, 1)

            def one_hot(k, n, cols):
                dve.wait_ge(s_seg3, n + 1)
                for t in range(4):
                    last = vec.tensor_scalar(OHF[:, k % 2, t, :], iota_256[:, :], REL3[:, cols(t)], None, ALU.is_equal)
                last.then_inc(s_ohf, 1)

            def message(k, n):
                dve.wait_ge(s_w3, n + 3)
                vec.tensor_copy(MS[:, k % 2, :], psum[:, 5, 0:4 * D]).then_inc(s_msg, 1)

            def add_sums(k, n, tile):
                dve.wait_ge(s_seg3, n + 3)
                dve.wait_ge(s_acc3, n + 2)
                at = ACC3[:, bass.ds(dve.snap(tile, min_val=0, max_val=NT) * D, 2 * D)]
                vec.tensor_tensor(at, at, psum[:, 6 + k % 2, 0:2 * D], ALU.add).then_inc(s_acc3, 1)

            def mlp(i, n, used, first=False, last=False):
                at = slice(i * 4, 4 + i * 4) if isinstance(i, int) else bass.ds(i * 4, 4)
                dve.load(base, TILE3[0:1, at])
                for k in range(4):
                    if not (last and k == 3):
                        one_hot_t((k + 1) % 4, n + (k + 1), used + (16 if k < 3 else 32))
                    if not (first and k == 0):
                        cols = (lambda t: slice(i * 16 + 4 * k - 4 + t, i * 16 + 4 * k - 3 + t)) if isinstance(i, int) else \
                            (lambda t: bass.ds(i * 16 + (4 * k - 4 + t), 1))
                        one_hot(k - 1, n + (k - 1), cols)
                        message(k - 1, n + (k - 1))
                    if not (first and k < 2):
                        add_sums(k - 2, n + (k - 2), base[k])

            with dve.Fori(0, most // 2 + 1) as p:
                n0 = dve.snap(p * NG)
                dve.wait_ge(s_relt, p)
                vec.tensor_scalar(CLAMP, REL3, -1.0, 2.0 * P, ALU.max, ALU.min).then_inc(s_clamp, 1)
                one_hot_t(0, n0, dve.snap(p * (16 * NG // 4) + 16))
                mlp(0, n0, dve.snap(p * (16 * NG // 4)), first=True)
                with dve.Fori(1, NG // 4 - 1) as i:
                    mlp(i, dve.snap(p * NG + i * 4), dve.snap(p * (16 * NG // 4) + i * 16))
                n1 = dve.snap(p * NG + (NG - 4))
                mlp(NG // 4 - 1, n1, dve.snap(p * (16 * NG // 4) + 16 * (NG // 4 - 1)), last=True)
                one_hot(3, n1 + 3, lambda t: slice(NC - 4 + t, NC - 3 + t))
                message(3, n1 + 3)
                dve.load(base[0:2], TILE3[0:1, NG:NG + 2])
                add_sums(2, n1 + 2, base[0])
                add_sums(3, n1 + 3, base[1])
                dve.wait_ge(s_acc3, n0 + (NG + 2))
                vec.tensor_scalar(REL3, REL3, 2.0 * P, None, ALU.subtract).then_inc(s_shift3, 1)
                vec.tensor_scalar(TILE3[0:1, 2:2 + NG], TILE3[0:1, 2:2 + NG], 2.0, float(NT), ALU.add, ALU.min).then_inc(s_shift3, 2)
                dve.wait_ge(s_shift3, p * 3 + 5)
            acc3 = ACC3[:, 0:NT * D].rearrange("p (q f) -> p q f", f=D)
            V.do(vec.tensor_scalar(st(0), cnt_in[:, :], 1.0, None, ALU.max))
            V.do(vec.reciprocal(st(1), st(0)))
            V.do(vec.tensor_tensor(acc3, acc3, bc(st(1)), ALU.mult))
            V.do(vec.tensor_scalar(st(2), cnt_in[:, :], 0.0, None, ALU.is_gt))
            V.do(vec.tensor_tensor(LNT3, B3R.unsqueeze(1).broadcast_to((P, NT, D)), bc(st(2)), ALU.mult))
            V.do(vec.tensor_tensor(acc3, acc3, LNT3, ALU.add))
            V.do(vec.tensor_tensor(acc3, acc3, H3, ALU.add))
            V.do(vec.tensor_tensor(x3, x3, acc3, ALU.add))
            dve.sem_inc(s_final, 1)


_INS = ['x', 'src', 'dst', 'edge_attr_16', 'edge_type_8', 'edge_weight1', 'L1_gnn_weight1', 'L1_gnn_weight2', 'L1_gnn_bias1',
        'L1_gnn_bias2', 'L2_gnn_lap_coefs', 'L2_gnn_mf_weights', 'L3_gnn_W1', 'L3_gnn_b1', 'L3_gnn_W2', 'L3_gnn_b2',
        'L3_gnn_W3', 'L3_gnn_b3']


def kernel(**inputs):
    import numpy as _np
    import concourse.bacc as _bacc
    from concourse import mybir as _mybir
    from concourse.bass_utils import run_bass_kernel_spmd as _run

    nc = _bacc.Bacc("TRN2", target_bir_lowering=False, num_devices=1)
    arrays, args = {}, []
    for name in _INS:
        a = _np.ascontiguousarray(inputs[name])
        arrays[f"in_{name}_dram"] = a
        args.append(nc.dram_tensor(f"in_{name}_dram", a.shape, _mybir.dt.from_np(a.dtype), kind="ExternalInput").ap())
    args.append(nc.dram_tensor("out_0_dram", (N, D), F32, kind="ExternalOutput").ap())
    gnn(nc, *args)
    r = _run(nc, [arrays], core_ids=[0])
    return r.results[0]["out_0_dram"]
```

```python
from contextlib import ExitStack
import math

import concourse.bass as bass
from concourse import mybir

ALU = mybir.AluOpType
ACT = mybir.ActivationFunctionType
AX = mybir.AxisListType
F32 = mybir.dt.float32
BF16 = mybir.dt.bfloat16
F16 = mybir.dt.float16
I32 = mybir.dt.int32
U32 = mybir.dt.uint32

P = 128
N, D = 3125, 48
E = 100000
NT = -(-N // P)
NP = NT * P
NREM = N - (NT - 1) * P
RE = 1024
RP = -(-E // RE)
RREM = E - (RP - 1) * RE
HE = 256
NH = RP * RE // HE
NC = 2 * NH
NG = NH // 2
WIN = 24
QS = WIN + 2
NQ = NT + 1
HALFQ = NQ // 2 * WIN
LASTBASE = NP - WIN
ADJ = NT * NP
HP = P // 2
BLANK = 2 * NT
NW = BLANK + 1
REL = 8
HID = 128
EF = 16
K = 10
PART = 3 * D
TPB = 3
NB = -(-NT // TPB)
BIG = 16384.0


def jacobi():
    a = b = 1.0
    an, cn = [(a + b + 2.0) / 2.0], [0.0]
    for n in range(2, K + 1):
        nab = 2 * n + a + b
        an.append(nab * (nab - 1) * (nab - 2) / (2 * n * (nab - n) * (nab - 2)))
        cn.append(-(2 * (n + a - 1) * (n + b - 1) * nab) / (2 * n * (nab - n) * (nab - 2)))
    norm = []
    for i in range(K + 1):
        t1 = math.pow(2.0, a + b + 1) / (2 * i + a + b + 1)
        t2 = math.exp(math.lgamma(i + a + 1) - math.lgamma(i + a + b + 1))
        t3 = math.exp(math.lgamma(i + b + 1) - math.lgamma(i + 1))
        norm.append(math.sqrt(t1 * t2 * t3))
    return an, cn, norm


class Count:

    def __init__(self, eng, sem):
        self.eng, self.sem, self.n, self.base = eng, sem, 0, 0

    def did(self, instruction):
        self.n += 1
        instruction.then_inc(self.sem, 1)

    def all(self):
        self.eng.wait_ge(self.sem, self.base + self.n)

    def do(self, instruction):
        self.did(instruction)
        self.all()


def gnn(nc, x_d, src_d, dst_d, ea_d, et_d, ew_d, w1_d, w2_d, b1_d, b2_d, lap_d, mf_d,
        m1_d, mb1_d, m2_d, mb2_d, m3_d, mb3_d, out_d):
    ctx = ExitStack()
    with ctx:
        def sb(name, shape, dt):
            return ctx.enter_context(nc.sbuf_tensor(name, shape, dt))

        def sem(name):
            return ctx.enter_context(nc.semaphore(name))

        msg_table = nc.dram_tensor("msg_table", (NP * REL, D), F32, kind="Internal").ap()
        node_table = nc.dram_tensor("node_table", (NP, D), F32, kind="Internal").ap()
        rel_rows = nc.dram_tensor("rel_rows", (NC, P), BF16, kind="Internal").ap()

        adj = sb("adj", [P, ADJ], F16)
        scr = sb("scr", [P, 6700], F32)
        x = sb("x", [P, NT * D], F32)
        rel_b = sb("rel_b", [P, NC], F32)
        norm_c = sb("norm_c", [P, NC], F32)
        idx_msg = sb("idx_msg", [P, NC], U32)
        idx_src = sb("idx_src", [P, NC], U32)
        iota_code = sb("iota_code", [P, NQ * WIN], F16)
        iota_256 = sb("iota_256", [P, 256], F16)
        iota_p = sb("iota_p", [P, 2], F32)
        ident = sb("ident", [P, P], F32)
        identh = sb("identh", [P, P], F16)
        ones = sb("ones", [P, P], F32)
        onesh = sb("onesh", [P, 2], F16)
        base_row = sb("base_row", [1, 2 + NH], I32)
        tile_row = sb("tile_row", [1, NG], I32)
        passes = sb("passes", [1, 2], I32)
        stat = sb("stat", [P, 9 * NT], F32)
        dinv_in = sb("dinv_in", [P, NT], F32)
        cnt_in = sb("cnt_in", [P, NT], F32)
        rec = sb("rec", [P, 3 * K + 1], F32)
        small = sb("small", [P, 64], F32)
        smi = sb("smi", [P, 16], I32)
        psum = ctx.enter_context(nc.psum_tensor("psum", [P, 8, 512], F32))
        psum_h = psum[:, :, :].bitcast(F16)
        x3 = x[:, :].rearrange("p (q f) -> p q f", f=D)
        adj3 = adj[:, :].rearrange("p (q n) -> p q n", n=NP)

        adj_f = adj[:, :].bitcast(F32)
        ROW0 = ADJ // 2 - 8 * RE

        def row(k):
            return adj_f[0:P, ROW0 + k * RE:ROW0 + (k + 1) * RE]
        dst_i, src_i, typ_i = (row(k).bitcast(I32) for k in range(3))
        nrm_f, dst_f, t_a, t_b, t_c = (row(k) for k in range(3, 8))
        code_c = scr[:, 0:NC]
        rel_a = scr[:, NC:2 * NC]
        q_c = scr[:, 2 * NC:3 * NC]
        r_c = scr[:, 3 * NC:4 * NC]
        ROWS = [t_b, t_c, t_b, t_c, t_b, t_c, nrm_f]
        COLS = [rel_a, q_c, r_c, rel_b[:, :], idx_msg[:, :], idx_src[:, :], norm_c[:, :]]
        s_final = sem("s_final")

        s_fill = sem("s_fill")
        s_in = sem("s_in")
        s_x = sem("s_x")
        s_const = sem("s_const")
        s_id0 = sem("s_id0")
        s_zero = sem("s_zero")
        v_seq = sem("v_seq")
        s_rowready = sem("s_rowready")
        s_rowt = sem("s_rowt")
        s_rowout = sem("s_rowout")
        s_statready = sem("s_statready")
        s_statrow = sem("s_statrow")
        s_passes = sem("s_passes")
        s_code = sem("s_code")
        s_oh = sem("s_oh")
        s_built = sem("s_built")
        s_stage = sem("s_stage")
        s_add = sem("s_add")
        s_adj = sem("s_adj")
        s_tp = sem("s_tp")
        s_tx = sem("s_tx")
        s_ty = sem("s_ty")
        s_deg = sem("s_deg")
        s_degread = sem("s_degread")
        s_var = sem("s_var")
        s_root = sem("s_root")
        s_xp = sem("s_xp")
        s_prop = sem("s_prop")
        s_bank = sem("s_bank")
        s_out = sem("s_out")

        H1T = scr[0:96, 0:2048].rearrange("p (c n) -> p c n", c=4)
        HT = scr[0:D, 2048:3072].rearrange("p (s n) -> p s n", s=2)
        H2 = scr[:, 3072:3840].rearrange("p (s c) -> p s c", s=2)
        W1R = scr[0:D, 3840:4224]
        W2R = scr[0:96, 4224:4608].rearrange("p (c j) -> p c j", c=4)
        B1R = scr[0:96, 4608:4609]
        H = scr[:, 4616:5816].rearrange("p (q f) -> p q f", f=D)
        LNT = scr[:, 0:1200].rearrange("p (q f) -> p q f", f=D)
        GM = scr[:, 0:768].rearrange("p (s c) -> p s c", s=4)
        IDX = scr[:, 768:784].bitcast(U32).rearrange("p (s c) -> p s c", s=4)
        OH1 = scr[:, 784:1296].bitcast(BF16).rearrange("p (s t c) -> p s t c", s=2, t=4)
        WM = scr[:, 1296:1488].rearrange("p (t f) -> p t f", t=4)
        GP = scr[:, 1488:2064].bitcast(BF16).rearrange("p (s t j f) -> p s t j f", s=2, t=4, j=3)
        ACC = scr[:, 2064:2064 + NW * D]
        B2R = scr[:, 4512:4512 + D]
        REL1 = scr[:, 4560:4560 + NC]
        TILE1 = scr[0:1, 5344:5344 + NG].bitcast(I32)
        WMR = scr[:, 5540:5732].rearrange("p (t f) -> p t f", t=4)
        JOIN = scr[:, 0:1200].rearrange("p (q f) -> p q f", f=D)
        HCH = [(c * 4, min(NT, c * 4 + 4)) for c in range(-(-NT // 4))]

        WCH = [(c * 4, min(NW, c * 4 + 4)) for c in range(-(-NW // 4))]

        spot = [0]

        def place(n):
            spot[0] += n
            return adj_f[:, spot[0] - n:spot[0]]
        PD = place(NW * 3 * HID // 2).bitcast(BF16)
        G3 = place(4 * 4 * 64).rearrange("p (s t c) -> p s t c", s=4, t=4)
        GT = place(2 * 512).rearrange("p (s c) -> p s c", s=2)
        REL_ROW = place(4 * 256).bitcast(BF16).rearrange("p (s c) -> p s c", s=4)
        OHT = place(512).bitcast(BF16).rearrange("p (s c) -> p s c", s=2)
        OHF = place(512).bitcast(BF16).rearrange("p (s t c) -> p s t c", s=2, t=4)
        R1 = place(2 * 512).rearrange("p (s c) -> p s c", s=2)
        R2 = place(2 * 512).rearrange("p (s c) -> p s c", s=2)
        MS = place(2 * 6 * D).bitcast(BF16).rearrange("p (s t j f) -> p s t j f", s=2, t=4, j=3)
        MSR = place(4 * D).rearrange("p (t f) -> p t f", t=4)
        SUM3 = place(D)
        ACC3 = place(NW * D)
        REL3 = place(NC)
        CLAMP = place(NC)
        RELT = place(7 * P // 2).bitcast(BF16).rearrange("p (j c) -> p j c", j=7)
        H3 = place(NT * D).rearrange("p (q f) -> p q f", f=D)
        LNT3 = place(NT * D).rearrange("p (q f) -> p q f", f=D)
        HT3 = place(NP + 2 * P)
        JOIN3 = HT3[:, 0:NT * D].rearrange("p (q f) -> p q f", f=D)
        PDR = place(1024).rearrange("p (s c) -> p s c", s=2)
        W1AC, W1B, W2M, W3M = place(HID), place(HID), place(HID), place(D)
        BM = place(2)
        B3R = place(D)
        TILE3 = place(2 + NG)[0:1, :].bitcast(I32)
        IDX3 = place(16).bitcast(U32).rearrange("p (s c) -> p s c", s=4)

        s_w = sem("s_w")
        s_wz = sem("s_wz")
        s_h = sem("s_h")
        s_ht = sem("s_ht")
        s_htc = sem("s_htc")
        s_h1 = sem("s_h1")
        s_h1r = sem("s_h1r")
        s_h2 = sem("s_h2")
        s_h2c = sem("s_h2c")
        s_tab = [sem("s_tab0"), sem("s_tab1")]
        s_loop1 = sem("s_loop1")
        s_idx = sem("s_idx")
        s_gath = [sem(f"s_gath{k}") for k in range(4)]
        s_woh = sem("s_woh")
        s_seg = sem("s_seg")
        s_acc = sem("s_acc")
        s_shift = sem("s_shift")
        s_coef = sem("s_coef")
        s_lap = sem("s_lap")
        s_lapin = sem("s_lapin")
        s_coefb = sem("s_coefb")
        v_l2 = sem("v_l2")
        s_w3in = sem("s_w3in")
        s_l2done = sem("s_l2done")
        s_node = sem("s_node")
        s_ht3 = sem("s_ht3")
        s_htc3 = sem("s_htc3")
        s_pd = sem("s_pd")
        s_pdc = sem("s_pdc")
        s_clamp = sem("s_clamp")
        s_relt = sem("s_relt")
        s_reltc = sem("s_reltc")
        s_relst = sem("s_relst")
        s_idx3 = sem("s_idx3")
        s_in3 = [sem(f"s_in3{k}") for k in range(4)]
        s_ef = [sem(f"s_ef{k}") for k in range(4)]
        s_rel3 = [sem(f"s_rel3{k}") for k in range(4)]
        s_t3 = sem("s_t3")
        s_gt = sem("s_gt")
        s_oht = sem("s_oht")
        s_z1 = sem("s_z1")
        s_r1 = sem("s_r1")
        s_z2 = sem("s_z2")
        s_r2 = sem("s_r2")
        s_w3 = sem("s_w3")
        s_msg = sem("s_msg")
        s_ohf = sem("s_ohf")
        s_seg3 = sem("s_seg3")
        s_acc3 = sem("s_acc3")
        s_shift3 = sem("s_shift3")
        v_msg = sem("v_msg")
        v_mlp = sem("v_mlp")
        s_pdhi = sem("s_pdhi")
        s_pdr = sem("s_pdr")
        s_mark = sem("s_mark")
        AN, CN, NORM = jacobi()

        block = ctx.enter_context(nc.Block())

        CH = [(q, m, min(8, NT - m)) for q in range(NT) for m in range(q, NT, 8)]
        LOWER = []
        for q, m, c in CH:
            LOWER.append((LOWER[-1] if LOWER else 0) + (m + c - 1 > q))
        adj_blk = adj[:, :].rearrange("p (q m r) -> p q m r", m=NT, r=P)
        NCONST = 7

        XP = [scr[:, k * 1800:(k + 1) * 1800].bitcast(BF16).rearrange("p (q j f) -> p q j f", j=3, f=D) for k in range(2)]
        PA = scr[:, 3600:4800].rearrange("p (q f) -> p q f", f=D)
        PB = scr[:, 4800:6000].rearrange("p (q f) -> p q f", f=D)
        TY = scr[:, 6000:6000 + TPB * D].rearrange("p (q f) -> p q f", f=D)
        TR = scr[:, 6144:6144 + TPB * D].rearrange("p (q f) -> p q f", f=D)
        BANKS = [(b * TPB, min(NT, (b + 1) * TPB)) for b in range(NB)]
        OHQ = scr[:, 4 * NC:4 * NC + 4 * NQ * WIN // 2].bitcast(F16).rearrange("p (s t c) -> p s t c", s=2, t=2)
        o = 4 * NC + 4 * NQ * WIN // 2
        OHR = scr[:, o:o + 256].bitcast(F16).rearrange("p (s t c) -> p s t c", s=2, t=2)
        o += 256
        STG = scr[:, o:o + NQ * WIN].bitcast(F16).rearrange("p (s c) -> p s c", s=2)

        def st(k, n=1):
            return stat[:, k * NT:(k + n) * NT]

        def bc(a, n=D):
            return a.unsqueeze(2).broadcast_to((a.shape[0], a.shape[1], n))

        @block.sync
        def _(sp):
            sp.wait_ge(s_fill, 4)
            for dst, src in ((dst_i, dst_d), (src_i, src_d), (typ_i, et_d)):
                sp.dma_start(dst[0:RP - 1, :], src[0:(RP - 1) * RE].rearrange("(p c) -> p c", c=RE)).then_inc(s_in, 16)
                sp.dma_start(dst[RP - 1:RP, 0:RREM], src[(RP - 1) * RE:E].rearrange("(p c) -> p c", c=RREM)).then_inc(s_in, 16)
            sp.dma_start(nrm_f[0:RP - 1, :], ew_d[0:(RP - 1) * RE, :].rearrange("(p c) o -> p (c o)", c=RE)).then_inc(s_in, 16)
            sp.dma_start(nrm_f[RP - 1:RP, 0:RREM], ew_d[(RP - 1) * RE:E, :].rearrange("(p c) o -> p (c o)", c=RREM)).then_inc(s_in, 16)
            sp.wait_ge(s_fill, 5)
            sp.dma_start(x3[:, 0:NT - 1, :], x_d[0:(NT - 1) * P, :].rearrange("(q r) f -> r q f", r=P)).then_inc(s_x, 16)
            sp.dma_start(x3[0:NREM, NT - 1, :], x_d[(NT - 1) * P:N, :]).then_inc(s_x, 16)
            sp.wait_ge(s_wz, 1)
            sp.dma_start(W1R.rearrange("p (r j) -> p r j", r=REL), w1_d.rearrange("r i j -> i r j")).then_inc(s_w, 16)
            w2_v = w2_d.rearrange("(c s) i j -> s i c j", s=2)
            for k in range(2):
                sp.dma_start(W2R[k * D:(k + 1) * D, :, k * D:(k + 1) * D], w2_v[k]).then_inc(s_w, 16)
                sp.dma_start(B1R[k * D:(k + 1) * D, :], b1_d.rearrange("(p o) -> p o", o=1)).then_inc(s_w, 16)
            table = msg_table.rearrange("(q r e) f -> q r (e f)", r=P, e=REL)
            for q in range(NT):
                sp.wait_ge(s_h2c, q + 1)
                sp.dma_start(table[q], H2[:, q % 2, :]).then_inc(s_tab[q % 2], 16)
            sp.wait_ge(s_loop1, 1)
            sp.dma_start(B2R, b2_d.partition_broadcast(P)).then_inc(s_w, 16)
            sp.dma_start(small[0:1, 0:K + 1], lap_d.rearrange("(o k) -> o k", o=1)).then_inc(s_lapin, 16)
            sp.dma_start(small[0:1, 16:16 + K + 1], mf_d.rearrange("o k e -> o (k e)")).then_inc(s_lapin, 16)
            sp.wait_ge(s_l2done, 1)
            for dst, src in ((W1AC[0:D, :], m1_d[0:D, :]), (W1AC[D:D + EF, :], m1_d[2 * D:2 * D + EF, :]), (W1B[0:D, :], m1_d[D:2 * D, :]),
                             (W2M, m2_d), (W3M, m3_d), (BM[:, 0:1], mb1_d.rearrange("(p o) -> p o", o=1)),
                             (BM[:, 1:2], mb2_d.rearrange("(p o) -> p o", o=1)), (B3R, mb3_d.partition_broadcast(P))):
                sp.dma_start(dst, src).then_inc(s_w3in, 16)
            sp.wait_ge(s_h, 2)
            sp.dma_start(node_table.rearrange("(q r) f -> r q f", r=P), H3).then_inc(s_node, 16)
            most = sp.value_load(passes[0:1, 1:2], min_val=0, max_val=BLANK)
            with sp.Fori(0, most // 2 + 1) as p:
                sp.wait_ge(s_reltc, p + 1)
                sp.wait_ge(s_oht, p * NG + 4)
                sp.dma_start(rel_rows.rearrange("(j c) e -> c j e", j=7), RELT[0:NC // 7, :, :]).then_inc(s_relst, 16)
                sp.wait_ge(s_relst, p * 16 + 16)
                sp.sem_inc(s_mark, 1)

                def load(i, n):
                    for k in range(4):
                        sp.wait_ge(s_oht, n + k + 1)
                        codes = rel_rows[bass.ds((i * 4 + k) * 4, 4), :] if not isinstance(i, int) else rel_rows[(i * 4 + k) * 4:(i * 4 + k) * 4 + 4, :]
                        sp.dma_start(REL_ROW[:, k, :], codes.rearrange("a b -> (a b)").partition_broadcast(P)).then_inc(s_rel3[k], 16)
                        sp.wait_ge(s_t3, n + k + 1)
                        for h in range(2):
                            if isinstance(i, int):
                                e0 = ((i * 4 + k) * 2 + h) * HE
                                m = min(HE, E - e0)
                                if m > 0:
                                    sp.dma_start(G3[0:m // 2, k, 2 * h:2 * h + 2, D:D + EF], ea_d[e0:e0 + m, :].rearrange("(p t) f -> p t f", t=2))\
                                      .then_inc(s_ef[k], 16 if h or e0 + HE < E else 32)
                            else:
                                sp.dma_start(G3[:, k, 2 * h:2 * h + 2, D:D + EF],
                                             ea_d[bass.ds(i * (8 * HE) + (2 * k + h) * HE, HE), :].rearrange("(p t) f -> p t f", t=2)).then_inc(s_ef[k], 16)
                with sp.Fori(0, NG // 4 - 1) as i:
                    load(i, sp.snap(p * NG + i * 4))
                load(NG // 4 - 1, sp.snap(p * NG + (NG - 4)))
            sp.wait_ge(s_final, 1)
            sp.dma_start(out_d[0:(NT - 1) * P, :].rearrange("(q r) f -> r q f", r=P), x3[:, 0:NT - 1, :]).then_inc(s_out, 16)
            sp.dma_start(out_d[(NT - 1) * P:N, :], x3[0:NREM, NT - 1, :]).then_inc(s_out, 16)
            sp.wait_ge(s_out, 32)

        @block.gpsimd
        def _(pool):
            for dst, fill in ((dst_i, -1), (src_i, 0), (typ_i, 0)):
                nc.gpsimd.memset(dst, fill).then_inc(s_fill, 1)
            nc.gpsimd.memset(nrm_f, 0.0).then_inc(s_fill, 1)
            nc.gpsimd.memset(x[:, :], 0.0).then_inc(s_fill, 1)
            nc.gpsimd.memset(ident[:, :], 0.0).then_inc(s_id0, 1)
            nc.gpsimd.memset(identh[:, :], 0.0).then_inc(s_id0, 1)
            nc.gpsimd.memset(ones[:, :], 1.0).then_inc(s_const, 1)
            nc.gpsimd.memset(onesh[:, :], 1.0).then_inc(s_const, 1)
            pool.wait_ge(s_id0, 2)
            for m in (ident, identh):
                nc.gpsimd.affine_select(out=m[:, :], in_=m[:, :], compare_op=ALU.not_equal, fill=1.0, base=0,
                                        pattern=[[-1, P]], channel_multiplier=1).then_inc(s_const, 1)
            nc.gpsimd.iota(iota_code[:, :], pattern=[[QS, NQ], [1, WIN]], base=0, channel_multiplier=0,
                           allow_small_or_imprecise_dtypes=True).then_inc(s_const, 1)
            nc.gpsimd.iota(iota_256[:, :], pattern=[[1, 256]], base=0, channel_multiplier=0,
                           allow_small_or_imprecise_dtypes=True).then_inc(s_const, 1)
            nc.gpsimd.iota(iota_p[:, :], pattern=[[P, 2]], base=0, channel_multiplier=1,
                           allow_small_or_imprecise_dtypes=True).then_inc(s_const, 1)
            nc.gpsimd.memset(adj_f[:, 0:ROW0], 0.0).then_inc(s_zero, 1)
            pool.wait_ge(s_rowready, 7)
            pool.wait_ge(s_rowt, 7)
            nc.gpsimd.memset(adj_f[:, ROW0:ADJ // 2], 0.0).then_inc(s_zero, 1)
            for n in range(K):
                nc.gpsimd.memset(rec[:, n:n + 1], 2.0 * AN[n]).then_inc(s_const, 1)
                nc.gpsimd.memset(rec[:, K + n:K + n + 1], CN[n]).then_inc(s_const, 1)
            for n in range(K + 1):
                nc.gpsimd.memset(rec[0:1, 2 * K + n:2 * K + n + 1], 1.0 / NORM[n]).then_inc(s_const, 1)
            pool.wait_ge(s_tab[0], 16 * ((NT + 1) // 2))
            pool.wait_ge(s_tab[1], 16 * (NT // 2))
            pool.wait_ge(s_loop1, 1)
            most = pool.value_load(passes[0:1, 1:2], min_val=0, max_val=BLANK)
            with pool.Fori(0, most // 2 + 1) as p:
                with pool.Fori(0, NG // 4) as i:
                    g = pool.snap(p * NG + i * 4)
                    for k in range(4):
                        pool.wait_ge(s_idx, g + k + 1)
                        pool.wait_ge(s_seg, g + k + 1)
                        pool.sem_inc(s_mark, 1)
                        for t in range(4):
                            pool.indirect_dma_start(out=GM[:, k, t * D:(t + 1) * D], out_offset=None, in_=msg_table,
                                                    in_offset=bass.IndirectOffsetOnAxis(ap=IDX[:, k, t:t + 1], axis=0)).then_inc(s_gath[k], 16)
            pool.wait_ge(s_node, 16)
            with pool.Fori(0, most // 2 + 1) as p:
                with pool.Fori(0, NG // 4) as i:
                    g = pool.snap(p * NG + i * 4)
                    for k in range(4):
                        pool.wait_ge(s_idx3, g + k + 1)
                        pool.wait_ge(s_t3, g + k + 1)
                        pool.sem_inc(s_mark, 1)
                        for t in range(4):
                            pool.indirect_dma_start(out=G3[:, k, t, 0:D], out_offset=None, in_=node_table,
                                                    in_offset=bass.IndirectOffsetOnAxis(ap=IDX3[:, k, t:t + 1], axis=0)).then_inc(s_in3[k], 16)

        @block.tensor
        def _(pe):
            pe.wait_ge(s_const, NCONST)
            for a, arr in enumerate(ROWS):
                pe.wait_ge(s_rowready, a + 1)
                if a >= 2:
                    pe.wait_ge(s_rowout, a - 1)
                for j in range(8):
                    b, t = j // 2, j % 2
                    bank = 2 * (a % 2) + j // 4
                    last = nc.tensor.transpose(psum[:, bank, (j % 4) * RP:(j % 4 + 1) * RP],
                                               arr[0:RP, b * HE + t:(b + 1) * HE:2], ident[0:RP, 0:RP])
                last.then_inc(s_rowt, 1)
            pe.wait_ge(s_statready, 1)
            for k in range(2):
                nc.tensor.matmul(psum[0:1, 4, k * P:(k + 1) * P], lhsT=small[:, 22 + k:23 + k], rhs=ident[:, :], start=True, stop=True)
                nc.tensor.matmul(psum[0:1, 6, k * RP:(k + 1) * RP], lhsT=small[0:RP, 12 + k:13 + k], rhs=ident[0:RP, 0:RP], start=True, stop=True)
            for b in range(4):
                last = nc.tensor.matmul(psum[0:1, 5, b * RP:(b + 1) * RP], lhsT=small[0:RP, b:b + 1], rhs=ident[0:RP, 0:RP], start=True, stop=True)
            last.then_inc(s_statrow, 1)
            pe.wait_ge(s_passes, 1)
            most = pe.value_load(passes[0:1, 0:1], min_val=0, max_val=N)
            pe.sem_inc(s_built, 2)
            with pe.Fori(0, most // WIN + 1) as p:
                with pe.Fori(0, NH // 4) as i:
                    g = pe.snap(p * NH + i * 4)
                    e = pe.snap(p * (NH + 2) + i * 4)
                    for k in range(4):
                        pe.wait_ge(s_oh, g + k + 2)
                        pe.wait_ge(s_stage, e + k + 1)
                        for t in range(2):
                            for half in range(2):
                                last = nc.tensor.matmul(psum[:, 4 + 2 * (k % 2) + half, 0:HALFQ], lhsT=OHR[:, k % 2, t, :],
                                                        rhs=OHQ[:, k % 2, t, half * HALFQ:(half + 1) * HALFQ], start=(t == 0), stop=(t == 1))
                        last.then_inc(s_built, 1)

            def transpose_adj(turn):
                for n, (q, m0, c) in enumerate(CH):
                    if n >= 4:
                        pe.wait_ge(s_tx, turn * len(CH) + n - 3)
                        pe.wait_ge(s_ty, turn * LOWER[-1] + LOWER[n - 4])
                    elif turn:
                        pe.wait_ge(s_tx, turn * len(CH))
                        pe.wait_ge(s_ty, turn * LOWER[-1])
                    bank = 2 * (n % 4)
                    for j in range(c):
                        last = nc.tensor.transpose(psum_h[:, bank, j * P:(j + 1) * P], adj_blk[:, q, m0 + j, :], identh[:, :])
                    for j in range(c):
                        if m0 + j > q:
                            last = nc.tensor.transpose(psum_h[:, bank + 1, j * P:(j + 1) * P], adj_blk[:, m0 + j, q, :], identh[:, :])
                    last.then_inc(s_tp, 1)

            def degrees(turn):
                pe.wait_ge(s_tx, (turn + 1) * len(CH))
                pe.wait_ge(s_ty, (turn + 1) * LOWER[-1])
                for m in range(NT):
                    for q in range(NT):
                        last = nc.tensor.matmul(psum[:, 0, m:m + 1], lhsT=adj_blk[:, q, m, :], rhs=onesh[:, 0:1], start=(q == 0), stop=(q == NT - 1))
                last.then_inc(s_deg, 1)

            def propagate(parts, banks_before):
                for b, (m0, m1) in enumerate(BANKS):
                    if b >= 8:
                        pe.wait_ge(s_bank, banks_before + b - 7)
                    for m in range(m0, m1):
                        for q in range(NT):
                            last = nc.tensor.matmul(psum[:, b % 8, (m - m0) * PART:(m - m0 + 1) * PART], lhsT=adj_blk[:, q, m, :],
                                                    rhs=parts[:, q, :, :], start=(q == 0), stop=(q == NT - 1))
                    last.then_inc(s_prop, 1)

            pe.wait_ge(s_adj, 1)
            transpose_adj(0)
            degrees(0)
            pe.wait_ge(s_degread, 1)
            for n in range(2):
                pe.wait_ge(s_xp, n + 1)
                propagate(XP[n], n * NB)
            pe.wait_ge(s_bank, 2 * NB)
            transpose_adj(1)
            degrees(1)
            def features(c, src, ready, ident_):
                m0, m1 = HCH[c]
                for j in range(m1 - m0):
                    last = nc.tensor.transpose(psum[0:D, 1, j * P:(j + 1) * P], src[:, m0 + j, :], ident_[:, :])
                last.then_inc(ready, 1)

            pe.wait_ge(s_w, 16 * 5)
            pe.wait_ge(s_h, 1)
            features(0, H, s_ht, ident)
            for c, (m0, m1) in enumerate(HCH):
                w = (m1 - m0) * P
                pe.wait_ge(s_htc, c + 1)
                for r in range(4):
                    nc.tensor.matmul(psum[0:96, 2 + r, 0:w], lhsT=W1R[:, r * 96:(r + 1) * 96], rhs=HT[:, c % 2, 0:w], start=True, stop=True).then_inc(s_h1, 1)
                if c + 1 < len(HCH):
                    features(c + 1, H, s_ht, ident)
                pe.wait_ge(s_h1r, 4 * c + 4)
                for j in range(m1 - m0):
                    q = m0 + j
                    if q >= 2:
                        pe.wait_ge(s_h2c, q - 1)
                    for r in range(4):
                        last = nc.tensor.matmul(psum[:, 6 + q % 2, r * 96:(r + 1) * 96], lhsT=H1T[:, r, j * P:(j + 1) * P], rhs=W2R[:, r, :], start=True, stop=True)
                    last.then_inc(s_h2, 1)
            pe.sem_inc(s_seg, 4)
            most = pe.value_load(passes[0:1, 1:2], min_val=0, max_val=BLANK)
            with pe.Fori(0, most // 2 + 1) as p:
                with pe.Fori(0, NG // 4) as i:
                    g = pe.snap(p * NG + i * 4)
                    for k in range(4):
                        pe.wait_ge(s_woh, g + k + 1)
                        pe.wait_ge(s_acc, g + k + 1)
                        for t in range(4):
                            for j in range(3):
                                last = nc.tensor.matmul(psum[:, 4 + k % 2, 0:D], lhsT=OH1[:, k % 2, t, :],
                                                        rhs=GP[:, k % 2, t, j, :], start=(t == 0 and j == 0), stop=(t == 3 and j == 2))
                        last.then_inc(s_seg, 1)
            pe.wait_ge(s_coef, 1)
            nc.tensor.matmul(psum[:, 7, 0:K + 1], lhsT=ones[0:1, :], rhs=small[0:1, 32:32 + K + 1], start=True, stop=True).then_inc(s_coefb, 1)
            with pe.Fori(0, K // 2) as i:
                for u in range(2):
                    pe.wait_ge(s_xp, i * 2 + (3 + u))
                    propagate(XP[u], pe.snap(i * (2 * NB) + (2 + u) * NB))
            pe.wait_ge(s_w3in, 16 * 8)
            pe.wait_ge(s_h, 2)
            features(0, H3, s_ht3, ident)
            for c in range(1, len(HCH)):
                pe.wait_ge(s_htc3, c)
                features(c, H3, s_ht3, ident)
            pe.wait_ge(s_htc3, len(HCH))
            for c, (w0, w1) in enumerate(WCH):
                if c >= 4:
                    pe.wait_ge(s_pdc, c - 3)
                for j in range(w1 - w0):
                    last = nc.tensor.matmul(psum[:, 2 + c % 4, j * HID:(j + 1) * HID], lhsT=HT3[0:D, (w0 + j) * HP:(w0 + j) * HP + P], rhs=W1B[0:D, :], start=True, stop=True)
                last.then_inc(s_pd, 1)
            pe.wait_ge(s_pdc, len(WCH))
            tile = [pe.alloc_register(f"pe_tile{k}") for k in range(4)]
            pe.sem_inc(s_t3, 4)
            pe.sem_inc(s_z1, 2)
            pe.sem_inc(s_z2, 2)
            pe.sem_inc(s_w3, 2)
            pe.sem_inc(s_seg3, 2)

            def inputs_t(k, n, used):
                pe.wait_ge(s_ef[k], used)
                pe.wait_ge(s_in3[k], used * 2)
                pe.wait_ge(s_gt, n + 1)
                pe.sem_inc(s_mark, 1)
                for t in range(4):
                    last = nc.tensor.transpose(psum[0:64, 4, t * P:(t + 1) * P], G3[:, k, t, :], ident[:, :])
                last.then_inc(s_t3, 1)

            def layer1(k, n, window):
                pe.wait_ge(s_gt, n + 2)
                pe.wait_ge(s_r1, n + 1)
                nc.tensor.matmul(psum[:, k % 2, :], lhsT=W1AC[0:64, :], rhs=GT[0:64, k % 2, :], start=True, stop=False)
                pe.wait_ge(s_oht, n + 5)
                for c in range(3):
                    last = nc.tensor.matmul(psum[:, k % 2, :], lhsT=PD[:, bass.ds(window * (3 * HID) + c * HID, HID)],
                                            rhs=OHT[:, k % 2, :], start=False, stop=(c == 2))
                last.then_inc(s_z1, 1)

            def layer2(k, n):
                pe.wait_ge(s_r1, n + 3)
                pe.wait_ge(s_r2, n + 1)
                nc.tensor.matmul(psum[:, 2 + k % 2, :], lhsT=W2M, rhs=R1[:, k % 2, :], start=True, stop=True).then_inc(s_z2, 1)

            def layer3(k, n):
                pe.wait_ge(s_r2, n + 3)
                pe.wait_ge(s_msg, n + 1)
                for t in range(4):
                    last = nc.tensor.matmul(psum[:, 5, t * D:(t + 1) * D], lhsT=R2[:, k % 2, t * P:(t + 1) * P], rhs=W3M, start=True, stop=True)
                last.then_inc(s_w3, 1)

            def sums(k, n):
                pe.wait_ge(s_ohf, n + 1)
                pe.wait_ge(s_msg, n + 2)
                pe.wait_ge(s_acc3, n + 1)
                for t in range(4):
                    last = nc.tensor.matmul(psum[:, 6 + k % 2, 0:PART], lhsT=OHF[:, k % 2, t, :],
                                            rhs=MS[:, k % 2, t, :, :], start=(t == 0), stop=(t == 3))
                last.then_inc(s_seg3, 1)

            def mlp(i, n, used, first=False, last=False):
                at = slice(2 + i * 4, 6 + i * 4) if isinstance(i, int) else bass.ds(i * 4 + 2, 4)
                pe.load(tile, TILE3[0:1, at])
                for k in range(4):
                    layer1(k, n + k, pe.snap(tile[k], min_val=0, max_val=BLANK))
                    if not (last and k == 3):
                        inputs_t((k + 1) % 4, n + (k + 1), used + (32 if k < 3 else 64))
                    if not (first and k == 0):
                        layer3(k - 1, n + (k - 1))
                    if not (first and k < 2):
                        sums(k - 2, n + (k - 2))
                    layer2(k, n + k)

            with pe.Fori(0, most // 2 + 1) as p:
                pe.wait_ge(s_shift3, p * 3 + 2)
                pe.wait_ge(s_clamp, p + 1)
                for j in range(7):
                    last = nc.tensor.transpose(psum[0:NC // 7, 2 * (j // 4), (j % 4) * P:(j % 4 + 1) * P], CLAMP[:, j * (NC // 7):(j + 1) * (NC // 7)], ident[:, :])
                last.then_inc(s_relt, 1)
                pe.wait_ge(s_reltc, p + 1)
                inputs_t(0, pe.snap(p * NG), pe.snap(p * (32 * NG // 4) + 32))
                mlp(0, pe.snap(p * NG), pe.snap(p * (32 * NG // 4)), first=True)
                with pe.Fori(1, NG // 4 - 1) as i:
                    mlp(i, pe.snap(p * NG + i * 4), pe.snap(p * (32 * NG // 4) + i * 32))
                mlp(NG // 4 - 1, pe.snap(p * NG + (NG - 4)), pe.snap(p * (32 * NG // 4) + 32 * (NG // 4 - 1)), last=True)
                layer3(3, pe.snap(p * NG + (NG - 1)))
                sums(2, pe.snap(p * NG + (NG - 2)))
                sums(3, pe.snap(p * NG + (NG - 1)))

        @block.scalar
        def _(act):
            for a, dest in enumerate(COLS):
                act.wait_ge(s_rowt, a + 1)
                for hf in range(2):
                    last = nc.scalar.activation(dest.rearrange("p (c j) -> p j c", j=8)[:, 4 * hf:4 * hf + 4, :],
                                                psum[:, 2 * (a % 2) + hf, 0:4 * RP].rearrange("p (j c) -> p j c", j=4), ACT.Copy)
                last.then_inc(s_rowout, 1)
            act.wait_ge(s_passes, 1)
            most = act.value_load(passes[0:1, 0:1], min_val=0, max_val=N)
            with act.Fori(0, most // WIN + 1) as p:
                with act.Fori(0, NH // 4) as i:
                    g = act.snap(p * NH + i * 4)
                    e = act.snap(p * (NH + 2) + i * 4)
                    for k in range(4):
                        act.wait_ge(s_built, g + k + 3)
                        act.wait_ge(s_add, e + k + 2)
                        nc.scalar.activation(STG[:, k % 2, :].rearrange("p (h c) -> p h c", h=2),
                                             psum[:, 4 + 2 * (k % 2):6 + 2 * (k % 2), 0:HALFQ], ACT.Copy, scale=0.5).then_inc(s_stage, 1)

            def transpose_adj(turn):
                for n, (q, m0, c) in enumerate(CH):
                    lo = max(m0, q + 1)
                    if m0 + c > lo:
                        act.wait_ge(s_tp, turn * len(CH) + n + 1)
                        nc.scalar.activation(adj_blk[:, q, lo:m0 + c, :],
                                             psum_h[:, 2 * (n % 4) + 1, (lo - m0) * P:c * P].rearrange("p (j r) -> p j r", r=P),
                                             ACT.Copy).then_inc(s_ty, 1)

            def root(n):
                act.wait_ge(s_var, n + 1)
                nc.scalar.activation(st(4), st(3), ACT.Sqrt).then_inc(s_root, 1)

            transpose_adj(0)
            root(0)
            root(1)
            transpose_adj(1)
            root(2)
            act.wait_ge(s_w, 16 * 5)
            for c, (m0, m1) in enumerate(HCH):
                w = (m1 - m0) * P
                if c:
                    act.wait_ge(s_h2, m0)
                for r in range(4):
                    act.wait_ge(s_h1, 4 * c + r + 1)
                    nc.scalar.activation(H1T[:, r, 0:w], psum[0:96, 2 + r, 0:w], ACT.Relu, bias=B1R).then_inc(s_h1r, 1)
            root(3)
            act.wait_ge(s_loop1, 1)
            most = act.value_load(passes[0:1, 1:2], min_val=0, max_val=BLANK)
            with act.Fori(0, most // 2 + 1) as p:
                with act.Fori(0, NG // 4) as i:
                    g = act.snap(p * NG + i * 4)
                    for k in range(4):
                        act.wait_ge(s_seg, g + k + 1)
                        nc.scalar.copy(IDX[:, k, :], idx_msg[:, bass.ds(i * 16 + 4 * k, 4)]).then_inc(s_idx, 1)
            act.wait_ge(s_lapin, 32)
            nc.scalar.activation(small[0:1, 0:K + 1], small[0:1, 0:K + 1], ACT.Tanh).then_inc(s_lap, 1)
            root(4)
            root(5)
            for c, (w0, w1) in enumerate(WCH):
                act.wait_ge(s_pd, c + 1)
                X = PD[:, w0 * 3 * HID:w1 * 3 * HID].rearrange("p (q j f) -> p q j f", j=3, f=HID)
                nc.scalar.activation(X[:, :, 0, :], psum[:, 2 + c % 4, 0:(w1 - w0) * HID].rearrange("p (q f) -> p q f", f=HID), ACT.Copy).then_inc(s_pdhi, 1)
                act.wait_ge(s_pdr, c + 1)
                nc.scalar.activation(X[:, :, 1, :], PDR[:, c % 2, 0:(w1 - w0) * HID].rearrange("p (q f) -> p q f", f=HID), ACT.Copy).then_inc(s_pdhi, 1)
            act.sem_inc(s_gt, 1)
            act.sem_inc(s_r1, 2)
            act.sem_inc(s_r2, 2)
            act.wait_ge(s_w3in, 16 * 8)

            def stage(g, k, n):
                act.wait_ge(s_t3, n + 1)
                nc.scalar.copy(IDX3[:, k, :], idx_src[:, g]).then_inc(s_idx3, 1)

            def inputs_out(k, n):
                act.wait_ge(s_t3, n + 5)
                act.wait_ge(s_z1, n + 1)
                nc.scalar.activation(GT[0:64, k % 2, :], psum[0:64, 4, :], ACT.Copy).then_inc(s_gt, 1)

            def mlp(i, n, last=False):
                for k in range(4):
                    act.wait_ge(s_z1, n + (k + 3))
                    act.wait_ge(s_z2, n + (k + 1))
                    nc.scalar.activation(R1[:, k % 2, :], psum[:, k % 2, :], ACT.Relu, bias=BM[:, 0:1]).then_inc(s_r1, 1)
                    if not (last and k == 3):
                        inputs_out(k + 1, n + (k + 1))
                    if not last:
                        stage(bass.ds(i * 16 + (4 * k + 16), 4), k, n + (k + 4))
                    act.wait_ge(s_z2, n + (k + 3))
                    act.wait_ge(s_w3, n + (k + 1))
                    nc.scalar.activation(R2[:, k % 2, :], psum[:, 2 + k % 2, :], ACT.Relu, bias=BM[:, 1:2]).then_inc(s_r2, 1)

            with act.Fori(0, most // 2 + 1) as p:
                act.wait_ge(s_relt, p + 2)
                for j in range(2):
                    w = (4, 3)[j]
                    last = nc.scalar.activation(RELT[0:NC // 7, 4 * j:4 * j + w, :], psum[0:NC // 7, 2 * j, 0:w * P].rearrange("p (j c) -> p j c", j=w), ACT.Copy)
                last.then_inc(s_reltc, 1)
                for k in range(4):
                    stage(slice(4 * k, 4 * k + 4), k, act.snap(p * NG + k))
                inputs_out(0, act.snap(p * NG))
                with act.Fori(0, NG // 4 - 1) as i:
                    mlp(i, act.snap(p * NG + i * 4))
                mlp(NG // 4 - 1, act.snap(p * NG + (NG - 4)), last=True)

        @block.vector
        def _(dve):
            V = Count(dve, v_seq)
            vec = nc.vector
            dve.wait_ge(s_in, 16 * 8)
            dve.wait_ge(s_const, NCONST)
            t_ai, t_bi = t_a.bitcast(I32), t_b.bitcast(I32)
            v4 = lambda a: a.rearrange("p (b c) -> p b c", b=4)
            v2 = lambda a: a.rearrange("p (b c) -> p b c", b=2)
            V.do(vec.tensor_copy(dst_f, dst_i))
            V.do(vec.tensor_scalar(t_a, dst_f, 0.0, BIG, ALU.is_lt, ALU.mult))
            V.do(vec.tensor_tensor(t_a, t_a, dst_f, ALU.add))
            V.did(vec.tensor_reduce(small[:, 4:8], v4(dst_f), AX.X, ALU.max))
            V.do(vec.tensor_reduce(small[:, 24:28], v4(t_a), AX.X, ALU.min))
            V.do(vec.tensor_scalar(small[:, 0:4], small[:, 24:28], float(N - 1), None, ALU.min))
            V.did(vec.tensor_reduce(small[:, 8:10], small[:, 0:4].rearrange("p (a b) -> p a b", b=2), AX.X, ALU.min))
            V.do(vec.tensor_reduce(small[:, 10:12], small[:, 4:8].rearrange("p (a b) -> p a b", b=2), AX.X, ALU.max))
            V.do(vec.tensor_copy(smi[:, 0:4], small[:, 8:12]))
            V.do(vec.tensor_scalar(smi[:, 4:8], smi[:, 0:4], 6, None, ALU.arith_shift_right))
            V.do(vec.tensor_copy(small[:, 12:16], smi[:, 4:8]))
            V.did(vec.tensor_tensor(small[:, 16:18], small[:, 14:16], small[:, 12:14], ALU.subtract))
            V.do(vec.tensor_tensor(small[:, 18:22], small[:, 4:8], small[:, 0:4], ALU.subtract))
            V.did(vec.tensor_reduce(small[:, 22:23], small[:, 18:22], AX.X, ALU.max))
            V.do(vec.tensor_reduce(small[:, 23:24], small[:, 16:18], AX.X, ALU.max))
            vec.tensor_scalar(small[:, 28:30], small[:, 12:14], float(HP), None, ALU.mult).then_inc(s_statready, 1)
            dve.wait_ge(s_statready, 1)
            vec.tensor_tensor(v4(t_b), v4(dst_f), bc(small[:, 0:4], HE), ALU.subtract).then_inc(s_rowready, 1)
            V.did(vec.tensor_scalar(t_ai, src_i, 7, None, ALU.arith_shift_right))
            V.all()
            vec.tensor_scalar(t_c, t_ai, float(QS), None, ALU.mult).then_inc(s_rowready, 1)
            dve.wait_ge(s_rowready, 2)
            V.do(vec.tensor_scalar(t_ai, src_i, P - 1, None, ALU.bitwise_and))
            dve.wait_ge(s_rowt, 1)
            vec.tensor_copy(t_b, t_ai).then_inc(s_rowready, 1)
            dve.wait_ge(s_rowt, 2)
            vec.tensor_tensor(v2(t_c), v2(dst_f), bc(small[:, 28:30], 2 * HE), ALU.subtract).then_inc(s_rowready, 1)
            dve.wait_ge(s_rowt, 3)
            vec.scalar_tensor_tensor(t_b, src_i, float(REL), typ_i, ALU.mult, ALU.add).then_inc(s_rowready, 1)
            dve.wait_ge(s_rowt, 4)
            V.did(vec.tensor_copy(t_c, src_i))
            V.all()
            dve.sem_inc(s_rowready, 2)
            dve.wait_ge(s_statrow, 1)
            V.did(vec.tensor_reduce(small[0:1, 32:34], psum[0:1, 4, 0:2 * P].rearrange("p (a b) -> p a b", b=P), AX.X, ALU.max))
            V.did(vec.tensor_copy(base_row[0:1, 2:2 + NH].rearrange("o (c b) -> o b c", b=4), psum[0:1, 5, 0:4 * RP].rearrange("o (b c) -> o b c", c=RP)))
            V.did(vec.memset(base_row[0:1, 0:2], LASTBASE))
            V.did(vec.tensor_copy(tile_row[0:1, :].rearrange("o (c b) -> o b c", b=2), psum[0:1, 6, 0:2 * RP].rearrange("o (b c) -> o b c", c=RP)))
            V.all()
            V.do(vec.tensor_scalar(small[0:1, 34:36], small[0:1, 32:34], 0.0, None, ALU.max))
            vec.tensor_copy(passes[0:1, :], small[0:1, 34:36]).then_inc(s_passes, 1)
            dve.wait_ge(s_passes, 1)
            dve.wait_ge(s_rowout, 7)
            dve.wait_ge(s_zero, 2)
            for s in (s_code, s_oh, s_add, s_msg, s_relt):
                dve.sem_inc(s, 1)
            most = dve.value_load(passes[0:1, 0:1], min_val=0, max_val=N)
            base = [dve.alloc_register(f"base{k}") for k in range(4)]
            adj_at = lambda b: adj3[:, :, bass.ds(b, WIN)]

            def add_step(k, b, count):
                b = dve.snap(b, min_val=0, max_val=LASTBASE)
                dve.wait_ge(s_stage, count + 1)
                dve.wait_ge(s_add, count + 1)
                vec.tensor_tensor(adj_at(b), adj_at(b), STG[:, k % 2, 0:NT * WIN].rearrange("p (q c) -> p q c", c=WIN), ALU.add).then_inc(s_add, 1)

            with dve.Fori(0, most // WIN + 1) as p:
                g0 = dve.snap(p * NH)
                e0 = dve.snap(p * (NH + 2))
                c0 = dve.snap(p * 4)
                dve.wait_ge(s_add, e0 + 1)
                for k in range(2):
                    vec.memset(STG[:, k, :], 0.0).then_inc(s_stage, 1)
                dve.wait_ge(s_oh, g0 + 1)
                dve.wait_ge(s_code, c0 + 1)
                vec.tensor_scalar(code_c, rel_a, -1.0, float(WIN), ALU.max, ALU.min).then_inc(s_code, 1)
                dve.wait_ge(s_code, c0 + 2)
                vec.tensor_tensor(code_c, code_c, q_c, ALU.add).then_inc(s_code, 1)
                vec.tensor_scalar(rel_a, rel_a, float(WIN), None, ALU.subtract).then_inc(s_code, 1)
                dve.wait_ge(s_code, c0 + 4)
                dve.sem_inc(s_mark, 1)
                with dve.Fori(0, NH // 4) as i:
                    g = dve.snap(p * NH + i * 4)
                    e = dve.snap(p * (NH + 2) + i * 4)
                    dve.load(base, base_row[0:1, bass.ds(i * 4, 4)])
                    for k in range(4):
                        dve.wait_ge(s_built, g + k + 1)
                        for t in range(2):
                            vec.tensor_scalar(OHQ[:, k % 2, t, :], iota_code[:, :], code_c[:, bass.ds(i * 8 + (2 * k + t), 1)], None, ALU.is_equal)
                        for t in range(2):
                            last = vec.tensor_scalar(OHR[:, k % 2, t, :], iota_256[:, 0:P], r_c[:, bass.ds(i * 8 + (2 * k + t), 1)], None, ALU.is_equal)
                        last.then_inc(s_oh, 1)
                        add_step(k, base[k], e + k)
                dve.load(base[0:2], base_row[0:1, NH:NH + 2])
                for k in range(2):
                    add_step(k, base[k], e0 + (NH + k))
                dve.wait_ge(s_add, e0 + (NH + 3))
                vec.tensor_scalar(base_row[0:1, 2:2 + NH], base_row[0:1, 2:2 + NH], float(WIN), float(LASTBASE), ALU.add, ALU.min).then_inc(s_code, 1)
                dve.wait_ge(s_code, c0 + 5)
            dve.sem_inc(s_adj, 1)

            def transpose_adj(turn):
                for n, (q, m0, c) in enumerate(CH):
                    dve.wait_ge(s_tp, turn * len(CH) + n + 1)
                    vec.tensor_copy(adj_blk[:, m0:m0 + c, q, :], psum_h[:, 2 * (n % 4), 0:c * P].rearrange("p (j r) -> p j r", r=P)).then_inc(s_tx, 1)

            roots = [0]

            def inv_root(out, v, n):
                dve.sem_inc(s_var, 1)
                roots[0] += 1
                dve.wait_ge(s_root, roots[0])
                V.do(vec.reciprocal(st(5), st(4)))
                V.do(vec.tensor_tensor(st(6), st(5), st(5), ALU.mult))
                V.do(vec.tensor_tensor(st(6), st(6), st(3), ALU.mult))
                V.do(vec.tensor_scalar(st(6), st(6), -0.5, 1.5, ALU.mult, ALU.add))
                V.do(vec.tensor_tensor(out, st(5), st(6), ALU.mult))

            def layernorm(h, t):
                V.do(vec.tensor_reduce(st(0), x3, AX.X, ALU.add))
                V.do(vec.tensor_scalar(st(1), st(0), 1.0 / D, None, ALU.mult))
                V.do(vec.tensor_tensor(h, x3, bc(st(1)), ALU.subtract))
                V.do(vec.tensor_tensor(t, h, h, ALU.mult))
                V.do(vec.tensor_reduce(st(2), t, AX.X, ALU.add))
                V.do(vec.tensor_scalar(st(3), st(2), 1.0 / D, 1e-5, ALU.mult, ALU.add))
                inv_root(st(7), st(3), 0)
                V.do(vec.scalar_tensor_tensor(h, h, 0.0, bc(st(7)), ALU.max, ALU.mult))

            def split(parts, z, r, m0, m1, did=None):
                X = parts[:, m0:m1, :, :]
                V.do(vec.tensor_copy(X[:, :, 0, :], z))
                V.do(vec.tensor_tensor(r, z, X[:, :, 0, :], ALU.subtract))
                V.do(vec.tensor_copy(X[:, :, 1, :], r))
                V.do(vec.tensor_tensor(X[:, :, 2, :], r, X[:, :, 1, :], ALU.subtract))

            transpose_adj(0)
            dve.wait_ge(s_x, 32)
            V.all()
            layernorm(PA, PB)
            dve.wait_ge(s_deg, 1)
            vec.tensor_scalar(st(3), psum[:, 0, 0:NT], 2.0, 1.0, ALU.mult, ALU.add).then_inc(s_degread, 1)
            dve.wait_ge(s_degread, 1)
            inv_root(st(8), st(3), 0)
            V.do(vec.tensor_tensor(PA, PA, bc(st(8)), ALU.mult))
            split(XP[0], PA, PB, 0, NT)
            dve.sem_inc(s_xp, 1)
            for n in range(2):
                for b, (m0, m1) in enumerate(BANKS):
                    w = m1 - m0
                    z, y, r = PA[:, m0:m1, :], TY[:, 0:w, :], TR[:, 0:w, :]
                    dve.wait_ge(s_prop, n * NB + b + 1)
                    vec.tensor_reduce(y, psum[:, b % 8, 0:w * PART].rearrange("p (m c f) -> p m f c", c=3, f=D), AX.X, ALU.add).then_inc(s_bank, 1)
                    dve.wait_ge(s_bank, n * NB + b + 1)
                    V.do(vec.scalar_tensor_tensor(y, y, 2.0, z, ALU.mult, ALU.add))
                    V.do(vec.tensor_tensor(y, y, bc(st(8)[:, m0:m1]), ALU.mult))
                    if n == 0:
                        V.do(vec.tensor_tensor(z, y, bc(st(8)[:, m0:m1]), ALU.mult))
                        split(XP[1], z, r, m0, m1)
                    else:
                        V.do(vec.tensor_tensor(x3[:, m0:m1, :], x3[:, m0:m1, :], y, ALU.add))
                if n == 0:
                    dve.sem_inc(s_xp, 1)
            V.all()
            V.do(vec.memset(W2R, 0.0))
            dve.sem_inc(s_wz, 1)
            transpose_adj(1)
            layernorm(H, LNT)
            dve.sem_inc(s_h, 1)
            dve.wait_ge(s_deg, 2)
            V.do(vec.tensor_scalar(cnt_in[:, :], psum[:, 0, 0:NT], 2.0, None, ALU.mult))

            def features_out(c, dest, ready, done):
                dve.wait_ge(ready, c + 1)
                w = (HCH[c][1] - HCH[c][0]) * P
                vec.tensor_copy(dest[0:D, c % 2, 0:w], psum[0:D, 1, 0:w]).then_inc(done, 1)

            features_out(0, HT, s_ht, s_htc)
            for c, (m0, m1) in enumerate(HCH):
                if c + 1 < len(HCH):
                    features_out(c + 1, HT, s_ht, s_htc)
                for q in range(m0, m1):
                    dve.wait_ge(s_h2, q + 1)
                    if q >= 2:
                        dve.wait_ge(s_tab[q % 2], 16 * (q // 2))
                    vec.tensor_copy(H2[:, q % 2, :], psum[:, 6 + q % 2, 0:384]).then_inc(s_h2c, 1)
            V.do(vec.tensor_scalar(st(3), cnt_in[:, :], 1.0, None, ALU.max))
            inv_root(st(7), st(3), 0)
            V.do(vec.tensor_scalar(st(6), cnt_in[:, :], 0.0, None, ALU.is_gt))
            V.do(vec.tensor_tensor(dinv_in[:, :], st(7), st(6), ALU.mult))
            dve.wait_ge(s_tab[0], 16 * ((NT + 1) // 2))
            dve.wait_ge(s_tab[1], 16 * (NT // 2))
            V.did(vec.memset(ACC, 0.0))
            V.did(vec.tensor_copy(REL1, rel_b[:, :]))
            V.do(vec.tensor_copy(TILE1, tile_row[0:1, :]))
            dve.sem_inc(s_loop1, 1)
            dve.sem_inc(s_acc, 2)
            most = dve.value_load(passes[0:1, 1:2], min_val=0, max_val=BLANK)
            with dve.Fori(0, most // 2 + 1) as p:
                with dve.Fori(0, NG // 4) as i:
                    g = dve.snap(p * NG + i * 4)
                    dve.load(base, TILE1[0:1, bass.ds(i * 4, 4)])
                    m = dve.snap((p * NG + i * 4) * 5)
                    u = dve.snap((p * (NG // 4) + i) * 64)
                    for k in range(4):
                        dve.wait_ge(s_seg, g + (k + 3))
                        for t in range(4):
                            vec.tensor_scalar(OH1[:, k % 2, t, :], iota_256[:, 0:P], REL1[:, bass.ds(i * 16 + (4 * k + t), 1)], None, ALU.is_equal)
                        dve.wait_ge(s_gath[k], u + 64)
                        parts = GP[:, k % 2, :, :, :]
                        vec.tensor_tensor(WM, GM[:, k, :].rearrange("p (t f) -> p t f", t=4), bc(norm_c[:, bass.ds(i * 16 + 4 * k, 4)]), ALU.mult).then_inc(v_msg, 1)
                        dve.wait_ge(v_msg, m + (5 * k + 1))
                        vec.tensor_copy(parts[:, :, 0, :], WM).then_inc(v_msg, 1)
                        dve.wait_ge(v_msg, m + (5 * k + 2))
                        vec.tensor_tensor(WMR, WM, parts[:, :, 0, :], ALU.subtract).then_inc(v_msg, 1)
                        dve.wait_ge(v_msg, m + (5 * k + 3))
                        vec.tensor_copy(parts[:, :, 1, :], WMR).then_inc(v_msg, 1)
                        dve.wait_ge(v_msg, m + (5 * k + 4))
                        vec.tensor_tensor(parts[:, :, 2, :], WMR, parts[:, :, 1, :], ALU.subtract).then_inc(v_msg, 1)
                        dve.wait_ge(v_msg, m + (5 * k + 5))
                        dve.sem_inc(s_woh, 1)
                        dve.wait_ge(s_seg, g + (k + 5))
                        dve.wait_ge(s_acc, g + (k + 2))
                        at = ACC[:, bass.ds(dve.snap(base[k], min_val=0, max_val=BLANK) * D, D)]
                        vec.tensor_tensor(at, at, psum[:, 4 + k % 2, 0:D], ALU.add).then_inc(s_acc, 1)
                dve.wait_ge(s_woh, p * NG + NG)
                vec.tensor_scalar(REL1, REL1, float(P), None, ALU.subtract).then_inc(s_shift, 1)
                vec.tensor_scalar(TILE1, TILE1, 2.0, float(BLANK), ALU.add, ALU.min).then_inc(s_shift, 1)
                dve.wait_ge(s_shift, p * 2 + 2)
                dve.wait_ge(s_acc, p * NG + (NG + 2))

            def join(acc, t):
                a = acc[:, 0:2 * NT * D].rearrange("p (q w f) -> p q w f", w=2, f=D)
                V.did(vec.memset(t[0:HP, 0:1, :], 0.0))
                V.did(vec.tensor_copy(t[HP:P, :, :], a[0:HP, :, 1, :]))
                V.do(vec.tensor_copy(t[0:HP, 1:NT, :], a[HP:P, 0:NT - 1, 1, :]))
                V.do(vec.tensor_tensor(t, t, a[:, :, 0, :], ALU.add))

            V.all()
            join(ACC, JOIN)
            dve.wait_ge(s_w, 16 * 6)
            V.do(vec.tensor_tensor(JOIN, JOIN, B2R.unsqueeze(1).broadcast_to((P, NT, D)), ALU.add))
            V.do(vec.scalar_tensor_tensor(x3, JOIN, 0.0, x3, ALU.max, ALU.add))
            dve.wait_ge(s_lap, 1)
            dve.wait_ge(s_const, NCONST + 3 * K + 1)
            sm = lambda a, b: small[0:1, a:b]
            for n in range(1, K):
                V.do(vec.tensor_tensor(sm(n, n + 1), sm(n, n + 1), sm(n - 1, n), ALU.mult))
            V.do(vec.tensor_tensor(sm(32, 33 + K), sm(16, 17 + K), rec[0:1, 2 * K:3 * K + 1], ALU.mult))
            V.do(vec.tensor_tensor(sm(33, 33 + K), sm(33, 33 + K), sm(0, K), ALU.mult))
            dve.sem_inc(s_coef, 1)
            dve.wait_ge(s_coefb, 1)
            V.do(vec.tensor_copy(small[:, 48:48 + K + 1], psum[:, 7, 0:K + 1]))
            layernorm(PA, PB)
            V.do(vec.memset(PB, 0.0))
            V.do(vec.scalar_tensor_tensor(x3, PA, small[:, 48:49], x3, ALU.mult, ALU.add))
            for b, (m0, m1) in enumerate(BANKS):
                V.do(vec.tensor_tensor(TY[:, 0:m1 - m0, :], PA[:, m0:m1, :], bc(dinv_in[:, m0:m1]), ALU.mult))
                split(XP[0], TY[:, 0:m1 - m0, :], TR[:, 0:m1 - m0, :], m0, m1)
            dve.sem_inc(s_xp, 1)
            L = Count(dve, v_l2)
            PER = 2 * (1 + 8 * NB)
            with dve.Fori(0, K // 2) as i:
                L.base = dve.snap(i * PER)
                for u in range(2):
                    new = (PB, PA)[u]
                    n = i * 2 + u
                    L.do(vec.tensor_scalar(st(0), dinv_in[:, :], rec[:, bass.ds(n, 1)], None, ALU.mult))
                    for b, (m0, m1) in enumerate(BANKS):
                        w = m1 - m0
                        y, r, pn = TY[:, 0:w, :], TR[:, 0:w, :], new[:, m0:m1, :]
                        dve.wait_ge(s_prop, i * (2 * NB) + ((2 + u) * NB + b + 1))
                        vec.tensor_reduce(y, psum[:, b % 8, 0:w * PART].rearrange("p (m c f) -> p m f c", c=3, f=D), AX.X, ALU.add).then_inc(s_bank, 1)
                        dve.wait_ge(s_bank, i * (2 * NB) + ((2 + u) * NB + b + 1))
                        L.do(vec.tensor_tensor(y, y, bc(st(0)[:, m0:m1]), ALU.mult))
                        L.do(vec.scalar_tensor_tensor(pn, pn, rec[:, bass.ds(n + K, 1)], y, ALU.mult, ALU.add))
                        L.did(vec.scalar_tensor_tensor(x3[:, m0:m1, :], pn, small[:, bass.ds(n + 49, 1)], x3[:, m0:m1, :], ALU.mult, ALU.add))
                        L.do(vec.tensor_tensor(y, pn, bc(dinv_in[:, m0:m1]), ALU.mult))
                        X = XP[1 - u][:, m0:m1, :, :]
                        L.do(vec.tensor_copy(X[:, :, 0, :], y))
                        L.do(vec.tensor_tensor(r, y, X[:, :, 0, :], ALU.subtract))
                        L.do(vec.tensor_copy(X[:, :, 1, :], r))
                        L.do(vec.tensor_tensor(X[:, :, 2, :], r, X[:, :, 1, :], ALU.subtract))
                    dve.sem_inc(s_xp, 1)
                assert L.n == PER
            dve.sem_inc(s_l2done, 1)
            layernorm(H3, LNT3)
            dve.sem_inc(s_h, 1)
            V.did(vec.memset(HT3[0:D, NP:], 0.0))
            V.did(vec.memset(ACC3, 0.0))
            V.did(vec.tensor_copy(REL3, rel_b[:, :]))
            V.did(vec.memset(TILE3[0:1, 0:2], BLANK))
            V.did(vec.tensor_copy(TILE3[0:1, 2:2 + NG], tile_row[0:1, :]))
            V.all()
            dve.sem_inc(s_shift3, 2)
            for c, (m0, m1) in enumerate(HCH):
                dve.wait_ge(s_ht3, c + 1)
                vec.tensor_copy(HT3[0:D, m0 * P:m1 * P], psum[0:D, 1, 0:(m1 - m0) * P]).then_inc(s_htc3, 1)
            for c, (w0, w1) in enumerate(WCH):
                w = (w1 - w0) * HID
                X = PD[:, w0 * 3 * HID:w1 * 3 * HID].rearrange("p (q j f) -> p q j f", j=3, f=HID)
                r = PDR[:, c % 2, 0:w].rearrange("p (q f) -> p q f", f=HID)
                dve.wait_ge(s_pdhi, 2 * c + 1)
                V.did(vec.tensor_tensor(r, psum[:, 2 + c % 4, 0:w].rearrange("p (q f) -> p q f", f=HID), X[:, :, 0, :], ALU.subtract))
                V.all()
                dve.sem_inc(s_pdr, 1)
                dve.wait_ge(s_pdhi, 2 * c + 2)
                V.do(vec.tensor_tensor(X[:, :, 2, :], r, X[:, :, 1, :], ALU.subtract))
                dve.sem_inc(s_pdc, 1)
            dve.sem_inc(s_oht, 4)
            dve.sem_inc(s_acc3, 2)

            def one_hot_t(k, n, used):
                dve.wait_ge(s_rel3[k], used)
                dve.wait_ge(s_z1, n + 1)
                vec.tensor_scalar(OHT[:, k % 2, :], REL_ROW[:, k, :], iota_p[:, 0:1], None, ALU.is_equal).then_inc(s_oht, 1)

            def one_hot(k, n, cols):
                dve.wait_ge(s_seg3, n + 1)
                for t in range(4):
                    last = vec.tensor_scalar(OHF[:, k % 2, t, :], iota_256[:, 0:P], REL3[:, cols(t)], None, ALU.is_equal)
                last.then_inc(s_ohf, 1)

            def message(k, n, m):
                dve.wait_ge(s_w3, n + 3)
                z, X = psum[:, 5, 0:4 * D].rearrange("p (t f) -> p t f", t=4), MS[:, k % 2, :, :, :]
                vec.tensor_copy(X[:, :, 0, :], z).then_inc(v_mlp, 1)
                dve.wait_ge(v_mlp, m + 1)
                vec.tensor_tensor(MSR, z, X[:, :, 0, :], ALU.subtract).then_inc(v_mlp, 1)
                dve.wait_ge(v_mlp, m + 2)
                vec.tensor_copy(X[:, :, 1, :], MSR).then_inc(v_mlp, 1)
                dve.wait_ge(v_mlp, m + 3)
                vec.tensor_tensor(X[:, :, 2, :], MSR, X[:, :, 1, :], ALU.subtract).then_inc(s_msg, 1)

            def add_sums(k, n, window, m):
                dve.wait_ge(s_seg3, n + 3)
                dve.wait_ge(s_acc3, n + 2)
                vec.tensor_reduce(SUM3, psum[:, 6 + k % 2, 0:PART].rearrange("p (j f) -> p f j", j=3), AX.X, ALU.add).then_inc(v_mlp, 1)
                dve.wait_ge(v_mlp, m + 1)
                at = ACC3[:, bass.ds(dve.snap(window, min_val=0, max_val=BLANK) * D, D)]
                vec.tensor_tensor(at, at, SUM3, ALU.add).then_inc(s_acc3, 1)

            def mlp(i, n, used, m, first=False, last=False):
                off = -5 if first else 0
                at = slice(i * 4, 4 + i * 4) if isinstance(i, int) else bass.ds(i * 4, 4)
                dve.load(base, TILE3[0:1, at])
                for k in range(4):
                    if not (last and k == 3):
                        one_hot_t((k + 1) % 4, n + (k + 1), used + (16 if k < 3 else 32))
                    if not (first and k == 0):
                        cols = (lambda t: slice(i * 16 + 4 * k - 4 + t, i * 16 + 4 * k - 3 + t)) if isinstance(i, int) else \
                            (lambda t: bass.ds(i * 16 + (4 * k - 4 + t), 1))
                        one_hot(k - 1, n + (k - 1), cols)
                        message(k - 1, n + (k - 1), m + (0 if first and k == 1 else 4 * k + off))
                    if not (first and k < 2):
                        add_sums(k - 2, n + (k - 2), base[k], m + (4 * k + 3 + off))

            with dve.Fori(0, most // 2 + 1) as p:
                n0 = dve.snap(p * NG)
                dve.wait_ge(s_relt, p + 1)
                vec.tensor_scalar(CLAMP, REL3, -1.0, float(P), ALU.max, ALU.min).then_inc(s_clamp, 1)
                one_hot_t(0, n0, dve.snap(p * (16 * NG // 4) + 16))
                mlp(0, n0, dve.snap(p * (16 * NG // 4)), dve.snap(p * (4 * NG)), first=True)
                with dve.Fori(1, NG // 4 - 1) as i:
                    mlp(i, dve.snap(p * NG + i * 4), dve.snap(p * (16 * NG // 4) + i * 16), dve.snap(p * (4 * NG) + i * 16 - 5))
                n1 = dve.snap(p * NG + (NG - 4))
                m1 = dve.snap(p * (4 * NG) + (4 * NG - 21))
                mlp(NG // 4 - 1, n1, dve.snap(p * (16 * NG // 4) + 16 * (NG // 4 - 1)), m1, last=True)
                one_hot(3, n1 + 3, lambda t: slice(NC - 4 + t, NC - 3 + t))
                message(3, n1 + 3, m1 + 16)
                dve.load(base[0:2], TILE3[0:1, NG:NG + 2])
                add_sums(2, n1 + 2, base[0], m1 + 19)
                add_sums(3, n1 + 3, base[1], m1 + 20)
                dve.wait_ge(s_acc3, n0 + (NG + 2))
                vec.tensor_scalar(REL3, REL3, float(P), None, ALU.subtract).then_inc(s_shift3, 1)
                vec.tensor_scalar(TILE3[0:1, 2:2 + NG], TILE3[0:1, 2:2 + NG], 2.0, float(BLANK), ALU.add, ALU.min).then_inc(s_shift3, 2)
                dve.wait_ge(s_shift3, p * 3 + 5)
            acc3 = JOIN3
            join(ACC3, JOIN3)
            V.do(vec.tensor_scalar(st(0), cnt_in[:, :], 1.0, None, ALU.max))
            V.do(vec.reciprocal(st(1), st(0)))
            V.do(vec.tensor_tensor(acc3, acc3, bc(st(1)), ALU.mult))
            V.do(vec.tensor_scalar(st(2), cnt_in[:, :], 0.0, None, ALU.is_gt))
            V.do(vec.tensor_tensor(LNT3, B3R.unsqueeze(1).broadcast_to((P, NT, D)), bc(st(2)), ALU.mult))
            V.do(vec.tensor_tensor(acc3, acc3, LNT3, ALU.add))
            V.do(vec.tensor_tensor(acc3, acc3, H3, ALU.add))
            V.do(vec.tensor_tensor(x3, x3, acc3, ALU.add))
            dve.sem_inc(s_final, 1)


_INS = ['x', 'src', 'dst', 'edge_attr_16', 'edge_type_8', 'edge_weight1', 'L1_gnn_weight1', 'L1_gnn_weight2', 'L1_gnn_bias1',
        'L1_gnn_bias2', 'L2_gnn_lap_coefs', 'L2_gnn_mf_weights', 'L3_gnn_W1', 'L3_gnn_b1', 'L3_gnn_W2', 'L3_gnn_b2',
        'L3_gnn_W3', 'L3_gnn_b3']


def kernel(**inputs):
    import numpy as _np
    import concourse.bacc as _bacc
    from concourse import mybir as _mybir
    from concourse.bass_utils import run_bass_kernel_spmd as _run

    nc = _bacc.Bacc("TRN2", target_bir_lowering=False, num_devices=1)
    arrays, args = {}, []
    for name in _INS:
        a = _np.ascontiguousarray(inputs[name])
        arrays[f"in_{name}_dram"] = a
        args.append(nc.dram_tensor(f"in_{name}_dram", a.shape, _mybir.dt.from_np(a.dtype), kind="ExternalInput").ap())
    args.append(nc.dram_tensor("out_0_dram", (N, D), F32, kind="ExternalOutput").ap())
    gnn(nc, *args)
    r = _run(nc, [arrays], core_ids=[0])
    return r.results[0]["out_0_dram"]
```

```python
from contextlib import ExitStack
import math

import concourse.bass as bass
from concourse import mybir

ALU = mybir.AluOpType
ACT = mybir.ActivationFunctionType
AX = mybir.AxisListType
F32 = mybir.dt.float32
BF16 = mybir.dt.bfloat16
F16 = mybir.dt.float16
I32 = mybir.dt.int32
U32 = mybir.dt.uint32

P = 128
N, D = 3125, 48
E = 100000
NT = -(-N // P)
NP = NT * P
NREM = N - (NT - 1) * P
RE = 1024
RP = -(-E // RE)
RREM = E - (RP - 1) * RE
HE = 256
NH = RP * RE // HE
NC = 2 * NH
UNR = 28
BATCH = 14
RING = 7
NG = NH // 2
WIN = 24
QS = WIN + 2
QH = -(-NT // 2)
HALF = [(0, QH), (QH, NT)]
LASTBASE = NP - WIN
ADJ = NT * NP
HP = P // 2
BLANK = 2 * NT
NW = BLANK + 1
REL = 8
HID = 128
EF = 16
K = 10
PART = 3 * D
TPB = 3
NB = -(-NT // TPB)
BIG = 16384.0


def jacobi():
    a = b = 1.0
    an, cn = [(a + b + 2.0) / 2.0], [0.0]
    for n in range(2, K + 1):
        nab = 2 * n + a + b
        an.append(nab * (nab - 1) * (nab - 2) / (2 * n * (nab - n) * (nab - 2)))
        cn.append(-(2 * (n + a - 1) * (n + b - 1) * nab) / (2 * n * (nab - n) * (nab - 2)))
    norm = []
    for i in range(K + 1):
        t1 = math.pow(2.0, a + b + 1) / (2 * i + a + b + 1)
        t2 = math.exp(math.lgamma(i + a + 1) - math.lgamma(i + a + b + 1))
        t3 = math.exp(math.lgamma(i + b + 1) - math.lgamma(i + 1))
        norm.append(math.sqrt(t1 * t2 * t3))
    return an, cn, norm


class Count:

    def __init__(self, eng, sem):
        self.eng, self.sem, self.n, self.base = eng, sem, 0, 0

    def did(self, instruction):
        self.n += 1
        instruction.then_inc(self.sem, 1)

    def all(self):
        self.eng.wait_ge(self.sem, self.base + self.n)

    def do(self, instruction):
        self.did(instruction)
        self.all()


def gnn(nc, x_d, src_d, dst_d, ea_d, et_d, ew_d, w1_d, w2_d, b1_d, b2_d, lap_d, mf_d,
        m1_d, mb1_d, m2_d, mb2_d, m3_d, mb3_d, out_d):
    ctx = ExitStack()
    with ctx:
        def sb(name, shape, dt):
            return ctx.enter_context(nc.sbuf_tensor(name, shape, dt))

        def sem(name):
            return ctx.enter_context(nc.semaphore(name))

        msg_table = nc.dram_tensor("msg_table", (NP * REL, D), F32, kind="Internal").ap()
        node_table = nc.dram_tensor("node_table", (NP, D), F32, kind="Internal").ap()
        rel_rows = nc.dram_tensor("rel_rows", (NC, P), BF16, kind="Internal").ap()

        adj = sb("adj", [P, ADJ], F16)
        scr = sb("scr", [P, 6700], F32)
        x = sb("x", [P, NT * D], F32)
        rel_b = sb("rel_b", [P, NC], F32)
        norm_c = sb("norm_c", [P, NC], F32)
        idx_msg = sb("idx_msg", [P, NC], U32)
        idx_src = sb("idx_src", [P, NC], U32)
        iota_code = sb("iota_code", [P, NT * WIN], F16)
        iota_256 = sb("iota_256", [P, 256], F16)
        iota_p = sb("iota_p", [P, 1], F32)
        ident = sb("ident", [P, P], F32)
        identh = sb("identh", [P, P], F16)
        identh2 = sb("identh2", [P, P], F16)
        ones = sb("ones", [P, P], F32)
        onesh = sb("onesh", [P, 2], F16)
        base_row = sb("base_row", [1, NH], I32)
        tile_row = sb("tile_row", [1, NG], I32)
        passes = sb("passes", [1, 2], I32)
        stat = sb("stat", [P, 9 * NT], F32)
        dinv_in = sb("dinv_in", [P, NT], F32)
        cnt_in = sb("cnt_in", [P, NT], F32)
        rec = sb("rec", [P, 3 * K + 1], F32)
        small = sb("small", [P, 64], F32)
        smi = sb("smi", [P, 16], I32)
        psum = ctx.enter_context(nc.psum_tensor("psum", [P, 8, 512], F32))
        psum_h = psum[:, :, :].bitcast(F16)
        x3 = x[:, :].rearrange("p (q f) -> p q f", f=D)
        adj3 = adj[:, :].rearrange("p (q n) -> p q n", n=NP)

        adj_f = adj[:, :].bitcast(F32)
        ROW0 = ADJ // 2 - 8 * RE

        ZERO0 = 3 * RE

        def row(k):
            return adj_f[0:RP, ROW0 + k * RE:ROW0 + (k + 1) * RE]
        dst_i, src_i, typ_i = (row(k).bitcast(I32) for k in range(3))
        nrm_f, dst_f, t_a, t_b, t_c = (row(k) for k in range(3, 8))
        code_c = scr[:, 0:NC]
        rel_a = scr[:, NC:2 * NC]
        q_c = scr[:, 2 * NC:3 * NC]
        r_c = scr[:, 3 * NC:4 * NC]
        ROWS = [t_b, t_c, t_b, t_c, t_b, t_c, nrm_f]
        COLS = [rel_a, q_c, r_c, rel_b[:, :], idx_msg[:, :], idx_src[:, :], norm_c[:, :]]
        s_final = sem("s_final")
        OUT = [(0, NT // 2), (NT // 2, NT)]

        s_fill = sem("s_fill")
        s_in = sem("s_in")
        s_x = sem("s_x")
        s_const = sem("s_const")
        s_id0 = sem("s_id0")
        s_zero = sem("s_zero")
        v_seq = sem("v_seq")
        s_rowready = sem("s_rowready")
        s_rowt = sem("s_rowt")
        s_rowout = sem("s_rowout")
        s_statready = sem("s_statready")
        s_statrow = sem("s_statrow")
        s_passes = sem("s_passes")
        s_code = sem("s_code")
        s_oh = sem("s_oh")
        s_used = sem("s_used")
        s_built = sem("s_built")
        s_land = sem("s_land")
        s_adj = sem("s_adj")
        s_tp = sem("s_tp")
        s_tx = sem("s_tx")
        s_ty = sem("s_ty")
        s_deg = sem("s_deg")
        s_degread = sem("s_degread")
        s_var = sem("s_var")
        s_root = sem("s_root")
        s_xp = sem("s_xp")
        s_prop = sem("s_prop")
        s_bank = sem("s_bank")
        s_out = sem("s_out")

        H1T = scr[:, 0:2048].rearrange("p (c n) -> p c n", c=4)
        HT = scr[0:D, 2048:3072].rearrange("p (s n) -> p s n", s=2)
        H2 = scr[:, 3072:3840].rearrange("p (s c) -> p s c", s=2)
        W1R = scr[0:D, 5816:6328].rearrange("p (c j) -> p c j", c=4)
        W2R = scr[:, 4224:4608].rearrange("p (c j) -> p c j", c=4)
        B1R = scr[:, 4608:4609]
        H = scr[:, 4616:5816].rearrange("p (q f) -> p q f", f=D)
        LNT = scr[:, 0:1200].rearrange("p (q f) -> p q f", f=D)
        GM = scr[:, 0:768].rearrange("p (s c) -> p s c", s=4)
        IDX = scr[:, 768:784].bitcast(U32).rearrange("p (s c) -> p s c", s=4)
        OH1 = scr[:, 784:1296].bitcast(BF16).rearrange("p (s t c) -> p s t c", s=2, t=4)
        WM = scr[:, 1296:1488].rearrange("p (t f) -> p t f", t=4)
        GP = scr[:, 1488:2064].bitcast(BF16).rearrange("p (s t j f) -> p s t j f", s=2, t=4, j=3)
        ACC = scr[:, 2064:2064 + NW * D]
        B2R = scr[:, 4512:4512 + D]
        REL1 = scr[:, 4560:4560 + NC]
        TILE1 = scr[0:1, 5344:5344 + NG].bitcast(I32)
        WMR = scr[:, 5540:5732].rearrange("p (t f) -> p t f", t=4)
        JOIN = scr[:, 0:1200].rearrange("p (q f) -> p q f", f=D)
        HCH = [(c * 4, min(NT, c * 4 + 4)) for c in range(-(-NT // 4))]

        WCH = [(c * 4, min(NW, c * 4 + 4)) for c in range(-(-NW // 4))]

        spot = [0]

        def place(n):
            spot[0] += n
            return adj_f[:, spot[0] - n:spot[0]]
        PD = place(NW * 3 * HID // 2).bitcast(BF16)
        G3 = place(4 * 4 * 64).rearrange("p (s t c) -> p s t c", s=4, t=4)
        GT = place(2 * 512).rearrange("p (s c) -> p s c", s=2)
        REL_ROW = place(4 * 256).bitcast(BF16).rearrange("p (s c) -> p s c", s=4)
        OHT = place(512).bitcast(BF16).rearrange("p (s c) -> p s c", s=2)
        OHF = place(512).bitcast(BF16).rearrange("p (s t c) -> p s t c", s=2, t=4)
        R1 = place(2 * 512).rearrange("p (s c) -> p s c", s=2)
        R2 = place(2 * 512).rearrange("p (s c) -> p s c", s=2)
        MS = place(2 * 6 * D).bitcast(BF16).rearrange("p (s t j f) -> p s t j f", s=2, t=4, j=3)
        MSR = place(4 * D).rearrange("p (t f) -> p t f", t=4)
        SUM3 = place(D)
        ACC3 = place(NW * D)
        REL3 = rel_b[:, :]
        CLAMP = norm_c[:, :]
        RELT = idx_msg[:, 0:7 * P // 2].bitcast(BF16).rearrange("p (j c) -> p j c", j=7)
        H3 = place(NT * D).rearrange("p (q f) -> p q f", f=D)
        LNT3 = place(NT * D).rearrange("p (q f) -> p q f", f=D)
        HT3 = place(NP + 2 * P)
        JOIN3 = HT3[:, 0:NT * D].rearrange("p (q f) -> p q f", f=D)
        PDR = place(1024).rearrange("p (s c) -> p s c", s=2)
        W1AC, W1B, W2M, W3M = place(HID), place(HID), place(HID), place(D)
        BM = place(2)
        B3R = place(D)
        TILE3 = place(2 + NG)[0:1, :].bitcast(I32)
        IDX3 = place(16).bitcast(U32).rearrange("p (s c) -> p s c", s=4)

        s_w = sem("s_w")
        s_wz = sem("s_wz")
        s_h = sem("s_h")
        s_ht = sem("s_ht")
        s_htc = sem("s_htc")
        s_h1 = sem("s_h1")
        s_h1r = sem("s_h1r")
        s_h2 = sem("s_h2")
        s_h2c = sem("s_h2c")
        s_tab = [sem("s_tab0"), sem("s_tab1")]
        s_loop1 = sem("s_loop1")
        s_idx = sem("s_idx")
        s_gath = [sem(f"s_gath{k}") for k in range(4)]
        s_woh = sem("s_woh")
        s_seg = sem("s_seg")
        s_acc = sem("s_acc")
        s_shift = sem("s_shift")
        s_coef = sem("s_coef")
        s_lap = sem("s_lap")
        s_lapin = sem("s_lapin")
        s_coefb = sem("s_coefb")
        v_l2 = sem("v_l2")
        s_w3in = sem("s_w3in")
        s_node = sem("s_node")
        s_ht3 = sem("s_ht3")
        s_htc3 = sem("s_htc3")
        s_pd = sem("s_pd")
        s_pdc = sem("s_pdc")
        s_clamp = sem("s_clamp")
        s_relt = sem("s_relt")
        s_reltc = sem("s_reltc")
        s_relst = sem("s_relst")
        s_idx3 = sem("s_idx3")
        s_in3 = [sem(f"s_in3{k}") for k in range(4)]
        s_ef = [sem(f"s_ef{k}") for k in range(4)]
        s_rel3 = [sem(f"s_rel3{k}") for k in range(4)]
        s_t3 = sem("s_t3")
        s_gt = sem("s_gt")
        s_oht = sem("s_oht")
        s_z1 = sem("s_z1")
        s_r1 = sem("s_r1")
        s_z2 = sem("s_z2")
        s_r2 = sem("s_r2")
        s_w3 = sem("s_w3")
        s_msg = sem("s_msg")
        s_ohf = sem("s_ohf")
        s_seg3 = sem("s_seg3")
        s_acc3 = sem("s_acc3")
        s_shift3 = sem("s_shift3")
        v_msg = sem("v_msg")
        v_mlp = sem("v_mlp")
        s_pdhi = sem("s_pdhi")
        s_pdr = sem("s_pdr")
        s_pdmid = sem("s_pdmid")
        s_mark = sem("s_mark")
        AN, CN, NORM = jacobi()

        block = ctx.enter_context(nc.Block())

        CH = [(q, m, min(8, NT - m)) for q in range(NT) for m in range(q, NT, 8)]
        LOWER = []
        for q, m, c in CH:
            LOWER.append((LOWER[-1] if LOWER else 0) + (m + c - 1 > q))
        adj_blk = adj[:, :].rearrange("p (q m r) -> p q m r", m=NT, r=P)
        PAIRS = ((0, 2, 4, 6), (0, 2, 6))
        NCONST = 8

        XP = [scr[:, k * 1800:(k + 1) * 1800].bitcast(BF16).rearrange("p (q j f) -> p q j f", j=3, f=D) for k in range(2)]
        PA = scr[:, 3600:4800].rearrange("p (q f) -> p q f", f=D)
        PB = scr[:, 4800:6000].rearrange("p (q f) -> p q f", f=D)
        TY = scr[:, 6000:6000 + TPB * D].rearrange("p (q f) -> p q f", f=D)
        TR = scr[:, 6144:6144 + TPB * D].rearrange("p (q f) -> p q f", f=D)
        Z2, R2S = (scr[:, 1800 + k * 3 * TPB * D:1800 + (k + 1) * 3 * TPB * D].rearrange("p (q f) -> p q f", f=D) for k in range(2))
        BANKS = [(b * TPB, min(NT, (b + 1) * TPB)) for b in range(NB)]
        o = 4 * NC
        OHQ = scr[:, o:o + RING * NT * WIN // 2].bitcast(F16).rearrange("p (s c) -> p s c", s=RING)
        o += RING * NT * WIN // 2
        OHR = scr[:, o:o + RING * P // 2].bitcast(F16).rearrange("p (s c) -> p s c", s=RING)

        def cut(start, n):
            return slice(start, start + n) if isinstance(start, int) else bass.ds(start, n)

        PEEL = 32
        BEFORE = [j * len(CH) // (PEEL - 4) for j in range(PEEL - 3)]

        def st(k, n=1):
            return stat[:, k * NT:(k + n) * NT]

        def bc(a, n=D):
            return a.unsqueeze(2).broadcast_to((a.shape[0], a.shape[1], n))

        @block.sync
        def _(sp):
            sp.wait_ge(s_fill, 4)
            for dst, src in ((dst_i, dst_d), (src_i, src_d), (typ_i, et_d)):
                sp.dma_start(dst[0:RP - 1, :], src[0:(RP - 1) * RE].rearrange("(p c) -> p c", c=RE)).then_inc(s_in, 16)
                sp.dma_start(dst[RP - 1:RP, 0:RREM], src[(RP - 1) * RE:E].rearrange("(p c) -> p c", c=RREM)).then_inc(s_in, 16)
            sp.dma_start(nrm_f[0:RP - 1, :], ew_d[0:(RP - 1) * RE, :].rearrange("(p c) o -> p (c o)", c=RE)).then_inc(s_in, 16)
            sp.dma_start(nrm_f[RP - 1:RP, 0:RREM], ew_d[(RP - 1) * RE:E, :].rearrange("(p c) o -> p (c o)", c=RREM)).then_inc(s_in, 16)
            sp.wait_ge(s_fill, 5)
            sp.dma_start(x3[:, 0:NT - 1, :], x_d[0:(NT - 1) * P, :].rearrange("(q r) f -> r q f", r=P)).then_inc(s_x, 16)
            sp.dma_start(x3[0:NREM, NT - 1, :], x_d[(NT - 1) * P:N, :]).then_inc(s_x, 16)
            sp.wait_ge(s_wz, 1)
            w1_v = w1_d.rearrange("(c s) i j -> s i c j", s=2)
            w2_v = w2_d.rearrange("(c s) i j -> s i c j", s=2)
            for k in range(2):
                sp.dma_start(W1R[:, :, k * D:(k + 1) * D], w1_v[k]).then_inc(s_w, 16)
                sp.dma_start(W2R[k * D:(k + 1) * D, :, k * D:(k + 1) * D], w2_v[k]).then_inc(s_w, 16)
                sp.dma_start(B1R[k * D:(k + 1) * D, :], b1_d.rearrange("(p o) -> p o", o=1)).then_inc(s_w, 16)
            table = msg_table.rearrange("(q r e) f -> q r (e f)", r=P, e=REL)
            for q in range(NT):
                sp.wait_ge(s_h2c, q + 1)
                sp.dma_start(table[q], H2[:, q % 2, :]).then_inc(s_tab[q % 2], 16)
            sp.wait_ge(s_loop1, 1)
            sp.dma_start(B2R, b2_d.partition_broadcast(P)).then_inc(s_w, 16)
            sp.dma_start(small[0:1, 0:K + 1], lap_d.rearrange("(o k) -> o k", o=1)).then_inc(s_lapin, 16)
            sp.dma_start(small[0:1, 16:16 + K + 1], mf_d.rearrange("o k e -> o (k e)")).then_inc(s_lapin, 16)
            sp.wait_ge(s_prop, (2 + K) * NB)
            for dst, src in ((W1AC[0:D, :], m1_d[0:D, :]), (W1AC[D:D + EF, :], m1_d[2 * D:2 * D + EF, :]), (W1B[0:D, :], m1_d[D:2 * D, :]),
                             (W2M, m2_d), (W3M, m3_d), (BM[:, 0:1], mb1_d.rearrange("(p o) -> p o", o=1)),
                             (BM[:, 1:2], mb2_d.rearrange("(p o) -> p o", o=1)), (B3R, mb3_d.partition_broadcast(P))):
                sp.dma_start(dst, src).then_inc(s_w3in, 16)

            def store_codes():
                sp.dma_start(rel_rows.rearrange("(j c) e -> c j e", j=7), RELT[0:NC // 7, :, :]).then_inc(s_relst, 16)

            sp.wait_ge(s_reltc, 1)
            store_codes()
            sp.wait_ge(s_h, 2)
            sp.dma_start(node_table.rearrange("(q r) f -> r q f", r=P), H3).then_inc(s_node, 16)
            sp.wait_ge(s_relst, 16)
            most = sp.value_load(passes[0:1, 1:2], min_val=0, max_val=BLANK)
            with sp.Fori(0, most // 2 + 1) as p:
                def load(i, n):
                    for k in range(4):
                        sp.wait_ge(s_oht, n + k + 1)
                        codes = rel_rows[bass.ds((i * 4 + k) * 4, 4), :] if not isinstance(i, int) else rel_rows[(i * 4 + k) * 4:(i * 4 + k) * 4 + 4, :]
                        sp.dma_start(REL_ROW[:, k, :], codes.rearrange("a b -> (a b)").partition_broadcast(P)).then_inc(s_rel3[k], 16)
                        sp.wait_ge(s_t3, n + k + 1)
                        for h in range(2):
                            if isinstance(i, int):
                                e0 = ((i * 4 + k) * 2 + h) * HE
                                m = min(HE, E - e0)
                                if m > 0:
                                    sp.dma_start(G3[0:m // 2, k, 2 * h:2 * h + 2, D:D + EF], ea_d[e0:e0 + m, :].rearrange("(p t) f -> p t f", t=2))\
                                      .then_inc(s_ef[k], 16 if h or e0 + HE < E else 32)
                            else:
                                sp.dma_start(G3[:, k, 2 * h:2 * h + 2, D:D + EF],
                                             ea_d[bass.ds(i * (8 * HE) + (2 * k + h) * HE, HE), :].rearrange("(p t) f -> p t f", t=2)).then_inc(s_ef[k], 16)
                with sp.Fori(0, NG // 4 - 1) as i:
                    load(i, sp.snap(p * NG + i * 4))
                load(NG // 4 - 1, sp.snap(p * NG + (NG - 4)))
                sp.wait_ge(s_reltc, p + 2)
                sp.sem_inc(s_mark, 1)
                sp.wait_ge(s_oht, p * NG + (NG + 4))
                sp.sem_inc(s_mark, 1)
                store_codes()
                sp.wait_ge(s_relst, p * 16 + 32)
                sp.sem_inc(s_mark, 1)
            for k, (m0, m1) in enumerate(OUT):
                sp.wait_ge(s_final, k + 1)
                m1 = min(m1, NT - 1)
                sp.dma_start(out_d[m0 * P:m1 * P, :].rearrange("(q r) f -> r q f", r=P), x3[:, m0:m1, :]).then_inc(s_out, 16)
            sp.dma_start(out_d[(NT - 1) * P:N, :], x3[0:NREM, NT - 1, :]).then_inc(s_out, 16)
            sp.wait_ge(s_out, 16 * (len(OUT) + 1))

        @block.gpsimd
        def _(pool):
            nc.gpsimd.memset(ident[:, :], 0.0).then_inc(s_id0, 1)
            nc.gpsimd.memset(identh[:, :], 0.0).then_inc(s_id0, 1)
            nc.gpsimd.memset(identh2[:, :], 0.0).then_inc(s_id0, 1)
            nc.gpsimd.memset(ones[:, :], 1.0).then_inc(s_const, 1)
            nc.gpsimd.memset(onesh[:, :], 1.0).then_inc(s_const, 1)
            pool.wait_ge(s_id0, 3)
            for m in (ident, identh):
                nc.gpsimd.affine_select(out=m[:, :], in_=m[:, :], compare_op=ALU.not_equal, fill=1.0, base=0,
                                        pattern=[[-1, P]], channel_multiplier=1).then_inc(s_const, 1)
            nc.gpsimd.affine_select(out=identh2[:, :], in_=identh2[:, :], compare_op=ALU.not_equal, fill=2.0, base=0,
                                    pattern=[[-1, P]], channel_multiplier=1).then_inc(s_const, 1)
            nc.gpsimd.iota(iota_code[:, :], pattern=[[QS, NT], [1, WIN]], base=0, channel_multiplier=0,
                           allow_small_or_imprecise_dtypes=True).then_inc(s_const, 1)
            nc.gpsimd.iota(iota_256[:, :], pattern=[[1, 256]], base=0, channel_multiplier=0,
                           allow_small_or_imprecise_dtypes=True).then_inc(s_const, 1)
            nc.gpsimd.iota(iota_p[:, :], pattern=[[1, 1]], base=0, channel_multiplier=1,
                           allow_small_or_imprecise_dtypes=True).then_inc(s_const, 1)
            nc.gpsimd.memset(adj_f[:, ZERO0:ROW0], 0.0).then_inc(s_zero, 1)
            pool.wait_ge(s_rowready, 7)
            nc.gpsimd.memset(adj_f[:, ROW0 + 4 * RE:ROW0 + 6 * RE], 0.0).then_inc(s_zero, 1)
            pool.wait_ge(s_rowt, 7)
            nc.gpsimd.memset(adj_f[:, ROW0 + 3 * RE:ROW0 + 4 * RE], 0.0).then_inc(s_zero, 1)
            nc.gpsimd.memset(adj_f[:, ROW0 + 6 * RE:ADJ // 2], 0.0).then_inc(s_zero, 1)
            for n in range(K):
                nc.gpsimd.memset(rec[:, n:n + 1], 2.0 * AN[n]).then_inc(s_const, 1)
                nc.gpsimd.memset(rec[:, K + n:K + n + 1], CN[n]).then_inc(s_const, 1)
            for n in range(K + 1):
                nc.gpsimd.memset(rec[0:1, 2 * K + n:2 * K + n + 1], 1.0 / NORM[n]).then_inc(s_const, 1)
            pool.wait_ge(s_tab[0], 16 * ((NT + 1) // 2))
            pool.wait_ge(s_tab[1], 16 * (NT // 2))
            pool.wait_ge(s_loop1, 1)
            most = pool.value_load(passes[0:1, 1:2], min_val=0, max_val=BLANK)
            with pool.Fori(0, most // 2 + 1) as p:
                with pool.Fori(0, NG // 4) as i:
                    g = pool.snap(p * NG + i * 4)
                    for k in range(4):
                        pool.wait_ge(s_idx, g + k + 1)
                        pool.wait_ge(s_seg, g + k + 1)
                        pool.sem_inc(s_mark, 1)
                        for t in range(4):
                            pool.indirect_dma_start(out=GM[:, k, t * D:(t + 1) * D], out_offset=None, in_=msg_table,
                                                    in_offset=bass.IndirectOffsetOnAxis(ap=IDX[:, k, t:t + 1], axis=0)).then_inc(s_gath[k], 16)
            pool.wait_ge(s_node, 16)
            with pool.Fori(0, most // 2 + 1) as p:
                with pool.Fori(0, NG // 4) as i:
                    g = pool.snap(p * NG + i * 4)
                    for k in range(4):
                        pool.wait_ge(s_idx3, g + k + 1)
                        pool.wait_ge(s_t3, g + k + 1)
                        pool.sem_inc(s_mark, 1)
                        for t in range(4):
                            pool.indirect_dma_start(out=G3[:, k, t, 0:D], out_offset=None, in_=node_table,
                                                    in_offset=bass.IndirectOffsetOnAxis(ap=IDX3[:, k, t:t + 1], axis=0)).then_inc(s_in3[k], 16)

        @block.tensor
        def _(pe):
            pe.wait_ge(s_const, NCONST)
            for a, arr in enumerate(ROWS):
                pe.wait_ge(s_rowready, a + 1)
                if a >= 2:
                    pe.wait_ge(s_rowout, a - 1)
                for j in range(8):
                    b, t = j // 2, j % 2
                    bank = 2 * (a % 2) + j // 4
                    last = nc.tensor.transpose(psum[:, bank, (j % 4) * RP:(j % 4 + 1) * RP],
                                               arr[0:RP, b * HE + t:(b + 1) * HE:2], ident[0:RP, 0:RP])
                last.then_inc(s_rowt, 1)
            pe.wait_ge(s_statready, 1)
            for k in range(2):
                nc.tensor.matmul(psum[0:1, 4, k * RP:(k + 1) * RP], lhsT=small[0:RP, 22 + k:23 + k], rhs=ident[0:RP, 0:RP], start=True, stop=True)
                nc.tensor.matmul(psum[0:1, 6, k * RP:(k + 1) * RP], lhsT=small[0:RP, 12 + k:13 + k], rhs=ident[0:RP, 0:RP], start=True, stop=True)
            for b in range(4):
                last = nc.tensor.matmul(psum[0:1, 5, b * RP:(b + 1) * RP], lhsT=small[0:RP, b:b + 1], rhs=ident[0:RP, 0:RP], start=True, stop=True)
            last.then_inc(s_statrow, 1)
            pe.wait_ge(s_passes, 1)
            most = pe.value_load(passes[0:1, 0:1], min_val=0, max_val=N)
            pe.sem_inc(s_used, RING // 2)
            pe_base = [pe.alloc_register(f"pe_base{k}") for k in range(BATCH)]
            with pe.Fori(0, most // WIN + 1) as p:
                with pe.Fori(0, NH // UNR) as i:
                    g = pe.snap(p * NH + i * UNR)
                    e = pe.snap((p * NH + i * UNR) * 2)
                    for k in range(UNR):
                        pe.wait_ge(s_oh, g + k + 2)
                        pe.wait_ge(s_land, e + (2 * k + 2))
                        for h, (q0, q1) in enumerate(HALF):
                            for t in range(2):
                                last = nc.tensor.matmul(psum[:, 4 + 2 * (k % 2) + h, 0:(q1 - q0) * WIN], lhsT=OHR[:, (2 * k + t) % RING, :],
                                                        rhs=OHQ[:, (2 * k + t) % RING, q0 * WIN:q1 * WIN], start=(t == 0), stop=False)
                            if h:
                                last.then_inc(s_used, 1)
                            elif k % BATCH == 0:
                                pe.load(pe_base, base_row[0:1, bass.ds(i * UNR + k, BATCH)])
                            b = pe.snap(pe_base[k % BATCH], min_val=0, max_val=LASTBASE)
                            pe.wait_ge(s_land, e + (2 * k + 3 + h))
                            nc.tensor.matmul(psum[:, 4 + 2 * (k % 2) + h, 0:(q1 - q0) * WIN], lhsT=identh2[:, :],
                                             rhs=adj3[:, q0:q1, bass.ds(b, WIN)], start=False, stop=True).then_inc(s_built, 1)

            def transpose_pairs(turn, n, q, m0, c):
                ring = len(PAIRS[turn])
                if n >= ring:
                    pe.wait_ge(s_tx, turn * len(CH) + n - ring + 1)
                    pe.wait_ge(s_ty, turn * LOWER[-1] + LOWER[n - ring])
                bank = PAIRS[turn][n % ring]
                for j in range(c):
                    last = nc.tensor.transpose(psum_h[:, bank, j * P:(j + 1) * P], adj_blk[:, q, m0 + j, :], identh[:, :])
                for j in range(c):
                    if m0 + j > q:
                        last = nc.tensor.transpose(psum_h[:, bank + 1, j * P:(j + 1) * P], adj_blk[:, m0 + j, q, :], identh[:, :])
                last.then_inc(s_tp, 1)

            def degrees(m0, m1):
                for m in range(m0, m1):
                    for q in range(NT):
                        last = nc.tensor.matmul(psum[:, 0, m:m + 1], lhsT=adj_blk[:, q, m, :], rhs=onesh[:, 0:1], start=(q == 0), stop=(q == NT - 1))
                if m1 == NT:
                    last.then_inc(s_deg, 1)

            def propagate(parts, before):
                for b, (m0, m1) in enumerate(BANKS):
                    if b > 5:
                        pe.wait_ge(s_bank, before + (b - 4))
                    elif 0 < b < 4 and not (isinstance(before, int) and before == 0):
                        pe.wait_ge(s_bank, before + (b - 3))
                    if b == 0:
                        for c, (q0, q1) in enumerate(BANKS):
                            pe.wait_ge(s_xp, before + (c + 1))
                            for q in range(q0, q1):
                                for m in range(TPB):
                                    last = nc.tensor.matmul(psum[:, m, 0:PART], lhsT=adj_blk[:, q, m, :], rhs=parts[:, q, :, :],
                                                            start=(q == 0), stop=(q == NT - 1))
                    else:
                        for m in range(m0, m1):
                            for q in range(NT):
                                last = nc.tensor.matmul(psum[:, 3 + (b - 1) % 5, (m - m0) * PART:(m - m0 + 1) * PART], lhsT=adj_blk[:, q, m, :],
                                                        rhs=parts[:, q, :, :], start=(q == 0), stop=(q == NT - 1))
                    last.then_inc(s_prop, 1)

            pe.wait_ge(s_adj, 1)
            for n, chunk in enumerate(CH):
                transpose_pairs(0, n, *chunk)
            pe.wait_ge(s_tx, len(CH))
            pe.wait_ge(s_ty, LOWER[-1])
            degrees(0, NT)
            pe.wait_ge(s_degread, 1)
            for n in range(2):
                propagate(XP[n], n * NB)
            pe.wait_ge(s_bank, 2 * NB)
            def features(c, src, ready, bank):
                m0, m1 = HCH[c]
                for j in range(m1 - m0):
                    last = nc.tensor.transpose(psum[0:D, bank, j * P:(j + 1) * P], src[:, m0 + j, :], ident[:, :])
                last.then_inc(ready, 1)

            pe.wait_ge(s_w, 16 * 6)
            pe.wait_ge(s_h, 1)
            features(0, H, s_ht, 1)
            for c, (m0, m1) in enumerate(HCH):
                w = (m1 - m0) * P
                pe.wait_ge(s_htc, c + 1)
                for r in range(4):
                    nc.tensor.matmul(psum[:, 2 + r, 0:w], lhsT=W1R[:, r, :], rhs=HT[:, c % 2, 0:w], start=True, stop=True).then_inc(s_h1, 1)
                if c + 1 < len(HCH):
                    features(c + 1, H, s_ht, 1)
                pe.wait_ge(s_h1r, 4 * c + 4)
                for j in range(m1 - m0):
                    q = m0 + j
                    if q >= 2:
                        pe.wait_ge(s_h2c, q - 1)
                    for r in range(4):
                        last = nc.tensor.matmul(psum[:, 6 + q % 2, r * 96:(r + 1) * 96], lhsT=H1T[:, r, j * P:(j + 1) * P], rhs=W2R[:, r, :], start=True, stop=True)
                    last.then_inc(s_h2, 1)
            pe.wait_ge(s_h2c, NT)
            pe.sem_inc(s_seg, 4)

            def segments(k, g):
                pe.wait_ge(s_woh, g + (k + 1))
                pe.wait_ge(s_acc, g + (k + 1))
                for t in range(4):
                    for j in range(3):
                        last = nc.tensor.matmul(psum[:, 4 + k % 2, 0:D], lhsT=OH1[:, k % 2, t, :],
                                                rhs=GP[:, k % 2, t, j, :], start=(t == 0 and j == 0), stop=(t == 3 and j == 2))
                last.then_inc(s_seg, 1)

            for j in range(PEEL):
                if j < PEEL - 4:
                    for n in range(BEFORE[j], BEFORE[j + 1]):
                        transpose_pairs(1, n, *CH[n])
                else:
                    pe.wait_ge(s_tx, 2 * len(CH))
                    pe.wait_ge(s_ty, 2 * LOWER[-1])
                    degrees((j - PEEL + 4) * NT // 4, (j - PEEL + 5) * NT // 4)
                if j:
                    segments((j - 1) % 4, (j - 1) // 4 * 4)
            segments(3, PEEL - 4)
            pe.wait_ge(s_coef, 1)
            nc.tensor.matmul(psum[:, 7, 0:K + 1], lhsT=ones[0:1, :], rhs=small[0:1, 32:32 + K + 1], start=True, stop=True).then_inc(s_coefb, 1)
            most = pe.value_load(passes[0:1, 1:2], min_val=0, max_val=BLANK)
            with pe.Fori(PEEL // 4, NG // 4) as i:
                for k in range(4):
                    segments(k, pe.snap(i * 4))
            with pe.If(most > 1):
                with pe.Fori(0, most // 2) as p:
                    with pe.Fori(0, NG // 4) as i:
                        g = pe.snap(p * NG + i * 4 + NG)
                        for k in range(4):
                            segments(k, g)
            with pe.Fori(0, K // 2) as i:
                for u in range(2):
                    propagate(XP[u], pe.snap(i * (2 * NB) + (2 + u) * NB))
            def codes_t():
                for j in range(7):
                    last = nc.tensor.transpose(psum[0:NC // 7, 2 * (j // 4), (j % 4) * P:(j % 4 + 1) * P], CLAMP[:, j * (NC // 7):(j + 1) * (NC // 7)], ident[:, :])
                last.then_inc(s_relt, 1)

            pe.wait_ge(s_clamp, 1)
            codes_t()
            pe.sem_inc(s_t3, 4)
            pe.wait_ge(s_h, 2)
            for c in range(len(HCH)):
                if c >= 2:
                    pe.wait_ge(s_htc3, c - 1)
                features(c, H3, s_ht3, 1 + 2 * (c % 2))
            pe.wait_ge(s_w3in, 16 * 8)
            pe.wait_ge(s_reltc, 1)
            pe.wait_ge(s_htc3, len(HCH))
            for c, (w0, w1) in enumerate(WCH):
                if c >= 4:
                    pe.wait_ge(s_pdc, c - 3)
                for j in range(w1 - w0):
                    last = nc.tensor.matmul(psum[:, 2 + c % 4, j * HID:(j + 1) * HID], lhsT=HT3[0:D, (w0 + j) * HP:(w0 + j) * HP + P], rhs=W1B[0:D, :], start=True, stop=True)
                last.then_inc(s_pd, 1)
            pe.wait_ge(s_pdc, len(WCH))
            tile = [pe.alloc_register(f"pe_tile{k}") for k in range(4)]
            pe.sem_inc(s_z1, 2)
            pe.sem_inc(s_z2, 2)
            pe.sem_inc(s_w3, 2)
            pe.sem_inc(s_seg3, 2)

            def inputs_t(k, n, used):
                pe.wait_ge(s_ef[k], used)
                pe.wait_ge(s_in3[k], used * 2)
                pe.wait_ge(s_gt, n + 1)
                pe.sem_inc(s_mark, 1)
                for t in range(4):
                    last = nc.tensor.transpose(psum[0:64, 4, t * P:(t + 1) * P], G3[:, k, t, :], ident[:, :])
                last.then_inc(s_t3, 1)

            def layer1(k, n, window):
                pe.wait_ge(s_gt, n + 2)
                pe.wait_ge(s_r1, n + 1)
                nc.tensor.matmul(psum[:, k % 2, :], lhsT=W1AC[0:64, :], rhs=GT[0:64, k % 2, :], start=True, stop=False)
                pe.wait_ge(s_oht, n + 5)
                for c in range(3):
                    last = nc.tensor.matmul(psum[:, k % 2, :], lhsT=PD[:, bass.ds(window * (3 * HID) + c * HID, HID)],
                                            rhs=OHT[:, k % 2, :], start=False, stop=(c == 2))
                last.then_inc(s_z1, 1)

            def layer2(k, n):
                pe.wait_ge(s_r1, n + 3)
                pe.wait_ge(s_r2, n + 1)
                nc.tensor.matmul(psum[:, 2 + k % 2, :], lhsT=W2M, rhs=R1[:, k % 2, :], start=True, stop=True).then_inc(s_z2, 1)

            def layer3(k, n):
                pe.wait_ge(s_r2, n + 3)
                pe.wait_ge(s_msg, n + 1)
                for t in range(4):
                    last = nc.tensor.matmul(psum[:, 5, t * D:(t + 1) * D], lhsT=R2[:, k % 2, t * P:(t + 1) * P], rhs=W3M, start=True, stop=True)
                last.then_inc(s_w3, 1)

            def sums(k, n):
                pe.wait_ge(s_ohf, n + 1)
                pe.wait_ge(s_msg, n + 2)
                pe.wait_ge(s_acc3, n + 1)
                for t in range(4):
                    last = nc.tensor.matmul(psum[:, 6 + k % 2, 0:PART], lhsT=OHF[:, k % 2, t, :],
                                            rhs=MS[:, k % 2, t, :, :], start=(t == 0), stop=(t == 3))
                last.then_inc(s_seg3, 1)

            def mlp(i, n, used, first=False, last=False):
                at = slice(2 + i * 4, 6 + i * 4) if isinstance(i, int) else bass.ds(i * 4 + 2, 4)
                pe.load(tile, TILE3[0:1, at])
                for k in range(4):
                    layer1(k, n + k, pe.snap(tile[k], min_val=0, max_val=BLANK))
                    if not (last and k == 3):
                        inputs_t((k + 1) % 4, n + (k + 1), used + (32 if k < 3 else 64))
                    if not (first and k == 0):
                        layer3(k - 1, n + (k - 1))
                    if not (first and k < 2):
                        sums(k - 2, n + (k - 2))
                    layer2(k, n + k)

            with pe.Fori(0, most // 2 + 1) as p:
                pe.wait_ge(s_shift3, p * 3 + 2)
                inputs_t(0, pe.snap(p * NG), pe.snap(p * (32 * NG // 4) + 32))
                mlp(0, pe.snap(p * NG), pe.snap(p * (32 * NG // 4)), first=True)
                with pe.Fori(1, NG // 4 - 1) as i:
                    mlp(i, pe.snap(p * NG + i * 4), pe.snap(p * (32 * NG // 4) + i * 32))
                mlp(NG // 4 - 1, pe.snap(p * NG + (NG - 4)), pe.snap(p * (32 * NG // 4) + 32 * (NG // 4 - 1)), last=True)
                layer3(3, pe.snap(p * NG + (NG - 1)))
                sums(2, pe.snap(p * NG + (NG - 2)))
                sums(3, pe.snap(p * NG + (NG - 1)))
                pe.wait_ge(s_clamp, p + 2)
                pe.sem_inc(s_mark, 1)
                codes_t()
                pe.wait_ge(s_reltc, p + 2)
                pe.sem_inc(s_mark, 1)

        @block.scalar
        def _(act):
            for a, dest in enumerate(COLS):
                act.wait_ge(s_rowt, a + 1)
                for hf in range(2):
                    last = nc.scalar.activation(dest.rearrange("p (c j) -> p j c", j=8)[:, 4 * hf:4 * hf + 4, :],
                                                psum[:, 2 * (a % 2) + hf, 0:4 * RP].rearrange("p (j c) -> p j c", j=4), ACT.Copy)
                last.then_inc(s_rowout, 1)
            act.wait_ge(s_passes, 1)
            most = act.value_load(passes[0:1, 0:1], min_val=0, max_val=N)
            act.sem_inc(s_land, 4)
            act_base = [act.alloc_register(f"act_base{k}") for k in range(BATCH)]
            with act.Fori(0, most // WIN + 1) as p:
                with act.Fori(0, NH // UNR) as i:
                    e = act.snap((p * NH + i * UNR) * 2)
                    act.wait_ge(s_oh, act.snap(p * NH + i * UNR) + 2)
                    for k in range(UNR):
                        if k % BATCH == 0:
                            act.load(act_base, base_row[0:1, bass.ds(i * UNR + k, BATCH)])
                        b = act.snap(act_base[k % BATCH], min_val=0, max_val=LASTBASE)
                        for h, (q0, q1) in enumerate(HALF):
                            act.wait_ge(s_built, e + (2 * k + h + 1))
                            nc.scalar.activation(adj3[:, q0:q1, bass.ds(b, WIN)],
                                                 psum[:, 4 + 2 * (k % 2) + h, 0:(q1 - q0) * WIN].rearrange("p (q c) -> p q c", c=WIN),
                                                 ACT.Copy, scale=0.5).then_inc(s_land, 1)

            def lower_blocks(turn, n, q, m0, c):
                lo = max(m0, q + 1)
                if m0 + c > lo:
                    act.wait_ge(s_tp, turn * len(CH) + n + 1)
                    nc.scalar.activation(adj_blk[:, q, lo:m0 + c, :],
                                         psum_h[:, PAIRS[turn][n % len(PAIRS[turn])] + 1, (lo - m0) * P:c * P].rearrange("p (j r) -> p j r", r=P),
                                         ACT.Copy).then_inc(s_ty, 1)

            def root(n):
                act.wait_ge(s_var, n + 1)
                nc.scalar.activation(st(4), st(3), ACT.Sqrt).then_inc(s_root, 1)

            for n, chunk in enumerate(CH):
                lower_blocks(0, n, *chunk)
            for n in range(3):
                root(n)
            act.wait_ge(s_w, 16 * 6)
            for c, (m0, m1) in enumerate(HCH):
                w = (m1 - m0) * P
                if c:
                    act.wait_ge(s_h2, m0)
                for r in range(4):
                    act.wait_ge(s_h1, 4 * c + r + 1)
                    nc.scalar.activation(H1T[:, r, 0:w], psum[:, 2 + r, 0:w], ACT.Relu, bias=B1R).then_inc(s_h1r, 1)
            act.wait_ge(s_loop1, 1)

            def stage1(k, c, g):
                act.wait_ge(s_seg, g + (k + 1))
                nc.scalar.copy(IDX[:, k, :], idx_msg[:, cut(c + 4 * k, 4)]).then_inc(s_idx, 1)

            for k in range(4):
                stage1(k, 0, 0)
            for j in range(PEEL - 4):
                for n in range(BEFORE[j], BEFORE[j + 1]):
                    lower_blocks(1, n, *CH[n])
                stage1(j % 4, 16 * (j // 4 + 1), j // 4 * 4 + 4)
            act.wait_ge(s_lapin, 32)
            nc.scalar.activation(small[0:1, 0:K + 1], small[0:1, 0:K + 1], ACT.Tanh).then_inc(s_lap, 1)
            most = act.value_load(passes[0:1, 1:2], min_val=0, max_val=BLANK)
            with act.Fori(PEEL // 4, NG // 4) as i:
                for k in range(4):
                    stage1(k, i * 16, act.snap(i * 4))
            with act.If(most > 1):
                with act.Fori(0, most // 2) as p:
                    with act.Fori(0, NG // 4) as i:
                        g = act.snap(p * NG + i * 4 + NG)
                        for k in range(4):
                            stage1(k, i * 16, g)
            root(3)
            root(4)
            def codes_out():
                for j in range(2):
                    w = (4, 3)[j]
                    last = nc.scalar.activation(RELT[0:NC // 7, 4 * j:4 * j + w, :], psum[0:NC // 7, 2 * j, 0:w * P].rearrange("p (j c) -> p j c", j=w), ACT.Copy)
                last.then_inc(s_reltc, 1)

            def stage(g, k, n):
                act.wait_ge(s_t3, n + 1)
                nc.scalar.copy(IDX3[:, k, :], idx_src[:, g]).then_inc(s_idx3, 1)

            act.wait_ge(s_relt, 1)
            codes_out()
            for k in range(4):
                stage(slice(4 * k, 4 * k + 4), k, k)
            root(5)

            def part(c, j, src, done):
                w0, w1 = WCH[c]
                nc.scalar.activation(PD[:, w0 * 3 * HID:w1 * 3 * HID].rearrange("p (q j f) -> p q j f", j=3, f=HID)[:, :, j, :],
                                     src[:, 0:(w1 - w0) * HID].rearrange("p (q f) -> p q f", f=HID), ACT.Copy).then_inc(done, 1)

            for c in range(len(WCH) + 1):
                if c < len(WCH):
                    act.wait_ge(s_pd, c + 1)
                    part(c, 0, psum[:, 2 + c % 4, :], s_pdhi)
                if c:
                    act.wait_ge(s_pdr, c)
                    part(c - 1, 1, PDR[:, (c - 1) % 2, :], s_pdmid)
            act.sem_inc(s_gt, 1)
            act.sem_inc(s_r1, 2)
            act.sem_inc(s_r2, 2)
            act.wait_ge(s_w3in, 16 * 8)

            def inputs_out(k, n):
                act.wait_ge(s_t3, n + 5)
                act.wait_ge(s_z1, n + 1)
                nc.scalar.activation(GT[0:64, k % 2, :], psum[0:64, 4, :], ACT.Copy).then_inc(s_gt, 1)

            def mlp(i, n, last=False):
                for k in range(4):
                    act.wait_ge(s_z1, n + (k + 3))
                    act.wait_ge(s_z2, n + (k + 1))
                    nc.scalar.activation(R1[:, k % 2, :], psum[:, k % 2, :], ACT.Relu, bias=BM[:, 0:1]).then_inc(s_r1, 1)
                    if not (last and k == 3):
                        inputs_out(k + 1, n + (k + 1))
                    if not last:
                        stage(bass.ds(i * 16 + (4 * k + 16), 4), k, n + (k + 4))
                    act.wait_ge(s_z2, n + (k + 3))
                    act.wait_ge(s_w3, n + (k + 1))
                    nc.scalar.activation(R2[:, k % 2, :], psum[:, 2 + k % 2, :], ACT.Relu, bias=BM[:, 1:2]).then_inc(s_r2, 1)

            with act.Fori(0, most // 2 + 1) as p:
                inputs_out(0, act.snap(p * NG))
                with act.Fori(0, NG // 4 - 1) as i:
                    mlp(i, act.snap(p * NG + i * 4))
                mlp(NG // 4 - 1, act.snap(p * NG + (NG - 4)), last=True)
                act.wait_ge(s_relt, p + 2)
                act.sem_inc(s_mark, 1)
                codes_out()
                for k in range(4):
                    stage(slice(4 * k, 4 * k + 4), k, act.snap(p * NG + (NG + k)))

        @block.vector
        def _(dve):
            V = Count(dve, v_seq)
            vec = nc.vector
            tail = slice((RP - 1) // 32 * 32, RP)
            for dst, fill in ((dst_i, -1), (src_i, 0), (typ_i, 0), (nrm_f, 0.0)):
                vec.memset(dst[tail, RREM:RE], fill).then_inc(s_fill, 1)
            vec.memset(x3[:, NT - 1, :], 0.0).then_inc(s_fill, 1)
            vec.memset(adj_f[:, 0:ZERO0], 0.0).then_inc(s_zero, 1)
            dve.wait_ge(s_in, 16 * 8)
            dve.wait_ge(s_const, NCONST)
            t_ai, t_bi = t_a.bitcast(I32), t_b.bitcast(I32)
            v4 = lambda a: a.rearrange("p (b c) -> p b c", b=4)
            v2 = lambda a: a.rearrange("p (b c) -> p b c", b=2)
            V.do(vec.tensor_copy(dst_f, dst_i))
            V.do(vec.tensor_scalar(t_a, dst_f, 0.0, BIG, ALU.is_lt, ALU.mult))
            V.do(vec.tensor_tensor(t_a, t_a, dst_f, ALU.add))
            V.did(vec.tensor_reduce(small[0:RP, 4:8], v4(dst_f), AX.X, ALU.max))
            V.do(vec.tensor_reduce(small[0:RP, 24:28], v4(t_a), AX.X, ALU.min))
            V.do(vec.tensor_scalar(small[0:RP, 0:4], small[0:RP, 24:28], float(N - 1), None, ALU.min))
            V.did(vec.tensor_reduce(small[0:RP, 8:10], small[0:RP, 0:4].rearrange("p (a b) -> p a b", b=2), AX.X, ALU.min))
            V.do(vec.tensor_reduce(small[0:RP, 10:12], small[0:RP, 4:8].rearrange("p (a b) -> p a b", b=2), AX.X, ALU.max))
            V.do(vec.tensor_copy(smi[0:RP, 0:4], small[0:RP, 8:12]))
            V.do(vec.tensor_scalar(smi[0:RP, 4:8], smi[0:RP, 0:4], 6, None, ALU.arith_shift_right))
            V.do(vec.tensor_copy(small[0:RP, 12:16], smi[0:RP, 4:8]))
            V.did(vec.tensor_tensor(small[0:RP, 16:18], small[0:RP, 14:16], small[0:RP, 12:14], ALU.subtract))
            V.do(vec.tensor_tensor(small[0:RP, 18:22], small[0:RP, 4:8], small[0:RP, 0:4], ALU.subtract))
            V.did(vec.tensor_reduce(small[0:RP, 22:23], small[0:RP, 18:22], AX.X, ALU.max))
            V.do(vec.tensor_reduce(small[0:RP, 23:24], small[0:RP, 16:18], AX.X, ALU.max))
            vec.tensor_scalar(small[0:RP, 28:30], small[0:RP, 12:14], float(HP), None, ALU.mult).then_inc(s_statready, 1)
            dve.wait_ge(s_statready, 1)
            vec.tensor_tensor(v4(t_b), v4(dst_f), bc(small[0:RP, 0:4], HE), ALU.subtract).then_inc(s_rowready, 1)
            V.did(vec.tensor_scalar(t_ai, src_i, 7, None, ALU.arith_shift_right))
            V.all()
            vec.tensor_scalar(t_c, t_ai, float(QS), None, ALU.mult).then_inc(s_rowready, 1)
            dve.wait_ge(s_rowready, 2)
            V.do(vec.tensor_scalar(t_ai, src_i, P - 1, None, ALU.bitwise_and))
            dve.wait_ge(s_rowt, 1)
            vec.tensor_copy(t_b, t_ai).then_inc(s_rowready, 1)
            dve.wait_ge(s_rowt, 2)
            vec.tensor_tensor(v2(t_c), v2(dst_f), bc(small[0:RP, 28:30], 2 * HE), ALU.subtract).then_inc(s_rowready, 1)
            dve.wait_ge(s_rowt, 3)
            vec.scalar_tensor_tensor(t_b, src_i, float(REL), typ_i, ALU.mult, ALU.add).then_inc(s_rowready, 1)
            dve.wait_ge(s_rowt, 4)
            V.did(vec.tensor_copy(t_c, src_i))
            V.all()
            dve.sem_inc(s_rowready, 2)
            vec.memset(adj_f[:, ROW0:ROW0 + 3 * RE], 0.0).then_inc(s_zero, 1)
            dve.wait_ge(s_statrow, 1)
            V.did(vec.tensor_reduce(small[0:1, 32:34], psum[0:1, 4, 0:2 * RP].rearrange("p (a b) -> p a b", b=RP), AX.X, ALU.max))
            V.did(vec.tensor_copy(base_row[0:1, :].rearrange("o (c b) -> o b c", b=4), psum[0:1, 5, 0:4 * RP].rearrange("o (b c) -> o b c", c=RP)))
            V.did(vec.tensor_copy(tile_row[0:1, :].rearrange("o (c b) -> o b c", b=2), psum[0:1, 6, 0:2 * RP].rearrange("o (b c) -> o b c", c=RP)))
            V.all()
            V.do(vec.tensor_scalar(small[0:1, 34:36], small[0:1, 32:34], 0.0, None, ALU.max))
            vec.tensor_copy(passes[0:1, :], small[0:1, 34:36]).then_inc(s_passes, 1)
            dve.wait_ge(s_passes, 1)
            dve.wait_ge(s_rowout, 7)
            dve.wait_ge(s_zero, 6)
            for s in (s_code, s_oh, s_msg):
                dve.sem_inc(s, 1)
            most = dve.value_load(passes[0:1, 0:1], min_val=0, max_val=N)
            base = [dve.alloc_register(f"base{k}") for k in range(4)]
            with dve.Fori(0, most // WIN + 1) as p:
                c0 = dve.snap(p * 4)
                dve.wait_ge(s_code, c0 + 1)
                vec.tensor_scalar(code_c, rel_a, -1.0, float(WIN), ALU.max, ALU.min).then_inc(s_code, 1)
                dve.wait_ge(s_code, c0 + 2)
                vec.tensor_tensor(code_c, code_c, q_c, ALU.add).then_inc(s_code, 1)
                vec.tensor_scalar(rel_a, rel_a, float(WIN), None, ALU.subtract).then_inc(s_code, 1)
                dve.wait_ge(s_code, c0 + 4)
                dve.sem_inc(s_mark, 1)
                with dve.Fori(0, NH // UNR) as i:
                    g = dve.snap(p * NH + i * UNR)
                    for k in range(UNR):
                        dve.wait_ge(s_used, g + k + 1)
                        for t in range(2):
                            vec.tensor_scalar(OHQ[:, (2 * k + t) % RING, :], iota_code[:, :], code_c[:, bass.ds(i * (2 * UNR) + (2 * k + t), 1)], None, ALU.is_equal)
                        for t in range(2):
                            last = vec.tensor_scalar(OHR[:, (2 * k + t) % RING, :], iota_256[:, 0:P], r_c[:, bass.ds(i * (2 * UNR) + (2 * k + t), 1)], None, ALU.is_equal)
                        last.then_inc(s_oh, 1)
                dve.wait_ge(s_land, p * (2 * NH) + (2 * NH + 4))
                vec.tensor_scalar(base_row[0:1, :], base_row[0:1, :], float(WIN), float(LASTBASE), ALU.add, ALU.min).then_inc(s_code, 1)
                dve.wait_ge(s_code, c0 + 5)
            dve.sem_inc(s_adj, 1)

            def upper_blocks(turn, n, q, m0, c):
                dve.wait_ge(s_tp, turn * len(CH) + n + 1)
                vec.tensor_copy(adj_blk[:, m0:m0 + c, q, :],
                                psum_h[:, PAIRS[turn][n % len(PAIRS[turn])], 0:c * P].rearrange("p (j r) -> p j r", r=P)).then_inc(s_tx, 1)

            roots = [0]

            def inv_root(out):
                dve.sem_inc(s_var, 1)
                roots[0] += 1
                dve.wait_ge(s_root, roots[0])
                V.do(vec.reciprocal(st(5), st(4)))
                V.do(vec.tensor_tensor(st(6), st(5), st(5), ALU.mult))
                V.do(vec.tensor_tensor(st(6), st(6), st(3), ALU.mult))
                V.do(vec.tensor_scalar(st(6), st(6), -0.5, 1.5, ALU.mult, ALU.add))
                V.do(vec.tensor_tensor(out, st(5), st(6), ALU.mult))

            def layernorm(h, t):
                V.do(vec.tensor_reduce(st(0), x3, AX.X, ALU.add))
                V.do(vec.tensor_scalar(st(1), st(0), 1.0 / D, None, ALU.mult))
                V.do(vec.tensor_tensor(h, x3, bc(st(1)), ALU.subtract))
                V.do(vec.tensor_tensor(t, h, h, ALU.mult))
                V.do(vec.tensor_reduce(st(2), t, AX.X, ALU.add))
                V.do(vec.tensor_scalar(st(3), st(2), 1.0 / D, 1e-5, ALU.mult, ALU.add))
                inv_root(st(7))
                V.do(vec.scalar_tensor_tensor(h, h, 0.0, bc(st(7)), ALU.max, ALU.mult))

            def bank_of(b):
                if b == 0:
                    return psum[:, 0:TPB, 0:PART].rearrange("p m (c f) -> p m f c", c=3)
                return psum[:, 3 + (b - 1) % 5, 0:(BANKS[b][1] - BANKS[b][0]) * PART].rearrange("p (m c f) -> p m f c", c=3, f=D)

            def split(parts, z, r, m0, m1):
                X = parts[:, m0:m1, :, :]
                V.do(vec.tensor_copy(X[:, :, 0, :], z))
                V.do(vec.tensor_tensor(r, z, X[:, :, 0, :], ALU.subtract))
                V.do(vec.tensor_copy(X[:, :, 1, :], r))
                V.do(vec.tensor_tensor(X[:, :, 2, :], r, X[:, :, 1, :], ALU.subtract))

            for n, chunk in enumerate(CH):
                upper_blocks(0, n, *chunk)
            dve.wait_ge(s_x, 32)
            V.all()
            layernorm(PA, PB)
            dve.wait_ge(s_deg, 1)
            vec.tensor_scalar(st(3), psum[:, 0, 0:NT], 2.0, 1.0, ALU.mult, ALU.add).then_inc(s_degread, 1)
            dve.wait_ge(s_degread, 1)
            inv_root(st(8))
            V.do(vec.tensor_tensor(PA, PA, bc(st(8)), ALU.mult))
            for b in range(0, NB, 3):
                m0, m1 = BANKS[b][0], BANKS[b + 2][1]
                split(XP[0], PA[:, m0:m1, :], PB[:, m0:m1, :], m0, m1)
                dve.sem_inc(s_xp, 3)
            for n in range(2):
                for b, (m0, m1) in enumerate(BANKS):
                    w = m1 - m0
                    z, y, r = PA[:, m0:m1, :], TY[:, 0:w, :], TR[:, 0:w, :]
                    dve.wait_ge(s_prop, n * NB + b + 1)
                    vec.tensor_reduce(y, bank_of(b), AX.X, ALU.add).then_inc(s_bank, 1)
                    dve.wait_ge(s_bank, n * NB + b + 1)
                    V.do(vec.scalar_tensor_tensor(y, y, 2.0, z, ALU.mult, ALU.add))
                    V.do(vec.tensor_tensor(y, y, bc(st(8)[:, m0:m1]), ALU.mult))
                    if n == 0:
                        V.do(vec.tensor_tensor(z, y, bc(st(8)[:, m0:m1]), ALU.mult))
                        split(XP[1], z, r, m0, m1)
                        dve.sem_inc(s_xp, 1)
                    else:
                        V.do(vec.tensor_tensor(x3[:, m0:m1, :], x3[:, m0:m1, :], y, ALU.add))
            V.all()
            V.did(vec.memset(W1R, 0.0))
            V.did(vec.memset(B1R, 0.0))
            V.do(vec.memset(W2R, 0.0))
            dve.sem_inc(s_wz, 1)
            layernorm(H, LNT)
            dve.sem_inc(s_h, 1)

            def features_out(c, dest, ready, done):
                dve.wait_ge(ready, c + 1)
                w = (HCH[c][1] - HCH[c][0]) * P
                vec.tensor_copy(dest[0:D, c % 2, 0:w], psum[0:D, 1, 0:w]).then_inc(done, 1)

            features_out(0, HT, s_ht, s_htc)
            for c, (m0, m1) in enumerate(HCH):
                if c + 1 < len(HCH):
                    features_out(c + 1, HT, s_ht, s_htc)
                for q in range(m0, m1):
                    dve.wait_ge(s_h2, q + 1)
                    if q >= 2:
                        dve.wait_ge(s_tab[q % 2], 16 * (q // 2))
                    vec.tensor_copy(H2[:, q % 2, :], psum[:, 6 + q % 2, 0:384]).then_inc(s_h2c, 1)
            dve.sem_inc(s_loop1, 1)
            dve.wait_ge(s_tab[0], 16 * ((NT + 1) // 2))
            dve.wait_ge(s_tab[1], 16 * (NT // 2))
            V.do(vec.memset(ACC, 0.0))
            dve.wait_ge(s_w, 16 * 7)
            V.did(vec.tensor_copy(ACC[:, 0:2 * NT * D].rearrange("p (q w f) -> p q w f", w=2, f=D)[:, :, 0, :], B2R.unsqueeze(1).broadcast_to((P, NT, D))))
            V.did(vec.tensor_copy(REL1, rel_b[:, :]))
            V.do(vec.tensor_copy(TILE1, tile_row[0:1, :]))
            dve.sem_inc(s_acc, 2)

            def message1(k, c, g, m, used):
                dve.wait_ge(s_seg, g + (k + 3))
                for t in range(4):
                    vec.tensor_scalar(OH1[:, k % 2, t, :], iota_256[:, 0:P], REL1[:, cut(c + (4 * k + t), 1)], None, ALU.is_equal)
                dve.wait_ge(s_gath[k], used)
                parts = GP[:, k % 2, :, :, :]
                vec.tensor_tensor(WM, GM[:, k, :].rearrange("p (t f) -> p t f", t=4), bc(norm_c[:, cut(c + 4 * k, 4)]), ALU.mult).then_inc(v_msg, 1)
                dve.wait_ge(v_msg, m + (5 * k + 1))
                vec.tensor_copy(parts[:, :, 0, :], WM).then_inc(v_msg, 1)
                dve.wait_ge(v_msg, m + (5 * k + 2))
                vec.tensor_tensor(WMR, WM, parts[:, :, 0, :], ALU.subtract).then_inc(v_msg, 1)
                dve.wait_ge(v_msg, m + (5 * k + 3))
                vec.tensor_copy(parts[:, :, 1, :], WMR).then_inc(v_msg, 1)
                dve.wait_ge(v_msg, m + (5 * k + 4))
                vec.tensor_tensor(parts[:, :, 2, :], WMR, parts[:, :, 1, :], ALU.subtract).then_inc(v_msg, 1)
                dve.wait_ge(v_msg, m + (5 * k + 5))
                dve.sem_inc(s_woh, 1)

            def add1(k, g):
                dve.wait_ge(s_seg, g + (k + 5))
                dve.wait_ge(s_acc, g + (k + 2))
                at = ACC[:, bass.ds(dve.snap(base[k], min_val=0, max_val=BLANK) * D, D)]
                vec.tensor_tensor(at, at, psum[:, 4 + k % 2, 0:D], ALU.add).then_inc(s_acc, 1)

            for j in range(PEEL):
                k, g = j % 4, j // 4 * 4
                if j < PEEL - 4:
                    for n in range(BEFORE[j], BEFORE[j + 1]):
                        upper_blocks(1, n, *CH[n])
                message1(k, 4 * g, g, 5 * g, (j // 4 + 1) * 64)
                if k == 1:
                    dve.load(base, TILE1[0:1, g:g + 4])
                if j:
                    add1((j - 1) % 4, (j - 1) // 4 * 4)
            add1(3, PEEL - 4)
            dve.wait_ge(s_lap, 1)
            dve.wait_ge(s_const, NCONST + 3 * K + 1)
            sm = lambda a, b: small[0:1, a:b]
            for n in range(1, K):
                V.do(vec.tensor_tensor(sm(n, n + 1), sm(n, n + 1), sm(n - 1, n), ALU.mult))
            V.do(vec.tensor_tensor(sm(32, 33 + K), sm(16, 17 + K), rec[0:1, 2 * K:3 * K + 1], ALU.mult))
            V.do(vec.tensor_tensor(sm(33, 33 + K), sm(33, 33 + K), sm(0, K), ALU.mult))
            dve.sem_inc(s_coef, 1)
            dve.wait_ge(s_coefb, 1)
            V.do(vec.tensor_copy(small[:, 48:48 + K + 1], psum[:, 7, 0:K + 1]))
            most = dve.value_load(passes[0:1, 1:2], min_val=0, max_val=BLANK)

            def groups(i, g):
                dve.load(base, TILE1[0:1, bass.ds(i * 4, 4)])
                m, used = dve.snap(g * 5), dve.snap(g * 16 + 64)
                for k in range(4):
                    message1(k, i * 16, g, m, used)
                    add1(k, g)

            with dve.Fori(PEEL // 4, NG // 4) as i:
                groups(i, dve.snap(i * 4))
            with dve.If(most > 1):
                with dve.Fori(0, most // 2) as p:
                    dve.wait_ge(s_acc, p * NG + (NG + 2))
                    vec.tensor_scalar(REL1, REL1, float(P), None, ALU.subtract).then_inc(s_shift, 1)
                    vec.tensor_scalar(TILE1, TILE1, 2.0, float(BLANK), ALU.add, ALU.min).then_inc(s_shift, 1)
                    dve.wait_ge(s_shift, p * 2 + 2)
                    dve.sem_inc(s_mark, 1)
                    with dve.Fori(0, NG // 4) as i:
                        groups(i, dve.snap(p * NG + i * 4 + NG))
            dve.wait_ge(s_acc, dve.snap(most // 2 * NG + (NG + 2)))
            dve.sem_inc(s_mark, 1)
            dve.wait_ge(s_deg, 2)
            V.do(vec.tensor_scalar(cnt_in[:, :], psum[:, 0, 0:NT], 2.0, None, ALU.mult))
            V.do(vec.tensor_scalar(st(3), cnt_in[:, :], 1.0, None, ALU.max))
            inv_root(st(7))
            V.do(vec.tensor_scalar(st(6), cnt_in[:, :], 0.0, None, ALU.is_gt))
            V.do(vec.tensor_tensor(dinv_in[:, :], st(7), st(6), ALU.mult))

            def join(acc, t):
                a = acc[:, 0:2 * NT * D].rearrange("p (q w f) -> p q w f", w=2, f=D)
                V.did(vec.memset(t[0:HP, 0:1, :], 0.0))
                V.did(vec.tensor_copy(t[HP:P, :, :], a[0:HP, :, 1, :]))
                V.do(vec.tensor_copy(t[0:HP, 1:NT, :], a[HP:P, 0:NT - 1, 1, :]))
                V.do(vec.tensor_tensor(t, t, a[:, :, 0, :], ALU.add))

            V.all()
            join(ACC, JOIN)
            V.do(vec.scalar_tensor_tensor(x3, JOIN, 0.0, x3, ALU.max, ALU.add))
            layernorm(PA, PB)
            for b in range(0, NB, 3):
                m0, m1 = BANKS[b][0], BANKS[b + 2][1]
                V.do(vec.tensor_tensor(Z2[:, 0:m1 - m0, :], PA[:, m0:m1, :], bc(dinv_in[:, m0:m1]), ALU.mult))
                split(XP[0], Z2[:, 0:m1 - m0, :], R2S[:, 0:m1 - m0, :], m0, m1)
                dve.sem_inc(s_xp, 3)
            V.do(vec.memset(PB, 0.0))
            V.do(vec.scalar_tensor_tensor(x3, PA, small[:, 48:49], x3, ALU.mult, ALU.add))
            vec.tensor_scalar(CLAMP, REL3, -1.0, float(P), ALU.max, ALU.min).then_inc(s_clamp, 1)
            L = Count(dve, v_l2)
            PER = 2 * (1 + 8 * NB)
            with dve.Fori(0, K // 2) as i:
                L.base = dve.snap(i * PER)
                for u in range(2):
                    new = (PB, PA)[u]
                    n = i * 2 + u
                    L.do(vec.tensor_scalar(st(0), dinv_in[:, :], rec[:, bass.ds(n, 1)], None, ALU.mult))
                    for b, (m0, m1) in enumerate(BANKS):
                        w = m1 - m0
                        y, r, pn = TY[:, 0:w, :], TR[:, 0:w, :], new[:, m0:m1, :]
                        dve.wait_ge(s_prop, i * (2 * NB) + ((2 + u) * NB + b + 1))
                        vec.tensor_reduce(y, bank_of(b), AX.X, ALU.add).then_inc(s_bank, 1)
                        dve.wait_ge(s_bank, i * (2 * NB) + ((2 + u) * NB + b + 1))
                        L.do(vec.tensor_tensor(y, y, bc(st(0)[:, m0:m1]), ALU.mult))
                        L.do(vec.scalar_tensor_tensor(pn, pn, rec[:, bass.ds(n + K, 1)], y, ALU.mult, ALU.add))
                        L.did(vec.scalar_tensor_tensor(x3[:, m0:m1, :], pn, small[:, bass.ds(n + 49, 1)], x3[:, m0:m1, :], ALU.mult, ALU.add))
                        L.do(vec.tensor_tensor(y, pn, bc(dinv_in[:, m0:m1]), ALU.mult))
                        X = XP[1 - u][:, m0:m1, :, :]
                        L.do(vec.tensor_copy(X[:, :, 0, :], y))
                        L.do(vec.tensor_tensor(r, y, X[:, :, 0, :], ALU.subtract))
                        L.do(vec.tensor_copy(X[:, :, 1, :], r))
                        L.do(vec.tensor_tensor(X[:, :, 2, :], r, X[:, :, 1, :], ALU.subtract))
                        dve.sem_inc(s_xp, 1)
                assert L.n == PER
            layernorm(H3, LNT3)
            dve.sem_inc(s_h, 1)
            dve.sem_inc(s_oht, 4)
            V.did(vec.memset(HT3[0:D, NP:], 0.0))
            V.did(vec.memset(ACC3, 0.0))
            V.did(vec.memset(TILE3[0:1, 0:2], BLANK))
            V.did(vec.tensor_copy(TILE3[0:1, 2:2 + NG], tile_row[0:1, :]))
            V.all()
            dve.sem_inc(s_shift3, 2)
            for c, (m0, m1) in enumerate(HCH):
                dve.wait_ge(s_ht3, c + 1)
                vec.tensor_copy(HT3[0:D, m0 * P:m1 * P], psum[0:D, 1 + 2 * (c % 2), 0:(m1 - m0) * P]).then_inc(s_htc3, 1)
            pos, inv = st(2), st(1)
            V.did(vec.tensor_scalar(st(0), cnt_in[:, :], 1.0, None, ALU.max))
            V.do(vec.tensor_scalar(pos, cnt_in[:, :], 0.0, None, ALU.is_gt))
            V.did(vec.reciprocal(inv, st(0)))
            dve.wait_ge(s_w3in, 16 * 8)
            for c in range(len(WCH) + 1):
                if c == 3:
                    V.did(vec.tensor_tensor(LNT3, B3R.unsqueeze(1).broadcast_to((P, NT, D)), bc(pos), ALU.mult))
                if c == 6:
                    V.did(vec.tensor_tensor(x3, x3, H3, ALU.add))
                if c == 9:
                    V.all()
                    V.did(vec.tensor_tensor(x3, x3, LNT3, ALU.add))
                if c < len(WCH):
                    w0, w1 = WCH[c]
                    if c >= 2:
                        dve.wait_ge(s_pdc, c - 1)
                    dve.wait_ge(s_pdhi, c + 1)
                    vec.tensor_tensor(PDR[:, c % 2, 0:(w1 - w0) * HID].rearrange("p (q f) -> p q f", f=HID),
                                      psum[:, 2 + c % 4, 0:(w1 - w0) * HID].rearrange("p (q f) -> p q f", f=HID),
                                      PD[:, w0 * 3 * HID:w1 * 3 * HID].rearrange("p (q j f) -> p q j f", j=3, f=HID)[:, :, 0, :], ALU.subtract).then_inc(s_pdr, 1)
                if c:
                    w0, w1 = WCH[c - 1]
                    X = PD[:, w0 * 3 * HID:w1 * 3 * HID].rearrange("p (q j f) -> p q j f", j=3, f=HID)
                    dve.wait_ge(s_pdr, c)
                    dve.wait_ge(s_pdmid, c)
                    vec.tensor_tensor(X[:, :, 2, :], PDR[:, (c - 1) % 2, 0:(w1 - w0) * HID].rearrange("p (q f) -> p q f", f=HID), X[:, :, 1, :], ALU.subtract).then_inc(s_pdc, 1)
            dve.sem_inc(s_acc3, 2)

            def one_hot_t(k, n, used):
                dve.wait_ge(s_rel3[k], used)
                dve.wait_ge(s_z1, n + 1)
                vec.tensor_scalar(OHT[:, k % 2, :], REL_ROW[:, k, :], iota_p[:, 0:1], None, ALU.is_equal).then_inc(s_oht, 1)

            def one_hot(k, n, cols):
                dve.wait_ge(s_seg3, n + 1)
                for t in range(4):
                    last = vec.tensor_scalar(OHF[:, k % 2, t, :], iota_256[:, 0:P], REL3[:, cols(t)], None, ALU.is_equal)
                last.then_inc(s_ohf, 1)

            def message(k, n, m):
                dve.wait_ge(s_w3, n + 3)
                z, X = psum[:, 5, 0:4 * D].rearrange("p (t f) -> p t f", t=4), MS[:, k % 2, :, :, :]
                vec.tensor_copy(X[:, :, 0, :], z).then_inc(v_mlp, 1)
                dve.wait_ge(v_mlp, m + 1)
                vec.tensor_tensor(MSR, z, X[:, :, 0, :], ALU.subtract).then_inc(v_mlp, 1)
                dve.wait_ge(v_mlp, m + 2)
                vec.tensor_copy(X[:, :, 1, :], MSR).then_inc(v_mlp, 1)
                dve.wait_ge(v_mlp, m + 3)
                vec.tensor_tensor(X[:, :, 2, :], MSR, X[:, :, 1, :], ALU.subtract).then_inc(s_msg, 1)

            def add_sums(k, n, window, m):
                dve.wait_ge(s_seg3, n + 3)
                dve.wait_ge(s_acc3, n + 2)
                vec.tensor_reduce(SUM3, psum[:, 6 + k % 2, 0:PART].rearrange("p (j f) -> p f j", j=3), AX.X, ALU.add).then_inc(v_mlp, 1)
                dve.wait_ge(v_mlp, m + 1)
                at = ACC3[:, bass.ds(dve.snap(window, min_val=0, max_val=BLANK) * D, D)]
                vec.tensor_tensor(at, at, SUM3, ALU.add).then_inc(s_acc3, 1)

            def mlp(i, n, used, m, first=False, last=False):
                off = -5 if first else 0
                at = slice(i * 4, 4 + i * 4) if isinstance(i, int) else bass.ds(i * 4, 4)
                dve.load(base, TILE3[0:1, at])
                for k in range(4):
                    if not (last and k == 3):
                        one_hot_t((k + 1) % 4, n + (k + 1), used + (16 if k < 3 else 32))
                    if not (first and k == 0):
                        cols = (lambda t: slice(i * 16 + 4 * k - 4 + t, i * 16 + 4 * k - 3 + t)) if isinstance(i, int) else \
                            (lambda t: bass.ds(i * 16 + (4 * k - 4 + t), 1))
                        one_hot(k - 1, n + (k - 1), cols)
                        message(k - 1, n + (k - 1), m + (0 if first and k == 1 else 4 * k + off))
                    if not (first and k < 2):
                        add_sums(k - 2, n + (k - 2), base[k], m + (4 * k + 3 + off))

            with dve.Fori(0, most // 2 + 1) as p:
                n0 = dve.snap(p * NG)
                one_hot_t(0, n0, dve.snap(p * (16 * NG // 4) + 16))
                mlp(0, n0, dve.snap(p * (16 * NG // 4)), dve.snap(p * (4 * NG)), first=True)
                with dve.Fori(1, NG // 4 - 1) as i:
                    mlp(i, dve.snap(p * NG + i * 4), dve.snap(p * (16 * NG // 4) + i * 16), dve.snap(p * (4 * NG) + i * 16 - 5))
                n1 = dve.snap(p * NG + (NG - 4))
                m1 = dve.snap(p * (4 * NG) + (4 * NG - 21))
                mlp(NG // 4 - 1, n1, dve.snap(p * (16 * NG // 4) + 16 * (NG // 4 - 1)), m1, last=True)
                one_hot(3, n1 + 3, lambda t: slice(NC - 4 + t, NC - 3 + t))
                message(3, n1 + 3, m1 + 16)
                dve.load(base[0:2], TILE3[0:1, NG:NG + 2])
                add_sums(2, n1 + 2, base[0], m1 + 19)
                add_sums(3, n1 + 3, base[1], m1 + 20)
                dve.wait_ge(s_acc3, n0 + (NG + 2))
                vec.tensor_scalar(REL3, REL3, float(P), None, ALU.subtract).then_inc(s_shift3, 1)
                vec.tensor_scalar(TILE3[0:1, 2:2 + NG], TILE3[0:1, 2:2 + NG], 2.0, float(BLANK), ALU.add, ALU.min).then_inc(s_shift3, 2)
                dve.wait_ge(s_shift3, p * 3 + 5)
                dve.wait_ge(s_relt, p + 1)
                vec.tensor_scalar(CLAMP, REL3, -1.0, float(P), ALU.max, ALU.min).then_inc(s_clamp, 1)
            join(ACC3, JOIN3)
            for m0, m1 in OUT:
                V.do(vec.tensor_tensor(JOIN3[:, m0:m1, :], JOIN3[:, m0:m1, :], bc(inv[:, m0:m1]), ALU.mult))
                V.do(vec.tensor_tensor(x3[:, m0:m1, :], x3[:, m0:m1, :], JOIN3[:, m0:m1, :], ALU.add))
                dve.sem_inc(s_final, 1)


_INS = ['x', 'src', 'dst', 'edge_attr_16', 'edge_type_8', 'edge_weight1', 'L1_gnn_weight1', 'L1_gnn_weight2', 'L1_gnn_bias1',
        'L1_gnn_bias2', 'L2_gnn_lap_coefs', 'L2_gnn_mf_weights', 'L3_gnn_W1', 'L3_gnn_b1', 'L3_gnn_W2', 'L3_gnn_b2',
        'L3_gnn_W3', 'L3_gnn_b3']


def kernel(**inputs):
    import numpy as _np
    import concourse.bacc as _bacc
    from concourse import mybir as _mybir
    from concourse.bass_utils import run_bass_kernel_spmd as _run

    nc = _bacc.Bacc("TRN2", target_bir_lowering=False, num_devices=1)
    arrays, args = {}, []
    for name in _INS:
        a = _np.ascontiguousarray(inputs[name])
        arrays[f"in_{name}_dram"] = a
        args.append(nc.dram_tensor(f"in_{name}_dram", a.shape, _mybir.dt.from_np(a.dtype), kind="ExternalInput").ap())
    args.append(nc.dram_tensor("out_0_dram", (N, D), F32, kind="ExternalOutput").ap())
    gnn(nc, *args)
    r = _run(nc, [arrays], core_ids=[0])
    return r.results[0]["out_0_dram"]
```
